# Optimizing a Trainium2 kernel written in Bass

```python
import numpy as np
import jax
import jax.numpy as jnp

def _softmax(x, axis=-1):
    return jax.nn.softmax(x, axis=axis)

def _gelu(x):
    return jax.nn.gelu(x, approximate=True)

def _silu(x):
    return jax.nn.silu(x)

def _sigmoid(x):
    return jax.nn.sigmoid(x)

def _layernorm(x, axis=-1, eps=1e-05):
    m = jnp.mean(x, axis=axis, keepdims=True)
    v = jnp.var(x, axis=axis, keepdims=True)
    return (x - m) / jnp.sqrt(v + eps)

def _scatter_add(tgt, idx, src, axis=0):
    return tgt.at[idx].add(src)

def _segment_sum(src, seg, n):
    return jax.ops.segment_sum(src, seg, n)
kernel_name = 'mk_hybrid_d1_jaxref_r4_ee0142'

def setup_inputs(seed: int=0):
    np.random.seed(seed)
    _w = jnp.asarray

    def _L0_attn_a_setup():
        import jax, jax.numpy as jnp
        from jax import lax
        import numpy as np
        DIM = 256
        HEADS = 16
        B, N = (2, 512)

        def sn_dense(x, W, u, sigma_param):
            v = lax.stop_gradient(W @ u)
            v = lax.stop_gradient(v / jnp.linalg.norm(v, ord=2))
            u2 = lax.stop_gradient(W.T @ v)
            u2 = lax.stop_gradient(u2 / jnp.linalg.norm(u2, ord=2))
            sigma = jnp.einsum('c,cd,d->', v, W, u2)
            return x @ (sigma_param[0] / sigma * W)
        key = jax.random.key(seed)
        ks = jax.random.split(key, 5)
        std = 0.1
        batch = jax.random.normal(ks[0], (B, N, DIM), dtype=jnp.float32)
        W_qkv = jax.random.normal(ks[1], (DIM, 3 * DIM), dtype=jnp.float32) * std
        W_proj = jax.random.normal(ks[2], (DIM, DIM), dtype=jnp.float32) * std
        u_qkv = jax.random.normal(ks[3], (3 * DIM,), dtype=jnp.float32)
        u_qkv = u_qkv / jnp.linalg.norm(u_qkv)
        u_proj = jax.random.normal(ks[4], (DIM,), dtype=jnp.float32)
        u_proj = u_proj / jnp.linalg.norm(u_proj)
        sigma_qkv = jnp.ones((1,), dtype=jnp.float32)
        sigma_proj = jnp.ones((1,), dtype=jnp.float32)
        return {'batch': batch, 'W_qkv': W_qkv, 'u_qkv': u_qkv, 'sigma_qkv': sigma_qkv, 'W_proj': W_proj, 'u_proj': u_proj, 'sigma_proj': sigma_proj}
    _L0_attn_a_in = _L0_attn_a_setup()

    def _L0_attn_b_setup():
        import jax, jax.numpy as jnp
        import numpy as np
        BATCH, SEQ, DMODEL, NSTATE = (4, 512, 256, 16)
        key = jax.random.key(seed)
        ks = jax.random.split(key, 6)

        def lin_w(k, out_d, in_d):
            return jax.random.uniform(k, (out_d, in_d), jnp.float32, -1.0, 1.0) / np.sqrt(in_d).astype(np.float32)
        return {'x': jax.random.normal(ks[0], (BATCH, SEQ, DMODEL), jnp.float32), 'W1': lin_w(ks[1], DMODEL, DMODEL), 'b1': jnp.zeros((DMODEL,), jnp.float32), 'W2': lin_w(ks[2], NSTATE, DMODEL), 'b2': jnp.zeros((NSTATE,), jnp.float32), 'W3': lin_w(ks[3], NSTATE, DMODEL), 'b3': jnp.zeros((NSTATE,), jnp.float32), 'A': jax.random.uniform(ks[4], (DMODEL, NSTATE), jnp.float32, -1.0, 1.0) * np.sqrt(6.0 / (DMODEL + NSTATE)).astype(np.float32)}
    _L0_attn_b_in = _L0_attn_b_setup()

    def _L0_ffn_setup():
        import jax, jax.numpy as jnp
        import numpy as np
        DIM = 256
        INTER = 256
        E = 8
        TOPK = 2
        ROUTE_SCALE = 1.0
        SHARED_INTER = 512
        B, S = (4, 512)

        def _moe_forward(x, gate_w, gate_b, w1, b1, w3, b3, w2, b2, ws1, bs1, ws3, bs3, ws2, bs2):
            Bq, Sq, D = x.shape
            xt = x.reshape(-1, D)
            logits = (xt @ gate_w.T + gate_b).astype(jnp.float32)
            scores = jax.nn.softmax(logits, axis=-1)
            top_w, top_i = jax.lax.top_k(scores, TOPK)
            weights = (top_w * ROUTE_SCALE).astype(x.dtype)
            gate_dense = jnp.sum(jax.nn.one_hot(top_i, E, dtype=x.dtype) * weights[..., None], axis=1)

            def expert(w1e, b1e, w3e, b3e, w2e, b2e):
                h = jax.nn.silu(xt @ w1e.T + b1e) * (xt @ w3e.T + b3e)
                return h @ w2e.T + b2e
            outs = jax.vmap(expert)(w1, b1, w3, b3, w2, b2)
            y = jnp.einsum('etd,te->td', outs, gate_dense)
            z = jax.nn.silu(xt @ ws1.T + bs1) * (xt @ ws3.T + bs3) @ ws2.T + bs2
            return (y + z).reshape(Bq, Sq, D)
        key = jax.random.key(seed)
        ks = jax.random.split(key, 10)

        def w(k, shape, scale=0.02):
            return jax.random.normal(k, shape, jnp.float32) * scale
        return {'x': jax.random.normal(ks[0], (B, S, DIM), jnp.float32), 'gate_w': w(ks[1], (E, DIM)), 'gate_b': jnp.zeros((E,), jnp.float32), 'w1': w(ks[2], (E, INTER, DIM)), 'b1': jnp.zeros((E, INTER), jnp.float32), 'w3': w(ks[3], (E, INTER, DIM)), 'b3': jnp.zeros((E, INTER), jnp.float32), 'w2': w(ks[4], (E, DIM, INTER)), 'b2': jnp.zeros((E, DIM), jnp.float32), 'ws1': w(ks[5], (SHARED_INTER, DIM)), 'bs1': jnp.zeros((SHARED_INTER,), jnp.float32), 'ws3': w(ks[6], (SHARED_INTER, DIM)), 'bs3': jnp.zeros((SHARED_INTER,), jnp.float32), 'ws2': w(ks[7], (DIM, SHARED_INTER)), 'bs2': jnp.zeros((DIM,), jnp.float32)}
    _L0_ffn_in = _L0_ffn_setup()
    _d = {'L0_attn_a_batch': _L0_attn_a_in['batch'], 'L0_attn_a_W_qkv': _L0_attn_a_in['W_qkv'], 'L0_attn_a_u_qkv': _L0_attn_a_in['u_qkv'], 'L0_attn_a_sigma_qkv': _L0_attn_a_in['sigma_qkv'], 'L0_attn_a_W_proj': _L0_attn_a_in['W_proj'], 'L0_attn_a_u_proj': _L0_attn_a_in['u_proj'], 'L0_attn_a_sigma_proj': _L0_attn_a_in['sigma_proj'], 'L0_attn_b_W1': _L0_attn_b_in['W1'], 'L0_attn_b_b1': _L0_attn_b_in['b1'], 'L0_attn_b_W2': _L0_attn_b_in['W2'], 'L0_attn_b_b2': _L0_attn_b_in['b2'], 'L0_attn_b_W3': _L0_attn_b_in['W3'], 'L0_attn_b_b3': _L0_attn_b_in['b3'], 'L0_attn_b_A': _L0_attn_b_in['A'], 'L0_ffn_gate_w': _L0_ffn_in['gate_w'], 'L0_ffn_gate_b': _L0_ffn_in['gate_b'], 'L0_ffn_w1': _L0_ffn_in['w1'], 'L0_ffn_b1': _L0_ffn_in['b1'], 'L0_ffn_w3': _L0_ffn_in['w3'], 'L0_ffn_b3': _L0_ffn_in['b3'], 'L0_ffn_w2': _L0_ffn_in['w2'], 'L0_ffn_b2': _L0_ffn_in['b2'], 'L0_ffn_ws1': _L0_ffn_in['ws1'], 'L0_ffn_bs1': _L0_ffn_in['bs1'], 'L0_ffn_ws3': _L0_ffn_in['ws3'], 'L0_ffn_bs3': _L0_ffn_in['bs3'], 'L0_ffn_ws2': _L0_ffn_in['ws2'], 'L0_ffn_bs2': _L0_ffn_in['bs2']}
    _x0 = _d['L0_attn_a_batch']
    _d['L0_attn_a_batch'] = jax.random.normal(jax.random.fold_in(jax.random.key(seed), 1), (2, 2048, 256), dtype=_x0.dtype)
    del _x0
    return _d

def reference(L0_attn_a_batch, L0_attn_a_W_qkv, L0_attn_a_u_qkv, L0_attn_a_sigma_qkv, L0_attn_a_W_proj, L0_attn_a_u_proj, L0_attn_a_sigma_proj, L0_attn_b_W1, L0_attn_b_b1, L0_attn_b_W2, L0_attn_b_b2, L0_attn_b_W3, L0_attn_b_b3, L0_attn_b_A, L0_ffn_gate_w, L0_ffn_gate_b, L0_ffn_w1, L0_ffn_b1, L0_ffn_w3, L0_ffn_b3, L0_ffn_w2, L0_ffn_b2, L0_ffn_ws1, L0_ffn_bs1, L0_ffn_ws3, L0_ffn_bs3, L0_ffn_ws2, L0_ffn_bs2):

    def _L0_attn_a_ref(batch, W_qkv, u_qkv, sigma_qkv, W_proj, u_proj, sigma_proj):
        import jax, jax.numpy as jnp
        from jax import lax
        import numpy as np
        DIM = 256
        HEADS = 16
        B, N = (2, 512)

        def sn_dense(x, W, u, sigma_param):
            v = lax.stop_gradient(W @ u)
            v = lax.stop_gradient(v / jnp.linalg.norm(v, ord=2))
            u2 = lax.stop_gradient(W.T @ v)
            u2 = lax.stop_gradient(u2 / jnp.linalg.norm(u2, ord=2))
            sigma = jnp.einsum('c,cd,d->', v, W, u2)
            return x @ (sigma_param[0] / sigma * W)
        b, n, d = batch.shape
        h = HEADS
        hd = d // h
        qkv = sn_dense(batch, W_qkv, u_qkv, sigma_qkv)
        q, k, v = jnp.split(qkv, 3, axis=-1)
        split_heads = lambda t: t.reshape(b, n, h, hd).transpose(0, 2, 1, 3)
        q, k, v = (split_heads(q), split_heads(k), split_heads(v))
        scale = hd ** (-0.5)
        att = jnp.einsum('bhqd,bhkd->bhqk', q, k) * scale
        causal = jnp.tril(jnp.ones((n, n), dtype=jnp.float32))
        big_neg = jnp.finfo(att.dtype).min
        att = jnp.where(causal[None, None] == 0, big_neg, att)
        att = jax.nn.softmax(att, axis=-1)
        x = jnp.einsum('bhqk,bhkd->bhqd', att, v)
        x = x.transpose(0, 2, 1, 3).reshape(b, n, d)
        x = sn_dense(x, W_proj, u_proj, sigma_proj)
        return x

    def _L0_attn_b_ref(x, W1, b1, W2, b2, W3, b3, A):
        import jax, jax.numpy as jnp
        import numpy as np
        BATCH, SEQ, DMODEL, NSTATE = (4, 512, 256, 16)
        Bmat = x @ W2.T + b2
        Cmat = x @ W3.T + b3
        delta = jax.nn.softplus(x @ W1.T + b1)
        bc = jnp.einsum('bln,bln->bl', Bmat, Cmat)
        y = x * delta * bc[..., None]
        return y

    def _L0_ffn_ref(x, gate_w, gate_b, w1, b1, w3, b3, w2, b2, ws1, bs1, ws3, bs3, ws2, bs2):
        import jax, jax.numpy as jnp
        import numpy as np
        DIM = 256
        INTER = 256
        E = 8
        TOPK = 2
        ROUTE_SCALE = 1.0
        SHARED_INTER = 512
        B, S = (4, 512)

        def _moe_forward(x, gate_w, gate_b, w1, b1, w3, b3, w2, b2, ws1, bs1, ws3, bs3, ws2, bs2):
            Bq, Sq, D = x.shape
            xt = x.reshape(-1, D)
            logits = (xt @ gate_w.T + gate_b).astype(jnp.float32)
            scores = jax.nn.softmax(logits, axis=-1)
            top_w, top_i = jax.lax.top_k(scores, TOPK)
            weights = (top_w * ROUTE_SCALE).astype(x.dtype)
            gate_dense = jnp.sum(jax.nn.one_hot(top_i, E, dtype=x.dtype) * weights[..., None], axis=1)

            def expert(w1e, b1e, w3e, b3e, w2e, b2e):
                h = jax.nn.silu(xt @ w1e.T + b1e) * (xt @ w3e.T + b3e)
                return h @ w2e.T + b2e
            outs = jax.vmap(expert)(w1, b1, w3, b3, w2, b2)
            y = jnp.einsum('etd,te->td', outs, gate_dense)
            z = jax.nn.silu(xt @ ws1.T + bs1) * (xt @ ws3.T + bs3) @ ws2.T + bs2
            return (y + z).reshape(Bq, Sq, D)
        return _moe_forward(x, gate_w, gate_b, w1, b1, w3, b3, w2, b2, ws1, bs1, ws3, bs3, ws2, bs2)
    x = L0_attn_a_batch
    x = x + _L0_attn_a_ref(_layernorm(x, axis=-1), L0_attn_a_W_qkv, L0_attn_a_u_qkv, L0_attn_a_sigma_qkv, L0_attn_a_W_proj, L0_attn_a_u_proj, L0_attn_a_sigma_proj)
    x = x + _L0_ffn_ref(_layernorm(x, axis=-1), L0_ffn_gate_w, L0_ffn_gate_b, L0_ffn_w1, L0_ffn_b1, L0_ffn_w3, L0_ffn_b3, L0_ffn_w2, L0_ffn_b2, L0_ffn_ws1, L0_ffn_bs1, L0_ffn_ws3, L0_ffn_bs3, L0_ffn_ws2, L0_ffn_bs2)
    x = x + _L0_attn_b_ref(_layernorm(x, axis=-1), L0_attn_b_W1, L0_attn_b_b1, L0_attn_b_W2, L0_attn_b_b2, L0_attn_b_W3, L0_attn_b_b3, L0_attn_b_A)
    x = x + _L0_ffn_ref(_layernorm(x, axis=-1), L0_ffn_gate_w, L0_ffn_gate_b, L0_ffn_w1, L0_ffn_b1, L0_ffn_w3, L0_ffn_b3, L0_ffn_w2, L0_ffn_b2, L0_ffn_ws1, L0_ffn_bs1, L0_ffn_ws3, L0_ffn_bs3, L0_ffn_ws2, L0_ffn_bs2)
    return x

_drawn_inputs = setup_inputs


def setup_inputs(seed=0):
    import zlib

    import numpy as np

    out = dict(_drawn_inputs(seed))
    spreads = {'L0_attn_b_b1': (0.0, 0.1),
     'L0_attn_b_b2': (0.0, 0.1),
     'L0_attn_b_b3': (0.0, 0.1),
     'L0_ffn_gate_b': (0.0, 0.308),
     'L0_ffn_b1': (0.0, 0.8),
     'L0_ffn_b3': (0.0, 0.8),
     'L0_ffn_b2': (0.0, 0.1),
     'L0_ffn_bs1': (0.0, 0.564),
     'L0_ffn_bs3': (0.0, 0.546),
     'L0_ffn_bs2': (0.0, 0.1)}
    factors = {'L0_attn_a_u_qkv': 8.0,
     'L0_attn_a_u_proj': 8.0,
     'L0_ffn_w1': 6.772,
     'L0_ffn_w3': 6.744,
     'L0_ffn_w2': 6.396}
    for name, (base, spread) in spreads.items():
        noise = np.random.default_rng([zlib.crc32(name.encode()), seed]).standard_normal(out[name].shape)
        drawn = base * np.exp(spread * noise) if base else spread * noise
        out[name] = jnp.asarray(drawn.astype(out[name].dtype))
    for name, factor in factors.items():
        out[name] = (out[name] * factor).astype(out[name].dtype)
    return out
```

```python
import concourse.bass as bass
from concourse import mybir
from contextlib import ExitStack

P = 128
B, N, D = 2, 2048, 256
H, HD = 16, 16
KC = D // P
TOK = B * N
CH = 512
TPC = CH // P
NCH = TOK // CH
EXP = 8
NE = 10
NST = 16
DW = D + 2 * NST
GW = DW + EXP
EPS = 1e-5
NEG = -1e30

HPG = 4
NG = H // HPG
NU = B * NG
QCH = N // CH
KT = N // P
PACK = 3 * HD
MROW = PACK

NPIECE = 3 * NE + 2
ROWS = 64 + MROW + 1
HALF_LD = 14 * 16
STEPS = [(c, j) for c in range(QCH) for j in range(TPC * (c + 1))]
NSTEP = len(STEPS)
LAG = 2
PRING = 4
PROJ = ((9, 10), (17, 18), (29, 30), (3, 4))
NPREP = {3: 2 * NCH, 4: 3 * NCH, 5: 4 * NCH}
MAXES = []
for _i in range(KT):
    for _c in range(_i // TPC + 1):
        _w = min(CH, (_i + 1) * P - _c * CH)
        MAXES.append((_i, _c, _w, CH // _w))
NBANK = sum(HPG // hb for _, _, _, hb in MAXES)
EARLY = NSTEP - TPC * (QCH // 2)
MAX_FROM, MAX_BY = 3, NSTEP - 5


BANKS = [(i, c, w, hb, n) for i, c, w, hb in MAXES for n in range(HPG // hb)]


def max_slot(k):
    total = sum(w * hb for _, _, w, hb, _ in BANKS)
    lo = total * (k - MAX_FROM) / (MAX_BY - MAX_FROM)
    hi = total * (k + 1 - MAX_FROM) / (MAX_BY - MAX_FROM)
    at, n = 0, []
    for bank, (_, _, w, hb, _) in enumerate(BANKS):
        if lo <= at < hi:
            n.append(bank)
        at += w * hb
    return n


def build(nc, x_in, wqkv_in, uqkv_in, sqkv_in, wproj_in, uproj_in, sproj_in,
          wffn_in, b13_in, b2_in, gb_in, bd_in, out, phases=5):
    f32, f32r, bf16 = mybir.dt.float32, mybir.dt.float32r, mybir.dt.bfloat16
    ALU = mybir.AluOpType
    ACT = mybir.ActivationFunctionType
    AX = mybir.AxisListType

    qk_s = nc.dram_tensor("qk_split", [2, 2 * D, TOK], f32, kind="Internal").ap()
    v_s = nc.dram_tensor("v_ones", [TOK, H * 32], f32, kind="Internal").ap()
    w_s = nc.dram_tensor("w_split", [NPIECE, 2, P, KC * D], f32, kind="Internal").ap()

    ctx = ExitStack()
    with ctx:
        def sb(name, shape, dt=f32, stack=ctx):
            return stack.enter_context(nc.sbuf_tensor(name, shape, dt))

        def sem(name):
            return ctx.enter_context(nc.semaphore(name))

        x = sb("x", [P, TOK // P, D])
        tok = ExitStack()
        xn = sb("xn", [P, TPC, D], f32, tok)
        xt = [[sb(f"xt{p}{h}", [P, KC, CH], f32r, tok) for h in range(2)] for p in range(2)]
        tok.close()
        pr = [sb(f"pr{i}", [P, HPG, CH]) for i in range(2)]
        osb = sb("osb", [P, CH])
        rdb = sb("rdb", [P, CH])
        stats = sb("stats", [P, TPC, 6])
        mv = sb("mv", [P, TPC, 2])
        vare = sb("vare", [P, TPC])
        rstd = sb("rstd", [P, TPC])
        mhalf = sb("mhalf", [P, TPC])
        ones = sb("ones", [P, P])
        ident = sb("ident", [P, P])
        att = ExitStack()
        identb = sb("identb", [P, P], bf16, att)
        mask_qk = sb("mask_qk", [P, P], bf16, att)
        mask_kq = sb("mask_kq", [P, P], bf16, att)
        wph = sb("wph", [P, NG, D], f32r, att)
        wpl = sb("wpl", [P, NG, D], f32r, att)
        wraw = [sb(f"wraw{i}", [P, KC * D], f32r, att) for i in range(2)]
        whi = [sb(f"whi{i}", [P, KC * D], f32r, att) for i in range(2)]
        prj = ExitStack()
        wq_raw = sb("wq_raw", [P, KC, 3 * D], f32, prj)
        wq_hl = [sb(f"wq_{h}", [P, KC, 3 * D], f32r, prj) for h in range(2)]
        wp_raw = sb("wp_raw", [P, NG, D], f32, prj)
        ub = sb("ub", [P, 3 * D + D], f32, prj)
        prod = sb("prod", [P, KC * 3 * D + NG * D], f32, prj)
        vr = sb("vr", [P, KC + NG], f32, prj)
        vsq = sb("vsq", [P, KC + NG], f32, prj)
        vn = sb("vn", [P, KC + NG], f32, prj)
        nrm = sb("nrm", [P, 2], f32, prj)
        rn = sb("rn", [P, 2], f32, prj)
        u2 = sb("u2", [P, 8], f32, prj)
        u2q = sb("u2q", [P, 8], f32, prj)
        u2s = sb("u2s", [P, 2], f32, prj)
        sg = sb("sg", [P, 2], f32, prj)
        rs = sb("rs", [P, 2], f32, prj)
        sp_in = sb("sp_in", [P, 2], f32, prj)
        scl = sb("scl", [P, 2], f32, prj)
        qst = [[sb(f"qst{p}{h}", [P, 4, CH], f32r, prj) for h in range(2)] for p in range(2)]
        vst = [sb(f"vst{p}", [P, TPC, H, 32], f32, prj) for p in range(2)]
        prj.close()
        qp = [sb(f"qp{p}", [P, 2, N], f32r, att) for p in range(2)]
        kp = [sb(f"kp{p}", [P, HPG, N], f32r, att) for p in range(2)]
        vt = [sb(f"vt{p}", [P, KT, HPG * 32], f32, att) for p in range(2)]
        pr += [sb(f"pr{i}", [P, HPG, CH], f32, att) for i in range(2, PRING)]
        part = [sb(f"part{p}", [P, HPG, KT, QCH], f32, att) for p in range(2)]
        mneg = sb("mneg", [P, HPG * KT], f32, att)
        mneg_t = sb("mneg_t", [HPG * KT, P], f32r, att)
        rden = sb("rden", [P, CH], f32, att)
        af = rden
        ah = sb("ah", [P, CH], f32r, att)
        al = sb("al", [P, CH], f32r, att)
        att.close()
        ffn = ExitStack()
        w13 = [[sb(f"w13_{e}_{h}", [P, 2, KC, D], f32r, ffn) for h in range(2)] for e in range(NE)]
        w2 = [[sb(f"w2_{e}_{h}", [P, KC, D], f32r, ffn) for h in range(2)] for e in range(NE)]
        wd = [sb(f"wd_{h}", [P, KC, GW], f32r, ffn) for h in range(2)]
        b13 = sb("b13", [P, 2, NE * KC], f32, ffn)
        b2 = sb("b2", [EXP + 1, D], f32, ffn)
        gb = sb("gb", [P, TPC, EXP], f32, ffn)
        bd = sb("bd", [P, DW], f32, ffn)
        rev = sb("rev", [P, TPC, EXP], f32, ffn)
        gate = sb("gate", [P, TPC, NE], f32, ffn)
        gate_t = sb("gate_t", [EXP + 1, CH], f32, ffn)
        lg = sb("lg", [P, TPC, EXP], f32, ffn)
        sc = sb("sc", [P, TPC, EXP], f32, ffn)
        eq = sb("eq", [P, TPC, EXP], f32, ffn)
        oh = sb("oh", [P, TPC, EXP], f32, ffn)
        mx = sb("mx", [P, TPC], f32, ffn)
        hst = ExitStack()
        hh = [[sb(f"hh{p}{h}", [P, KC, CH], f32r, hst) for h in range(2)] for p in range(2)]
        sil = [sb(f"sil{p}", [P, CH], f32, hst) for p in range(2)]
        hf = [sb(f"hf{p}", [P, CH], f32, hst) for p in range(2)]
        hst.close()
        zt = sb("zt", [P, TPC, DW], f32, hst)
        e1 = sb("e1", [P, TPC, D], f32, hst)
        l1 = sb("l1", [P, TPC, D], f32, hst)
        u1 = sb("u1", [P, TPC, D], f32, hst)
        bcp = sb("bcp", [P, TPC, NST], f32, hst)
        bcs = sb("bcs", [P, TPC], f32, hst)
        hst.close()
        ffn.close()

        def ps(name, shape, stack):
            return stack.enter_context(nc.psum_tensor(name, shape, f32))

        pa = ExitStack()
        tr = [ps(f"tr{k}", [P, CH], pa) for k in range(2)]
        pa2 = ExitStack()
        pqk = [ps(f"pqk{m}", [P, CH], pa2) for m in range(4)]
        pv_ = [ps(f"pv{k}", [P, 2, H, HD], pa2) for k in range(2)]
        pa2.close()
        pup = [[ps(f"pup{p}{k}", [P, CH], pa2) for k in range(2)] for p in range(2)]
        py = [ps(f"py{k}", [P, 2, D], pa2) for k in range(2)]
        pa2.close()
        pd = [ps(f"pd{t}", [P, CH], pa2) for t in range(TPC)]
        pa2.close()
        pa.close()
        ps2 = [ps(f"ps2_{k}", [P, 2, CH], pa) for k in range(2)]
        ps1 = [ps(f"ps1_{k}", [P, CH], pa) for k in range(2)]
        po = ps("po", [P, CH], pa)
        pp = ps("pp", [P, 2, D], pa)
        pa.close()

        s_x0, s_xr, s_w, s_ffnc = sem("s_x0"), sem("s_xr"), sem("s_w"), sem("s_ffnc")
        s_const, s_dconst = sem("s_const"), sem("s_dconst")
        s_sig = sem("s_sig")
        s_stats, s_aggr, s_var, s_rstd, s_xn = (sem(n) for n in ("s_stats", "s_aggr", "s_var", "s_rstd", "s_xn"))
        s_tr, s_xhi, s_xlo = sem("s_tr"), sem("s_xhi"), sem("s_xlo")
        s_lg, s_lgd, s_ex, s_gate, s_gt, s_gts = (sem(n) for n in ("s_lg", "s_lgd", "s_ex", "s_gate", "s_gt", "s_gts"))
        s_rt = sem("s_rt")
        s_qk, s_qhi, s_qlo, s_vp, s_ve = (sem(n) for n in ("s_qk", "s_qhi", "s_qlo", "s_vp", "s_ve"))
        s_qout = [sem("s_qout0"), sem("s_qout1")]
        s_ld = [[sem(f"s_ld{p}{h}") for h in range(2)] for p in range(2)]
        s_lv = [sem("s_lv0"), sem("s_lv1")]
        s_m = sem("s_m")
        s_s1, s_mx, s_pm, s_mt, s_mts = (sem(n) for n in ("s_s1", "s_mx", "s_pm", "s_mt", "s_mts"))
        s_s2, s_ex2, s_pv = sem("s_s2"), sem("s_ex2"), sem("s_pv")
        s_oc, s_rd, s_sh, s_am, s_ah, s_al = (sem(n) for n in ("s_oc", "s_rd", "s_sh", "s_am", "s_ah", "s_al"))
        s_pj, s_xa = sem("s_pj"), sem("s_xa")
        s_wr = [sem("s_wr0"), sem("s_wr1")]
        s_wh, s_wl = sem("s_wh"), sem("s_wl")
        s_ws = [sem("s_ws0"), sem("s_ws1")]
        s_we = [sem(f"s_we{e}") for e in range(NE)]
        s_wd = sem("s_wd")
        names = ("up_a", "up_b", "silu", "h", "h_hi", "h_lo", "y", "acc")
        F = {ph: {n: sem(f"s_{n}_{ph}") for n in names} for ph in "CE"}
        s_dp, s_dz, s_dab, s_de, s_du, s_dl, s_dr, s_dm, s_dx, s_dbc = (
            sem(n) for n in ("s_dp", "s_dz", "s_dab", "s_de", "s_du", "s_dl", "s_dr", "s_dm", "s_dx", "s_dbc"))
        s_out = sem("s_out")

        block = ctx.enter_context(nc.Block())

        x_v = x_in.rearrange("b (k t p) d -> (b k) p t d", t=TPC, p=P)
        o_v = out.rearrange("b (k t p) d -> (b k) p t d", t=TPC, p=P)
        def pairs(eng, count, body, peel_last=False):
            turns = count // 2 - (1 if peel_last else 0)
            with eng.Fori(0, turns) as i:
                body(2 * i, 0, False)
                body(2 * i + 1, 1, False)
            if peel_last:
                body(count - 2, 0, False)
                body(count - 1, 1, True)

        def wait_apart(eng, semaphore, value):
            if not isinstance(value, int):
                value = eng.to_reg(value)
            eng.wait_ge(s_const, 1)
            eng.wait_ge(semaphore, value)

        def units(eng, body):
            body(0, 0, True, False)
            with eng.Fori(0, (NU - 2) // 2) as i:
                body(2 * i + 1, 1, False, False)
                body(2 * i + 2, 0, False, False)
            body(NU - 1, 1, False, True)

        @block.sync
        def _(sp):
            sp.dma_start(x[:, 0:TPC, :], x_v[0]).then_inc(s_x0, 16)
            sp.dma_start(wq_raw[:, :, :], wqkv_in.rearrange("(k p) n -> p k n", p=P)).then_inc(s_w, 16)
            sp.dma_start(ub[:, 0:3 * D], uqkv_in[None, :].to_broadcast([P, 3 * D])).then_inc(s_w, 16)
            sp.dma_start(ub[:, 3 * D:4 * D], uproj_in[None, :].to_broadcast([P, D])).then_inc(s_w, 16)
            sp.dma_start(sp_in[:, 0:1], sqkv_in[None, :].to_broadcast([P, 1])).then_inc(s_w, 16)
            sp.dma_start(sp_in[:, 1:2], sproj_in[None, :].to_broadcast([P, 1])).then_inc(s_w, 16)
            wp_v = wproj_in.rearrange("(g h d) n -> h d g n", h=HPG, d=HD)
            sp.wait_ge(s_dconst, 1)
            for h in range(HPG):
                sp.dma_start(wp_raw[32 * h:32 * h + HD, :, :], wp_v[h]).then_inc(s_w, 16)
            for c in range(1, NCH):
                sp.dma_start(x[:, c * TPC:(c + 1) * TPC, :], x_v[c]).then_inc(s_xr, 16)

            def store(c, p, last):
                sp.wait_ge(s_qlo, c * 4 + 4)
                for h in range(2):
                    sp.dma_start(qk_s[h, :, bass.ds(c * CH, CH)].rearrange("(m p) t -> p m t", p=P),
                                 qst[p][h][:, :, :].bitcast(f32)).then_inc(s_qout[p], 16)
                sp.wait_ge(s_ve, c * 2 + 2)
                sp.dma_start(v_s[bass.ds(c * CH, CH), :].rearrange("(t p) n -> p t n", p=P),
                             vst[p][:, :, :, :].rearrange("p t h w -> p t (h w)")).then_inc(s_qout[p], 16)

            pairs(sp, NCH, store)
            for p in range(2):
                sp.wait_ge(s_qout[p], NCH // 2 * 48)

            def load(u, p, half):
                b, g = u // NG, u % NG
                t0 = half * (N // 2)
                for r0 in (MROW, 64 + MROW):
                    sp.dma_start(qp[p][r0:r0 + 1, :, t0:t0 + N // 2].bitcast(f32),
                                 kp[p][MROW + 1:MROW + 2, 0:HPG - 1:2, t0:t0 + N // 2].bitcast(f32)).then_inc(s_ld[p][half], 16)
                for base, parts in ((0, (0, 0, 1)), (D, (0, 1, 0))):
                    for s in range(2):
                        for n, hl in enumerate(parts):
                            src = qk_s[hl, bass.ds(g * (HPG * HD) + base, HPG * HD), bass.ds(b * N + t0, N // 2)]
                            src = src.rearrange("(r s f) t -> s f r t", r=2, s=2)[s]
                            r0 = 64 * s + HD * n
                            if base == 0:
                                packed = qp[p][r0:r0 + HD, :, t0:t0 + N // 2]
                            else:
                                packed = kp[p][r0:r0 + HD, s:HPG:2, t0:t0 + N // 2]
                            sp.dma_start(packed.bitcast(f32), src).then_inc(s_ld[p][half], 16)

            def load_values(u, p):
                b, g = u // NG, u % NG
                src = v_s[bass.ds(b * N, N), bass.ds(g * (HPG * 32), HPG * 32)]
                sp.dma_start(vt[p][:, :, :], src.rearrange("(j p) n -> p j n", p=P)).then_inc(s_lv[p], 16)

            def reload(u, p):
                sp.wait_ge(s_s2, (u - 2) * (2 * NSTEP) + 2 * EARLY)
                load(u, p, 0)
                sp.wait_ge(s_pv, (u - 1) * NSTEP)
                load(u, p, 1)
                load_values(u, p)

            def max_rows(u, p):
                sp.wait_ge(s_mts, u + 1)
                for h in range(HPG):
                    r0 = 64 * (h % 2) + MROW
                    sp.dma_start(qp[p][r0:r0 + 1, h // 2, :].rearrange("o (i q) -> o i q", q=P).bitcast(f32),
                                 mneg_t[KT * h:KT * (h + 1), :].bitcast(f32)).then_inc(s_m, 16)

            if phases >= 2:
                sp.wait_ge(s_dconst, 4)
                for p in range(2):
                    for h in range(HPG):
                        r0 = 64 * (h % 2) + MROW
                        sp.dma_start(kp[p][r0:r0 + 1, h, :].rearrange("o (i q) -> o i q", q=P).bitcast(f32),
                                     ones[0:KT, :]).then_inc(s_lv[p], 16)
                for half in range(2):
                    load(0, 0, half)
                load_values(0, 0)
                for half in range(2):
                    load(1, 1, half)
                load_values(1, 1)
                max_rows(0, 0)
                with sp.Fori(0, (NU - 2) // 2) as i:
                    max_rows(2 * i + 1, 1)
                    reload(2 * i + 2, 0)
                    max_rows(2 * i + 2, 0)
                    reload(2 * i + 3, 1)
                max_rows(NU - 1, 1)

            if phases >= 3:
                sp.wait_ge(s_pv, NU * NSTEP)
                sp.wait_ge(s_xa, 2 * QCH * NU)
                for i in range(2):
                    sp.wait_ge(s_ws[i], 32 * (NPIECE // 2))
                sp.dma_start(b13[:, :, :], b13_in).then_inc(s_ffnc, 16)
                sp.dma_start(b2[:, :], b2_in).then_inc(s_ffnc, 16)
                sp.dma_start(gb[:, :, :], gb_in[None, None, :].to_broadcast([P, TPC, EXP])).then_inc(s_ffnc, 16)
                sp.dma_start(bd[:, :], bd_in[None, :].to_broadcast([P, DW])).then_inc(s_ffnc, 16)
                for h in range(2):
                    wv = w_s[NPIECE - 2, h].rearrange("p (k n) -> p k n", k=KC)
                    sp.dma_start(wd[h][:, :, 0:D].bitcast(f32), wv).then_inc(s_wd, 16)
                    wv = w_s[NPIECE - 1, h].rearrange("p (k n) -> p k n", k=KC)
                    sp.dma_start(wd[h][:, :, D:GW].bitcast(f32), wv[:, :, 0:GW - D]).then_inc(s_wd, 16)
                for e in range(NE):
                    for h in range(2):
                        for k in range(2):
                            sp.dma_start(w13[e][h][:, k, :, :].bitcast(f32),
                                         w_s[3 * e + k, h].rearrange("p (k n) -> p k n", k=KC)).then_inc(s_we[e], 16)
                        sp.dma_start(w2[e][h][:, :, :].bitcast(f32),
                                     w_s[3 * e + 2, h].rearrange("p (k n) -> p k n", k=KC)).then_inc(s_we[e], 16)

            def emit(c, p, last):
                if phases >= 5:
                    sp.wait_ge(F["E"]["acc"], c * (2 * NE) + 2 * NE + 2)
                sp.dma_start(o_v[bass.ds(c, 1)].rearrange("o p t d -> (o p) t d"), x[:, bass.ds(c * TPC, TPC), :]).then_inc(s_out, 16)

            if phases == 4:
                sp.wait_ge(s_dx, NCH)
            if phases == 3:
                sp.wait_ge(F["C"]["acc"], NCH * 2 * NE + 2)
            if phases == 2:
                sp.wait_ge(s_xa, 2 * QCH * NU)
            pairs(sp, NCH, emit)
            sp.wait_ge(s_out, 16 * NCH)

        @block.gpsimd
        def _(pool):
            pool.memset(mhalf[:, :], -0.5).then_inc(s_const, 1)
            pool.memset(ones[:, :], 1.0).then_inc(s_const, 1)
            pool.memset(ident[:, :], 0.0).then_inc(s_const, 1)
            pool.memset(identb[:, :], 0.0).then_inc(s_const, 1)
            pool.memset(mask_qk[:, :], 0.0).then_inc(s_const, 1)
            pool.memset(mask_kq[:, :], 0.0).then_inc(s_const, 1)
            pool.wait_ge(s_const, 6)
            for m in (ident, identb):
                pool.affine_select(out=m[:, :], in_=m[:, :], compare_op=ALU.not_equal, fill=1.0,
                                   base=0, pattern=[[-1, P]], channel_multiplier=1).then_inc(s_const, 1)
            pool.affine_select(out=mask_qk[:, :], in_=mask_qk[:, :], compare_op=ALU.is_ge, fill=NEG,
                               base=0, pattern=[[-1, P]], channel_multiplier=1).then_inc(s_const, 1)
            pool.affine_select(out=mask_kq[:, :], in_=mask_kq[:, :], compare_op=ALU.is_ge, fill=NEG,
                               base=0, pattern=[[1, P]], channel_multiplier=-1).then_inc(s_const, 1)

            def inverse_std(n):
                pool.wait_ge(s_var, n + 1)
                pool.tensor_tensor(rstd[:, :], vare[:, :], mhalf[:, :], ALU.pow).then_inc(s_rstd, 1)

            inverse_std(0)
            pool.wait_ge(s_sig, 4)
            pool.tensor_tensor(rn[:, :], nrm[:, :], mhalf[:, 0:2], ALU.pow).then_inc(s_sig, 1)
            pool.wait_ge(s_sig, 12)
            pool.tensor_tensor(rs[:, :], sg[:, :], mhalf[:, 0:2], ALU.pow).then_inc(s_sig, 1)
            with pool.Fori(1, NCH) as n:
                inverse_std(n)

            def raw(k, i):
                pool.dma_start(wraw[i][:, :].bitcast(f32), wffn_in[bass.ds(k, 1)].rearrange("o p n -> (o p) n")).then_inc(s_wr[i], 16)

            def finish(u, c, begin, end):
                n = u * QCH + c
                pool.wait_ge(s_sh, n + 1)
                pool.tensor_tensor(af[:, :], osb[:, :], rdb[:, :], ALU.mult).then_inc(s_am, 1)
                if not (begin and c == 0):
                    wait_apart(pool, s_pj, n * 2)
                wait_apart(pool, s_am, n + 1)
                pool.tensor_copy(ah[:, :], af[:, :]).then_inc(s_ah, 1)
                pool.wait_ge(s_ah, n + 1)
                pool.tensor_tensor(al[:, :], af[:, :], ah[:, :].bitcast(f32), ALU.subtract).then_inc(s_al, 1)
                i = c % 2
                turn = u * (QCH // 2) + c // 2
                wait_apart(pool, s_wr[i], turn * 16 + 16)
                pool.tensor_copy(whi[i][:, :], wraw[i][:, :].bitcast(f32)).then_inc(s_wh, 1)
                pool.wait_ge(s_wh, n + 1)
                pool.tensor_tensor(wraw[i][:, :], wraw[i][:, :].bitcast(f32), whi[i][:, :].bitcast(f32),
                                   ALU.subtract).then_inc(s_wl, 1)
                pool.wait_ge(s_wl, n + 1)
                pool.dma_start(w_s[bass.ds(n, 1), 0].rearrange("o p n -> (o p) n"), whi[i][:, :].bitcast(f32)).then_inc(s_ws[i], 16)
                pool.dma_start(w_s[bass.ds(n, 1), 1].rearrange("o p n -> (o p) n"), wraw[i][:, :].bitcast(f32)).then_inc(s_ws[i], 16)
                if not (end and c == QCH - 1):
                    if not (begin and c == 0):
                        pool.wait_ge(s_ws[1 - i], turn * 32 + (32 if i == 1 else 0))
                    raw(n + 1, 1 - i)

            def finish_unit(u, begin, end):
                for c in range(QCH):
                    finish(u, c, begin, end)

            if phases >= 2:
                for p in range(2):
                    pool.wait_ge(s_qout[p], NCH // 2 * 48)
                for p in range(2):
                    pool.memset(kp[p][:, :, :].bitcast(f32), 0.0).then_inc(s_dconst, 1)
                raw(0, 0)
                finish_unit(0, True, False)
                with pool.Fori(1, NU - 1) as u:
                    finish_unit(u, False, False)
                finish_unit(NU - 1, False, True)

            if phases >= 3:
                with pool.Fori(NCH, NPREP[phases]) as n:
                    inverse_std(n)

        @block.scalar
        def _(act):
            def split_high(n, p):
                for k in range(KC):
                    act.wait_ge(s_tr, n * KC + k + 1)
                    act.activation(xt[p][0][:, k, :], tr[k][:, :], ACT.Copy).then_inc(s_xhi, 1)

            def evacuate(c, p, last):
                if not last:
                    split_high(c + 1, 1 - p)
                if not isinstance(c, int) or c >= 2:
                    act.wait_ge(s_qout[p], c // 2 * 48)
                for m in range(4):
                    act.wait_ge(s_qk, c * 4 + m + 1)
                    act.activation(qst[p][0][:, m, :], pqk[m][:, :], ACT.Copy).then_inc(s_qhi, 1)
                for k in range(2):
                    act.wait_ge(s_vp, c * 2 + k + 1)
                    act.activation(vst[p][:, 2 * k:2 * k + 2, :, 0:HD], pv_[k][:, :, :, :],
                                   ACT.Copy).then_inc(s_ve, 1)

            split_high(0, 0)
            act.wait_ge(s_dconst, 1)
            evacuate(0, 0, False)
            evacuate(1, 1, False)
            with act.Fori(1, NCH // 2 - 1) as i:
                evacuate(2 * i, 0, False)
                evacuate(2 * i + 1, 1, False)
            evacuate(NCH - 2, 0, False)
            evacuate(NCH - 1, 1, True)

            def transposed_max(u, begin):
                if not begin:
                    act.wait_ge(s_m, u * 64)
                act.wait_ge(s_mt, u + 1)
                act.activation(mneg_t[:, :], pp[0:HPG * KT, 0, 0:P], ACT.Copy).then_inc(s_mts, 1)

            def exps(u, p, begin, end):
                for k, (c, j) in enumerate(STEPS):
                    w0 = max(0, j - TPC * c) * P
                    if not (begin and k < PRING):
                        act.wait_ge(s_pv, u * NSTEP + (k - PRING + 1))
                    for r in range(2):
                        act.wait_ge(s_s2, u * (2 * NSTEP) + (2 * k + r + 1))
                        act.activation(pr[k % PRING][:, 2 * r:2 * r + 2, w0:CH], ps2[r][:, :, w0:CH],
                                       ACT.Exp, scale=HD ** -0.5).then_inc(s_ex2, 1)
                    if k == MAX_BY and not end:
                        transposed_max(u + 1, False)

            if phases >= 2:
                for p in range(2):
                    act.wait_ge(s_qout[p], NCH // 2 * 48)
                transposed_max(0, True)
                units(act, exps)

            def gate_exp(g):
                act.wait_ge(s_lgd, g + 1)
                act.activation(sc[:, :, :], lg[:, :, :], ACT.Exp).then_inc(s_ex, 1)

            def gate_out(g):
                act.wait_ge(s_gt, g + 1)
                act.activation(gate_t[:, :], tr[1][0:EXP + 1, :], ACT.Copy).then_inc(s_gts, 1)

            def experts(S, n0, g0, q0):
                def body(c, p, last):
                    for e in range(NE):
                        for k in range(KC):
                            v = KC * e + k
                            act.wait_ge(S["up_a"], c * (2 * NE) + (v + 1))
                            act.wait_ge(S["h"], c * (2 * NE) + (v + 1))
                            act.activation(sil[k][:, :], pup[k][0][:, :], ACT.Silu,
                                           bias=b13[:, 0, v:v + 1]).then_inc(S["silu"], 1)
                            act.wait_ge(S["h"], c * (2 * NE) + (v + 3))
                            act.wait_ge(S["y"], c * (2 * NE) + (2 * e + 2))
                            act.activation(hh[e % 2][0][:, k, :], hf[k][:, :], ACT.Copy).then_inc(S["h_hi"], 1)
                        if e == 2:
                            gate_out(c + q0)
                        if not last:
                            if e == 4:
                                split_high(c + (n0 + 1), 1 - p)
                            if e == 6:
                                gate_exp(c + (g0 + 1))
                return body

            def softplus(c, p, last):
                act.wait_ge(s_dz, c + 1)
                act.activation(e1[:, :, :], zt[:, :, 0:D], ACT.Abs).then_inc(s_dab, 1)
                act.wait_ge(s_dab, c + 1)
                act.activation(e1[:, :, :], e1[:, :, :], ACT.Exp, scale=-1.0).then_inc(s_de, 1)
                act.wait_ge(s_du, c + 1)
                act.activation(l1[:, :, :], u1[:, :, :], ACT.Ln).then_inc(s_dl, 1)
                if not last:
                    split_high(c + (2 * NCH + 1), 1 - p)

            if phases >= 3:
                act.wait_ge(s_ffnc, 64)
                split_high(NCH, 0)
                gate_exp(0)
                pairs(act, NCH, experts(F["C"], NCH, 0, 0), peel_last=phases == 3)
            if phases >= 4:
                pairs(act, NCH, softplus, peel_last=phases == 4)
            if phases >= 5:
                gate_exp(NCH + 1)
                pairs(act, NCH, experts(F["E"], 3 * NCH, NCH + 1, NCH), peel_last=True)

        @block.tensor
        def _(pe):
            def three(out_ap, lh, ll, rh, rl, start, stop):
                pe.matmul(out_ap, lh, rh, start=start, stop=False)
                pe.matmul(out_ap, lh, rl, start=False, stop=False)
                return pe.matmul(out_ap, ll, rh, start=False, stop=stop)

            def transposes(n, begin=False, g=None, q=None):
                pe.wait_ge(s_xn, n + 1)
                if not begin:
                    pe.wait_ge(s_xlo, n * KC)
                if g is not None:
                    pe.wait_ge(s_lgd, g)
                    pe.wait_ge(s_gts, q)
                for k in range(KC):
                    for t in range(TPC):
                        mm = pe.transpose(tr[k][:, t * P:(t + 1) * P], xn[:, t, k * P:(k + 1) * P], ident[:, :])
                    mm.then_inc(s_tr, 1)

            def logits(n, p):
                pe.wait_ge(s_xlo, n * KC + KC)
                for t in range(TPC):
                    ts = slice(t * P, (t + 1) * P)
                    for k in range(KC):
                        mm = three(tr[0][:, t * EXP:(t + 1) * EXP], xt[p][0][:, k, ts], xt[p][1][:, k, ts],
                                   wd[0][:, k, DW:GW], wd[1][:, k, DW:GW], k == 0, k == KC - 1)
                mm.then_inc(s_lg, 1)

            def gates_t(g, n):
                pe.wait_ge(s_gate, g + 1)
                pe.wait_ge(s_xlo, n * KC + KC)
                for t in range(TPC):
                    mm = pe.transpose(tr[1][0:EXP + 1, t * P:(t + 1) * P], gate[:, t, 0:EXP + 1], ident[:, :])
                mm.then_inc(s_gt, 1)

            pe.wait_ge(s_const, 10)
            transposes(0, begin=True)
            pe.wait_ge(s_xlo, KC)
            pe.wait_ge(s_sig, 2)
            for n, (k0, k1) in enumerate(((0, KC), (KC, KC + NG))):
                for k in range(k0, k1):
                    mm = pe.matmul(tr[0][:, n:n + 1], ones[:, :], vsq[:, k:k + 1], start=(k == k0), stop=(k == k1 - 1))
            mm.then_inc(s_sig, 1)
            pe.wait_ge(s_sig, 6)
            for m in range(3 * KC):
                for k in range(KC):
                    pe.matmul(tr[1][:, m:m + 1], wq_raw[:, k, m * P:(m + 1) * P], vn[:, k:k + 1],
                              start=(k == 0), stop=(k == KC - 1))
            for m in range(KC):
                for k in range(NG):
                    mm = pe.matmul(tr[1][:, 3 * KC + m:3 * KC + m + 1], wp_raw[:, k, m * P:(m + 1) * P],
                                   vn[:, KC + k:KC + k + 1], start=(k == 0), stop=(k == NG - 1))
            mm.then_inc(s_sig, 1)
            pe.wait_ge(s_sig, 10)
            pe.matmul(tr[0][:, 8:10], ones[:, :], u2s[:, 0:2], start=True, stop=True).then_inc(s_sig, 1)
            pe.wait_ge(s_sig, 20)

            def project(c, p, last):
                if not last:
                    transposes(c + 1)
                pe.wait_ge(s_xlo, c * KC + KC)
                for m in range(4):
                    if not isinstance(c, int) or c > 0:
                        pe.wait_ge(s_qlo, c * 4 + (m - 3))
                    ms = slice(m * P, (m + 1) * P)
                    for k in range(KC):
                        mm = three(pqk[m][:, :], wq_hl[0][:, k, ms], wq_hl[1][:, k, ms],
                                   xt[p][0][:, k, :], xt[p][1][:, k, :], k == 0, k == KC - 1)
                    mm.then_inc(s_qk, 1)
                for t in range(TPC):
                    if t % 2 == 0 and (not isinstance(c, int) or c > 0):
                        pe.wait_ge(s_ve, c * 2 + (t // 2 - 1))
                    ts = slice(t * P, (t + 1) * P)
                    for k in range(KC):
                        mm = three(pv_[t // 2][:, t % 2, :, :].rearrange("p h w -> p (h w)"),
                                   xt[p][0][:, k, ts], xt[p][1][:, k, ts],
                                   wq_hl[0][:, k, 2 * D:3 * D], wq_hl[1][:, k, 2 * D:3 * D],
                                   k == 0, k == KC - 1)
                    if t % 2 == 1:
                        mm.then_inc(s_vp, 1)

            project(0, 0, False)
            project(1, 1, False)
            with pe.Fori(1, NCH // 2 - 1) as i:
                project(2 * i, 0, False)
                project(2 * i + 1, 1, False)
            project(NCH - 2, 0, False)
            project(NCH - 1, 1, True)

            def max_scores(u, p, bank, begin):
                i, cc, w, hb, n = BANKS[bank]
                if not (begin and bank < 2):
                    pe.wait_ge(s_mx, u * NBANK + (bank - 1))
                diag = cc == i // TPC
                for q in range(hb):
                    h = n * hb + q
                    o = ps1[bank % 2][:, q * w:(q + 1) * w]
                    mm = pe.matmul(o, qp[p][0:ROWS, h // 2, i * P:(i + 1) * P], kp[p][0:ROWS, h, cc * CH:cc * CH + w],
                                   start=True, stop=not diag)
                    if diag:
                        mm = pe.matmul(o[:, w - P:w], identb[:, :], mask_qk[:, :], start=False, stop=True)
                mm.then_inc(s_s1, 1)

            def transpose_max(u, wait_free):
                if wait_free is not None:
                    wait_apart(pe, s_xa, wait_free)
                wait_apart(pe, s_pm, u + 1)
                pe.transpose(pp[0:HPG * KT, 0, 0:P], mneg[:, :], ident[:, :]).then_inc(s_mt, 1)

            def scores(u, p, k, r, begin):
                c, j = STEPS[k]
                w0 = max(0, j - TPC * c) * P
                if not (begin and k == 0):
                    pe.wait_ge(s_ex2, u * (2 * NSTEP) + (2 * k + r - 1))
                for s in range(2):
                    h = 2 * r + s
                    mm = pe.matmul(ps2[r][:, s, w0:CH], kp[p][0:ROWS, h, j * P:(j + 1) * P],
                                   qp[p][0:ROWS, h // 2, c * CH + w0:(c + 1) * CH], start=True, stop=j < TPC * c)
                if j >= TPC * c:
                    for s in range(2):
                        mm = pe.matmul(ps2[r][:, s, w0:w0 + P], identb[:, :], mask_kq[:, :], start=False, stop=True)
                mm.then_inc(s_s2, 1)

            def values(u, p, k, begin):
                c, j = STEPS[k]
                w0 = max(0, j - TPC * c) * P
                pe.wait_ge(s_ex2, u * (2 * NSTEP) + (2 * k + 2))
                if j == 0 and not (begin and c == 0):
                    pe.wait_ge(s_oc, u * QCH + c)
                for h in range(HPG):
                    mm = pe.matmul(po[32 * h:32 * h + 32, w0:CH], vt[p][:, j, 32 * h:32 * h + 32],
                                   pr[k % PRING][:, h, w0:CH], start=(j == 0), stop=(j == TPC * c + TPC - 1))
                mm.then_inc(s_pv, 1)

            def project_out(n, g, half, begin, after_max):
                if half == 0:
                    pe.wait_ge(s_al, n + 1)
                if not (begin and half == 0):
                    pe.wait_ge(s_xa, n * 2 + half)
                if after_max is not None:
                    pe.wait_ge(s_mts, after_max)
                for t in range(2):
                    ts = slice((2 * half + t) * P, (2 * half + t + 1) * P)
                    mm = three(pp[:, t, :], ah[:, ts], al[:, ts],
                               wph[:, bass.ds(g, 1), :].rearrange("p g n -> p (g n)"),
                               wpl[:, bass.ds(g, 1), :].rearrange("p g n -> p (g n)"), True, True)
                mm.then_inc(s_pj, 1)

            def unit(u, p, begin, end):
                turn = u // 2
                pe.wait_ge(s_lv[p], turn * 16 + (HPG + 1) * 16)
                pe.wait_ge(s_m, u * 64 + 64)
                def next_max(banks):
                    for bank in banks:
                        if bank == 0:
                            pe.wait_ge(s_ld[1 - p][0], (u + 1) // 2 * HALF_LD + HALF_LD)
                        if BANKS[bank][0] == KT // 2 and BANKS[bank][1] == 0 and BANKS[bank][4] == 0:
                            pe.wait_ge(s_ld[1 - p][1], (u + 1) // 2 * HALF_LD + HALF_LD)
                        max_scores(u + 1, 1 - p, bank, False)

                for k in range(NSTEP + LAG):
                    banks = max_slot(k) if not end and k < NSTEP else []
                    if k < NSTEP:
                        scores(u, p, k, 0, begin)
                        next_max(banks[0:1])
                        scores(u, p, k, 1, begin)
                        next_max(banks[1:3])
                    if k >= LAG:
                        values(u, p, k - LAG, begin)
                    next_max(banks[3:])
                    if k in (PROJ[3][0], PROJ[3][1]) and not begin:
                        n = u * QCH - 1
                        project_out(n, (u - 1) % NG, PROJ[3].index(k), False, u + 1 if k == PROJ[3][0] else None)
                    for c in range(QCH - 1):
                        if k in PROJ[c]:
                            project_out(u * QCH + c, u % NG, PROJ[c].index(k), begin and c == 0,
                                        u + 1 if begin and c == 0 else None)
                    if k == MAX_BY and not end:
                        transpose_max(u + 1, (u * QCH + QCH - 1) * 2)

            if phases >= 2:
                pe.wait_ge(s_ld[0][0], HALF_LD)
                pe.wait_ge(s_ld[0][1], HALF_LD)
                for bank in range(NBANK):
                    max_scores(0, 0, bank, True)
                transpose_max(0, None)
                units(pe, unit)
                for half in range(2):
                    project_out(NU * QCH - 1, NG - 1, half, False, None)

            def experts(S, n0, g0, q0, weights):
                def up(c, p, e, k):
                    v = KC * e + k
                    if weights and k == 0:
                        pe.wait_ge(s_we[e], 96)
                    pe.wait_ge(S["h"], c * (2 * NE) + (v + 1))
                    ks = slice(k * P, (k + 1) * P)
                    for q, done in enumerate(("up_a", "up_b")):
                        for kk in range(KC):
                            mm = three(pup[k][q][:, :], w13[e][0][:, q, kk, ks], w13[e][1][:, q, kk, ks],
                                       xt[p][0][:, kk, :], xt[p][1][:, kk, :], kk == 0, kk == KC - 1)
                        mm.then_inc(S[done], 1)

                def down(c, e):
                    pe.wait_ge(S["h_lo"], c * (2 * NE) + (2 * e + 2))
                    for half in range(2):
                        pe.wait_ge(S["acc"], c * (2 * NE) + (2 * e + half + 1))
                        for t in range(2):
                            ts = slice((2 * half + t) * P, (2 * half + t + 1) * P)
                            if e == EXP:
                                if t == 0 and half == 0:
                                    pe.wait_ge(s_gts, c + (q0 + 1))
                                pe.matmul(py[half][:, t, :], gate_t[:, ts], b2[:, :], start=True, stop=False)
                            for kk in range(KC):
                                mm = three(py[half][:, t, :], hh[e % 2][0][:, kk, ts], hh[e % 2][1][:, kk, ts],
                                           w2[e][0][:, kk, :], w2[e][1][:, kk, :],
                                           kk == 0 and e != EXP, kk == KC - 1)
                        mm.then_inc(S["y"], 1)

                def body(c, p, last):
                    for e in range(NE):
                        up(c, p, e, 0)
                        up(c, p, e, 1)
                        if e > 0:
                            down(c, e - 1)
                        if e == 2:
                            gates_t(c + g0, c + n0)
                        if not last:
                            if e == 3:
                                transposes(c + (n0 + 1), g=c + (g0 + 1), q=c + (q0 + 1))
                            if e == 5:
                                logits(c + (n0 + 1), 1 - p)
                    down(c, NE - 1)
                return body

            def gate_stage(c, p, last):
                pe.wait_ge(s_xlo, (c + 2 * NCH) * KC + KC)
                for t in range(TPC):
                    ts = slice(t * P, (t + 1) * P)
                    for k in range(KC):
                        mm = three(pd[t][:, 0:DW], xt[p][0][:, k, ts], xt[p][1][:, k, ts],
                                   wd[0][:, k, 0:DW], wd[1][:, k, 0:DW], k == 0, k == KC - 1)
                    mm.then_inc(s_dp, 1)
                if not last:
                    transposes(c + (2 * NCH + 1), g=NCH + 1, q=NCH)

            if phases >= 3:
                pe.wait_ge(s_wd, 64)
                pe.wait_ge(s_xa, 2 * QCH * NU)
                transposes(NCH)
                logits(NCH, 0)
                pairs(pe, NCH, experts(F["C"], NCH, 0, 0, True), peel_last=phases == 3)
            if phases >= 4:
                pe.wait_ge(F["C"]["acc"], NCH * 2 * NE + 2)
                pairs(pe, NCH, gate_stage, peel_last=phases == 4)
            if phases >= 5:
                pe.wait_ge(s_dx, NCH)
                logits(3 * NCH, 0)
                pairs(pe, NCH, experts(F["E"], 3 * NCH, NCH + 1, NCH, False), peel_last=True)

        @block.vector
        def _(dve):
            def statistics(n, t0):
                for t in range(TPC):
                    i = dve.bn_stats(stats[:, t, :], x[:, bass.ds(t0 + t, 1), :].rearrange("p o d -> p (o d)"))
                i.then_inc(s_stats, 1)
                wait_apart(dve, s_stats, n + 1)
                for t in range(TPC):
                    i = dve.bn_aggr(mv[:, t, :], stats[:, t, :])
                i.then_inc(s_aggr, 1)
                dve.wait_ge(s_aggr, n + 1)
                dve.tensor_scalar(vare[:, :], mv[:, :, 1], EPS, None, ALU.add).then_inc(s_var, 1)

            def normalise(n, t0):
                dve.wait_ge(s_rstd, n + 1)
                if not isinstance(n, int) or n > 0:
                    dve.wait_ge(s_tr, n * KC)
                for t in range(TPC):
                    i = dve.tensor_scalar(xn[:, t, :], x[:, bass.ds(t0 + t, 1), :].rearrange("p o d -> p (o d)"),
                                          mv[:, t, 0:1], rstd[:, t:t + 1], ALU.subtract, ALU.mult)
                i.then_inc(s_xn, 1)

            def split_low(n, p):
                for k in range(KC):
                    dve.wait_ge(s_xhi, n * KC + k + 1)
                    dve.tensor_tensor(xt[p][1][:, k, :], tr[k][:, :], xt[p][0][:, k, :].bitcast(f32),
                                      ALU.subtract).then_inc(s_xlo, 1)

            ROUTE = 17

            def over(col):
                return col[:, :].unsqueeze(2).to_broadcast([P, TPC, EXP])

            def route_logits(g):
                dve.wait_ge(s_lg, g + 1)
                dve.tensor_tensor(lg[:, :, :], tr[0][:, 0:TPC * EXP].rearrange("p (t e) -> p t e", e=EXP),
                                  gb[:, :, :], ALU.add).then_inc(s_rt, 1)
                dve.wait_ge(s_rt, g * ROUTE + 1)
                dve.tensor_reduce(mx[:, :], lg[:, :, :], AX.X, ALU.max).then_inc(s_rt, 1)
                dve.wait_ge(s_rt, g * ROUTE + 2)
                dve.tensor_tensor(lg[:, :, :], lg[:, :, :], over(mx), ALU.subtract).then_inc(s_lgd, 1)

            def route(g):
                at = [2]

                def step(ins):
                    at[0] += 1
                    ins.then_inc(s_rt, 1)
                    dve.wait_ge(s_rt, g * ROUTE + at[0])

                dve.wait_ge(s_ex, g + 1)
                step(dve.tensor_reduce(mx[:, :], sc[:, :, :], AX.X, ALU.add))
                step(dve.reciprocal(mx[:, :], mx[:, :]))
                step(dve.tensor_tensor(sc[:, :, :], sc[:, :, :], over(mx), ALU.mult))
                for src, hot in ((sc, oh), (lg, eq)):
                    step(dve.tensor_reduce(mx[:, :], src[:, :, :], AX.X, ALU.max))
                    step(dve.tensor_tensor(eq[:, :, :], src[:, :, :], over(mx), ALU.is_equal))
                    step(dve.tensor_tensor(eq[:, :, :], eq[:, :, :], rev[:, :, :], ALU.mult))
                    step(dve.tensor_reduce(mx[:, :], eq[:, :, :], AX.X, ALU.max))
                    step(dve.tensor_tensor(hot[:, :, :], eq[:, :, :], over(mx), ALU.is_equal))
                    if hot is oh:
                        step(dve.scalar_tensor_tensor(lg[:, :, :], oh[:, :, :], -2.0, sc[:, :, :], ALU.mult, ALU.add))
                step(dve.tensor_tensor(eq[:, :, :], eq[:, :, :], oh[:, :, :], ALU.add))
                assert at[0] == ROUTE, at[0]
                dve.tensor_tensor(gate[:, :, 0:EXP], sc[:, :, :], eq[:, :, :], ALU.mult).then_inc(s_gate, 1)

            for ph in "CE":
                dve.sem_inc(F[ph]["h"], 2)
                dve.sem_inc(F[ph]["acc"], 2)
                dve.sem_inc(F[ph]["y"], 4)
            dve.memset(wp_raw[:, :, :], 0.0)
            for p in range(2):
                i = dve.memset(vst[p][:, :, :, :], 1.0)
            i.then_inc(s_dconst, 1)

            dve.wait_ge(s_x0, 16)
            statistics(0, 0)
            normalise(0, 0)
            split_low(0, 0)
            dve.wait_ge(s_w, 9 * 16)
            for k in range(KC):
                dve.tensor_tensor_reduce(out=prod[:, k * 3 * D:(k + 1) * 3 * D], in0=wq_raw[:, k, :], in1=ub[:, 0:3 * D], scale=1.0, scalar=0.0,
                                         op0=ALU.mult, op1=ALU.add, accum_out=vr[:, k:k + 1])
            for k in range(NG):
                i = dve.tensor_tensor_reduce(out=prod[:, KC * 3 * D + k * D:KC * 3 * D + (k + 1) * D], in0=wp_raw[:, k, :], in1=ub[:, 3 * D:4 * D], scale=1.0,
                                             scalar=0.0, op0=ALU.mult, op1=ALU.add, accum_out=vr[:, KC + k:KC + k + 1])
            i.then_inc(s_sig, 1)
            dve.wait_ge(s_sig, 1)
            dve.tensor_tensor(vsq[:, :], vr[:, :], vr[:, :], ALU.mult).then_inc(s_sig, 1)
            dve.wait_ge(s_sig, 3)
            dve.tensor_copy(nrm[:, :], tr[0][:, 0:2]).then_inc(s_sig, 1)
            dve.wait_ge(s_sig, 5)
            dve.tensor_scalar(vn[:, 0:KC], vr[:, 0:KC], rn[:, 0:1], None, ALU.mult)
            dve.tensor_scalar(vn[:, KC:KC + NG], vr[:, KC:KC + NG], rn[:, 1:2], None, ALU.mult).then_inc(s_sig, 1)
            dve.wait_ge(s_sig, 7)
            dve.tensor_copy(u2[:, :], tr[1][:, 0:8]).then_inc(s_sig, 1)
            dve.wait_ge(s_sig, 8)
            dve.tensor_tensor(u2q[:, :], u2[:, :], u2[:, :], ALU.mult).then_inc(s_sig, 1)
            dve.wait_ge(s_sig, 9)
            dve.tensor_reduce(u2s[:, 0:1], u2q[:, 0:3 * KC], AX.X, ALU.add)
            dve.tensor_reduce(u2s[:, 1:2], u2q[:, 3 * KC:4 * KC], AX.X, ALU.add).then_inc(s_sig, 1)
            dve.wait_ge(s_sig, 11)
            dve.tensor_copy(sg[:, :], tr[0][:, 8:10]).then_inc(s_sig, 1)
            dve.wait_ge(s_sig, 13)
            dve.tensor_tensor(scl[:, :], rs[:, :], sp_in[:, :], ALU.mult).then_inc(s_sig, 1)
            dve.wait_ge(s_sig, 14)
            dve.tensor_scalar(wq_raw[:, :, :], wq_raw[:, :, :], scl[:, 0:1], None, ALU.mult).then_inc(s_sig, 1)
            dve.tensor_scalar(wp_raw[:, :, :], wp_raw[:, :, :], scl[:, 1:2], None, ALU.mult).then_inc(s_sig, 1)
            dve.wait_ge(s_sig, 16)
            dve.tensor_copy(wq_hl[0][:, :, :], wq_raw[:, :, :]).then_inc(s_sig, 1)
            dve.tensor_copy(wph[:, :, :], wp_raw[:, :, :]).then_inc(s_sig, 1)
            dve.wait_ge(s_sig, 18)
            dve.tensor_tensor(wq_hl[1][:, :, :], wq_raw[:, :, :], wq_hl[0][:, :, :].bitcast(f32),
                              ALU.subtract).then_inc(s_sig, 1)
            dve.tensor_tensor(wpl[:, :, :], wp_raw[:, :, :], wph[:, :, :].bitcast(f32), ALU.subtract).then_inc(s_sig, 1)

            dve.wait_ge(s_xr, (NCH - 1) * 16)

            def low_parts(c, p, last):
                if not last:
                    statistics(c + 1, (c + 1) * TPC)
                    normalise(c + 1, (c + 1) * TPC)
                    split_low(c + 1, 1 - p)
                for m in range(4):
                    dve.wait_ge(s_qhi, c * 4 + m + 1)
                    dve.tensor_tensor(qst[p][1][:, m, :], pqk[m][:, :], qst[p][0][:, m, :].bitcast(f32),
                                      ALU.subtract).then_inc(s_qlo, 1)

            pairs(dve, NCH, low_parts, peel_last=True)

            def take_max(u, p, bank):
                i, cc, w, hb, n = BANKS[bank]
                dve.wait_ge(s_s1, u * NBANK + (bank + 1))
                dve.tensor_reduce(part[p][:, n * hb:(n + 1) * hb, i, cc], ps1[bank % 2][:, 0:hb * w].rearrange("p (h w) -> p h w", w=w),
                                  AX.X, ALU.max, negate=True).then_inc(s_mx, 1)

            def join_max(u, p, begin):
                if not begin:
                    dve.wait_ge(s_mt, u)
                dve.wait_ge(s_mx, u * NBANK + NBANK)
                dve.tensor_reduce(mneg[:, :], part[p][:, :, :, :].rearrange("p h i c -> p (h i) c"),
                                  AX.X, ALU.min).then_inc(s_pm, 1)

            def reciprocals(n, done, begin):
                dve.wait_ge(s_pv, done)
                if not begin:
                    dve.wait_ge(s_al, n)
                dve.tensor_copy(osb[:, :], po[:, :]).then_inc(s_oc, 1)
                dve.wait_ge(s_oc, n + 1)
                dve.reciprocal(rden[:, :], osb[:, :]).then_inc(s_rd, 1)
                wait_apart(dve, s_rd, n + 1)
                dve.stream_shuffle(rdb[:, :], rden[:, :], [HD + i % HD for i in range(32)]).then_inc(s_sh, 1)

            def add_out(n, t0, half):
                dve.wait_ge(s_pj, n * 2 + (half + 1))
                xs = x[:, bass.ds(t0 + 2 * half, 2), :]
                dve.tensor_tensor(xs, xs, pp[:, :, :], ALU.add).then_inc(s_xa, 1)

            def unit(u, p, begin, end):
                for k in range(NSTEP + LAG):
                    if not end and k < NSTEP:
                        for bank in max_slot(k):
                            take_max(u + 1, 1 - p, bank)
                    if k == MAX_BY - 1 and not end:
                        join_max(u + 1, 1 - p, False)
                    if k in PROJ[3] and not begin:
                        n, v = u * QCH - 1, u - 1
                        add_out(n, v // NG * KT + (QCH - 1) * TPC, PROJ[3].index(k))
                    for c in range(QCH - 1):
                        if k in PROJ[c]:
                            add_out(u * QCH + c, u // NG * KT + c * TPC, PROJ[c].index(k))
                    if k >= LAG and STEPS[k - LAG][1] == TPC * (STEPS[k - LAG][0] + 1) - 1:
                        c = STEPS[k - LAG][0]
                        reciprocals(u * QCH + c, u * NSTEP + (k - LAG + 1), begin and c == 0)

            if phases >= 2:
                for p in range(2):
                    dve.wait_ge(s_qout[p], NCH // 2 * 48)
                for p in range(2):
                    dve.memset(qp[p][:, :, :].bitcast(f32), 0.0)
                    i = dve.memset(part[p][:, :, :, :], 3e38)
                i.then_inc(s_dconst, 1)
                dve.wait_ge(s_dconst, 4)
                for bank in range(NBANK):
                    take_max(0, 0, bank)
                join_max(0, 0, True)
                units(dve, unit)
                for half in range(2):
                    add_out(NU * QCH - 1, (NU - 1) // NG * KT + (QCH - 1) * TPC, half)

            def experts(S, n0, g0):
                def body(c, p, last):
                    nt = (c + 1) % NCH * TPC
                    n, g = c + (n0 + 1), c + (g0 + 1)

                    def add_expert(e):
                        for half in range(2):
                            dve.wait_ge(S["y"], c * (2 * NE) + (2 * e + half + 5))
                            for t in range(2):
                                tile = 2 * half + t
                                xs = x[:, bass.ds(c * TPC + tile, 1), :].rearrange("p o d -> p (o d)")
                                i = dve.scalar_tensor_tensor(xs, py[half][:, t, :], gate[:, tile, e:e + 1], xs,
                                                             ALU.mult, ALU.add)
                            i.then_inc(S["acc"], 1)

                    for e in range(NE):
                        for k in range(KC):
                            v = KC * e + k
                            dve.wait_ge(S["silu"], c * (2 * NE) + (v + 1))
                            dve.wait_ge(S["up_b"], c * (2 * NE) + (v + 1))
                            dve.scalar_tensor_tensor(hf[k][:, :], pup[k][1][:, :], b13[:, 1, v:v + 1], sil[k][:, :],
                                                     ALU.add, ALU.mult).then_inc(S["h"], 1)
                            dve.wait_ge(S["h_hi"], c * (2 * NE) + (v + 1))
                            dve.tensor_tensor(hh[e % 2][1][:, k, :], hf[k][:, :], hh[e % 2][0][:, k, :].bitcast(f32),
                                              ALU.subtract).then_inc(S["h_lo"], 1)
                        if e > 0:
                            add_expert(e - 1)
                        if not last:
                            if e == 1:
                                statistics(n, nt)
                            if e == 2:
                                normalise(n, nt)
                            if e == 4:
                                split_low(n, 1 - p)
                            if e == 6:
                                route_logits(g)
                    add_expert(NE - 1)
                    if not last:
                        route(g)
                return body

            def gate_stage(c, p, last):
                for t in range(TPC):
                    dve.wait_ge(s_dp, c * TPC + (t + 1))
                    i = dve.tensor_tensor(zt[:, t, :], pd[t][:, 0:DW], bd[:, :], ALU.add)
                i.then_inc(s_dz, 1)
                dve.wait_ge(s_dz, c + 1)
                nt, n = (c + 1) % NCH * TPC, c + (2 * NCH + 1)
                if not last:
                    statistics(n, nt)
                dve.tensor_tensor(bcp[:, :, :], zt[:, :, D:D + NST], zt[:, :, D + NST:DW], ALU.mult).then_inc(s_dbc, 1)
                dve.wait_ge(s_dbc, c * 2 + 1)
                dve.tensor_reduce(bcs[:, :], bcp[:, :, :], AX.X, ALU.add).then_inc(s_dbc, 1)
                dve.wait_ge(s_de, c + 1)
                dve.tensor_scalar(u1[:, :, :], e1[:, :, :], 1.0, None, ALU.add).then_inc(s_du, 1)
                dve.wait_ge(s_du, c + 1)
                dve.scalar_tensor_tensor(e1[:, :, :], u1[:, :, :], 1.0, e1[:, :, :], ALU.subtract,
                                         ALU.subtract).then_inc(s_dr, 1)
                dve.wait_ge(s_dr, c * 4 + 1)
                dve.wait_ge(s_dl, c + 1)
                dve.tensor_tensor(l1[:, :, :], l1[:, :, :], e1[:, :, :], ALU.subtract).then_inc(s_dr, 1)
                dve.wait_ge(s_dr, c * 4 + 2)
                dve.scalar_tensor_tensor(l1[:, :, :], zt[:, :, 0:D], 0.0, l1[:, :, :], ALU.max, ALU.add).then_inc(s_dr, 1)
                dve.wait_ge(s_dr, c * 4 + 3)
                dve.tensor_tensor(l1[:, :, :], l1[:, :, :], xn[:, :, :], ALU.mult).then_inc(s_dr, 1)
                dve.wait_ge(s_dr, c * 4 + 4)
                dve.wait_ge(s_dbc, c * 2 + 2)
                for t in range(TPC):
                    xs = x[:, bass.ds(c * TPC + t, 1), :].rearrange("p o d -> p (o d)")
                    i = dve.scalar_tensor_tensor(xs, l1[:, t, :], bcs[:, t:t + 1], xs, ALU.mult, ALU.add)
                i.then_inc(s_dx, 1)
                if not last:
                    normalise(n, nt)
                    split_low(n, 1 - p)

            if phases >= 3:
                dve.wait_ge(s_wd, 64)
                dve.wait_ge(s_ffnc, 64)
                for e in range(EXP):
                    dve.memset(rev[:, :, e], float(EXP - e))
                dve.memset(gate[:, :, EXP:NE], 1.0).then_inc(s_dconst, 1)
                dve.wait_ge(s_dconst, 5)
                statistics(NCH, 0)
                normalise(NCH, 0)
                split_low(NCH, 0)
                route_logits(0)
                route(0)
                pairs(dve, NCH, experts(F["C"], NCH, 0), peel_last=phases == 3)
            if phases >= 4:
                pairs(dve, NCH, gate_stage, peel_last=phases == 4)
            if phases >= 5:
                route_logits(NCH + 1)
                route(NCH + 1)
                pairs(dve, NCH, experts(F["E"], 3 * NCH, NCH + 1), peel_last=True)


_KINDS = ["x_in", "wqkv_in", "uqkv_in", "sqkv_in", "wproj_in", "uproj_in", "sproj_in",
          "wffn_in", "b13_in", "b2_in", "gb_in", "bd_in"]


def kernel(**inputs):
    import numpy as np
    import concourse.bacc as bacc
    from concourse.bass_utils import run_bass_kernel_spmd

    a = {k.removeprefix("L0_"): np.asarray(v) for k, v in inputs.items()}

    def rows(m):
        return m.reshape(KC, P, -1).transpose(1, 0, 2).reshape(P, -1)

    pieces = []
    for e in range(NE):
        if e < EXP:
            up, gated, down = a["ffn_w1"][e].T, a["ffn_w3"][e].T, a["ffn_w2"][e].T
        else:
            s = slice((e - EXP) * D, (e - EXP + 1) * D)
            up, gated, down = a["ffn_ws1"][s].T, a["ffn_ws3"][s].T, a["ffn_ws2"][:, s].T
        pieces += [rows(up), rows(gated), rows(down)]
    pieces.append(rows(a["attn_b_W1"].T))
    rest = [a["attn_b_W2"].T, a["attn_b_W3"].T, a["ffn_gate_w"].T]
    rest.append(np.zeros((D, D - 2 * NST - EXP), rest[0].dtype))
    pieces.append(rows(np.concatenate(rest, axis=1)))

    def hidden(m, s):
        return np.concatenate([m.reshape(-1), s]).reshape(NE * KC, P).T

    b13 = np.stack([hidden(a["ffn_b1"], a["ffn_bs1"]), hidden(a["ffn_b3"], a["ffn_bs3"])], axis=1)
    arrays = [a["attn_a_batch"], a["attn_a_W_qkv"], a["attn_a_u_qkv"], a["attn_a_sigma_qkv"], a["attn_a_W_proj"],
              a["attn_a_u_proj"], a["attn_a_sigma_proj"], np.stack(pieces), b13,
              np.concatenate([a["ffn_b2"], a["ffn_bs2"][None]]), a["ffn_gate_b"],
              np.concatenate([a["attn_b_b1"], a["attn_b_b2"], a["attn_b_b3"]])]
    nc = bacc.Bacc("TRN2", target_bir_lowering=False, num_devices=1)
    feeds, args = {}, []
    for name, v in zip(_KINDS, arrays):
        feeds[name] = np.ascontiguousarray(v)
        args.append(nc.dram_tensor(name, v.shape, mybir.dt.from_np(v.dtype), kind="ExternalInput").ap())
    args.append(nc.dram_tensor("x_out", (B, N, D), mybir.dt.float32, kind="ExternalOutput").ap())
    build(nc, *args)
    return run_bass_kernel_spmd(nc, [feeds], core_ids=[0]).results[0]["x_out"]
```

```python
import concourse.bass as bass
from concourse import mybir
from contextlib import ExitStack

P = 128
B, N, D = 2, 2048, 256
H, HD = 16, 16
KC = D // P
TOK = B * N
CH = 512
TPC = CH // P
NCH = TOK // CH
EXP = 8
NE = 10
NST = 16
DW = D + 2 * NST
GW = DW + EXP
EPS = 1e-5
NEG = -1e30

HPG = 4
NG = H // HPG
NU = B * NG
QCH = N // CH
KT = N // P
PACK = 3 * HD
MROW = PACK

NPIECE = 3 * NE + 2
ROWS = 64 + MROW + 1
HALF_LD = 14 * 16
STEPS = [(c, j) for c in range(QCH) for j in range(TPC * (c + 1))]
NSTEP = len(STEPS)
LAG = 2
PRING = 4
RECIP, SPREAD = 2, 4
PROJ = ((12, 13), (20, 21), (32, 33), (7, 8))
NPREP = {3: 2 * NCH, 4: 3 * NCH, 5: 4 * NCH}
MAXES = []
for _i in range(KT):
    for _c in range(_i // TPC + 1):
        _w = min(CH, (_i + 1) * P - _c * CH)
        MAXES.append((_i, _c, _w, CH // _w))
NBANK = sum(HPG // hb for _, _, _, hb in MAXES)
EARLY = NSTEP - TPC * (QCH // 2)
MAX_FROM, MAX_BY = 0, NSTEP - 2


BANKS = [(i, c, w, hb, n) for i, c, w, hb in MAXES for n in range(HPG // hb)]


def max_slot(k):
    total = sum(w * hb for _, _, w, hb, _ in BANKS)
    lo = total * (k - MAX_FROM) / (MAX_BY - MAX_FROM)
    hi = total * (k + 1 - MAX_FROM) / (MAX_BY - MAX_FROM)
    at, n = 0, []
    for bank, (_, _, w, hb, _) in enumerate(BANKS):
        if lo <= at < hi:
            n.append(bank)
        at += w * hb
    return n


def build(nc, x_in, wqkv_in, uqkv_in, sqkv_in, wproj_in, uproj_in, sproj_in,
          wffn_in, b13_in, b2_in, gb_in, bd_in, out, phases=5):
    f32, f32r, bf16 = mybir.dt.float32, mybir.dt.float32r, mybir.dt.bfloat16
    ALU = mybir.AluOpType
    ACT = mybir.ActivationFunctionType
    AX = mybir.AxisListType

    qk_s = nc.dram_tensor("qk_split", [2, 2 * D, TOK], f32, kind="Internal").ap()
    v_s = nc.dram_tensor("v_ones", [TOK, H * 32], f32, kind="Internal").ap()
    w_s = nc.dram_tensor("w_split", [NPIECE, 2, P, KC * D], f32, kind="Internal").ap()

    ctx = ExitStack()
    with ctx:
        def sb(name, shape, dt=f32, stack=ctx):
            return stack.enter_context(nc.sbuf_tensor(name, shape, dt))

        def sem(name):
            return ctx.enter_context(nc.semaphore(name))

        x = sb("x", [P, TOK // P, D])
        tok = ExitStack()
        xn = sb("xn", [P, TPC, D], f32, tok)
        xt = [[sb(f"xt{p}{h}", [P, KC, CH], f32r, tok) for h in range(2)] for p in range(2)]
        tok.close()
        pr = [sb(f"pr{i}", [P, HPG, CH]) for i in range(2)]
        osb = sb("osb", [P, CH])
        rdb = sb("rdb", [P, CH])
        stats = sb("stats", [P, TPC, 6])
        mv = sb("mv", [P, TPC, 2])
        vare = sb("vare", [P, TPC])
        rstd = sb("rstd", [P, TPC])
        mhalf = sb("mhalf", [P, TPC])
        ones = sb("ones", [P, P])
        ident = sb("ident", [P, P])
        att = ExitStack()
        identb = sb("identb", [P, P], bf16, att)
        mask_qk = sb("mask_qk", [P, P], bf16, att)
        mask_kq = sb("mask_kq", [P, P], bf16, att)
        wph = sb("wph", [P, NG, D], f32r, att)
        wpl = sb("wpl", [P, NG, D], f32r, att)
        wraw = [sb(f"wraw{i}", [P, KC * D], f32r, att) for i in range(2)]
        whi = [sb(f"whi{i}", [P, KC * D], f32r, att) for i in range(2)]
        prj = ExitStack()
        wq_raw = sb("wq_raw", [P, KC, 3 * D], f32, prj)
        wq_hl = [sb(f"wq_{h}", [P, KC, 3 * D], f32r, prj) for h in range(2)]
        wp_raw = sb("wp_raw", [P, NG, D], f32, prj)
        ub = sb("ub", [P, 3 * D + D], f32, prj)
        prod = sb("prod", [P, KC * 3 * D + NG * D], f32, prj)
        vr = sb("vr", [P, KC + NG], f32, prj)
        vsq = sb("vsq", [P, KC + NG], f32, prj)
        vn = sb("vn", [P, KC + NG], f32, prj)
        nrm = sb("nrm", [P, 2], f32, prj)
        rn = sb("rn", [P, 2], f32, prj)
        u2 = sb("u2", [P, 8], f32, prj)
        u2q = sb("u2q", [P, 8], f32, prj)
        u2s = sb("u2s", [P, 2], f32, prj)
        sg = sb("sg", [P, 2], f32, prj)
        rs = sb("rs", [P, 2], f32, prj)
        sp_in = sb("sp_in", [P, 2], f32, prj)
        scl = sb("scl", [P, 2], f32, prj)
        qst = [[sb(f"qst{p}{h}", [P, 4, CH], f32r, prj) for h in range(2)] for p in range(2)]
        vst = [sb(f"vst{p}", [P, TPC, H, 32], f32, prj) for p in range(2)]
        prj.close()
        qp1 = sb("qp1", [P, 2, N], f32r, att)
        kp1 = sb("kp1", [P, HPG, N], f32r, att)
        vt = [sb(f"vt{p}", [P, KT, HPG * 32], f32, att) for p in range(2)]
        pr += [sb(f"pr{i}", [P, HPG, CH], f32, att) for i in range(2, PRING)]
        rden = sb("rden", [P, CH], f32, att)
        ah = sb("ah", [P, CH], f32r, att)
        al = sb("al", [P, CH], f32r, att)
        qp = [sb("qp0", [P, 2, N], f32r, att), qp1]
        kp = [sb("kp0", [P, HPG, N], f32r, att), kp1]
        part = [sb(f"part{p}", [P, HPG, KT, QCH], f32, att) for p in range(2)]
        mneg = sb("mneg", [P, HPG * KT], f32, att)
        mneg_t = sb("mneg_t", [HPG * KT, P], f32r, att)
        dsum = sb("dsum", [P, HPG * CH // P], f32, att)
        att.close()
        ffn = ExitStack()
        w13 = [[sb(f"w13_{e}_{h}", [P, 2, KC, D], f32r, ffn) for h in range(2)] for e in range(NE)]
        w2 = [[sb(f"w2_{e}_{h}", [P, KC, D], f32r, ffn) for h in range(2)] for e in range(NE)]
        wd = [sb(f"wd_{h}", [P, KC, GW], f32r, ffn) for h in range(2)]
        b13 = sb("b13", [P, 2, NE * KC], f32, ffn)
        b2 = sb("b2", [EXP + 1, D], f32, ffn)
        gb = sb("gb", [P, TPC, EXP], f32, ffn)
        bd = sb("bd", [P, DW], f32, ffn)
        rev = sb("rev", [P, TPC, EXP], f32, ffn)
        gate = sb("gate", [P, TPC, NE], f32, ffn)
        gate_t = sb("gate_t", [EXP + 1, CH], f32, ffn)
        lg = sb("lg", [P, TPC, EXP], f32, ffn)
        sc = sb("sc", [P, TPC, EXP], f32, ffn)
        eq = sb("eq", [P, TPC, EXP], f32, ffn)
        oh = sb("oh", [P, TPC, EXP], f32, ffn)
        mx = sb("mx", [P, TPC], f32, ffn)
        hst = ExitStack()
        hh = [[sb(f"hh{p}{h}", [P, KC, CH], f32r, hst) for h in range(2)] for p in range(2)]
        sil = [sb(f"sil{p}", [P, CH], f32, hst) for p in range(2)]
        hf = [sb(f"hf{p}", [P, CH], f32, hst) for p in range(2)]
        hst.close()
        xn_b = sb("xn_b", [P, TPC, D], f32, hst)
        zt = sb("zt", [P, TPC, DW], f32, hst)
        e1 = sb("e1", [P, TPC, D], f32, hst)
        l1 = sb("l1", [P, TPC, D], f32, hst)
        u1 = sb("u1", [P, TPC, D], f32, hst)
        bcp = sb("bcp", [P, TPC, NST], f32, hst)
        bcs = sb("bcs", [P, TPC], f32, hst)
        hst.close()
        ffn.close()

        def ps(name, shape, stack):
            return stack.enter_context(nc.psum_tensor(name, shape, f32))

        pa = ExitStack()
        tr = [ps(f"tr{k}", [P, CH], pa) for k in range(2)]
        pa2 = ExitStack()
        pqk = [ps(f"pqk{m}", [P, CH], pa2) for m in range(4)]
        pv_ = [ps(f"pv{k}", [P, 2, H, HD], pa2) for k in range(2)]
        pa2.close()
        pup = [[ps(f"pup{p}{k}", [P, CH], pa2) for k in range(2)] for p in range(2)]
        py = [ps(f"py{k}", [P, 2, D], pa2) for k in range(2)]
        pa2.close()
        pd = [ps(f"pd{t}", [P, CH], pa2) for t in range(TPC)]
        pa2.close()
        pa.close()
        ps2 = [ps(f"ps2_{k}", [P, 2, CH], pa) for k in range(2)]
        ps1 = [ps(f"ps1_{k}", [P, CH], pa) for k in range(2)]
        po = ps("po", [P, CH], pa)
        pp = ps("pp", [P, 2, D], pa)
        pa.close()

        every = [ps1[0], ps1[1]] + [ps2[k][:, i, :] for k in range(2) for i in range(2)]

        s_x0, s_xr, s_w, s_ffnc = sem("s_x0"), sem("s_xr"), sem("s_w"), sem("s_ffnc")
        s_zero = [sem("s_zero0"), sem("s_zero1")]
        s_const, s_dconst = sem("s_const"), sem("s_dconst")
        s_sig = sem("s_sig")
        s_stats, s_aggr, s_var, s_rstd, s_xn = (sem(n) for n in ("s_stats", "s_aggr", "s_var", "s_rstd", "s_xn"))
        s_tr, s_xhi, s_xlo = sem("s_tr"), sem("s_xhi"), sem("s_xlo")
        s_lg, s_lgd, s_ex, s_gate, s_gt, s_gts = (sem(n) for n in ("s_lg", "s_lgd", "s_ex", "s_gate", "s_gt", "s_gts"))
        s_rt = sem("s_rt")
        s_qk, s_qhi, s_qlo, s_vp, s_ve = (sem(n) for n in ("s_qk", "s_qhi", "s_qlo", "s_vp", "s_ve"))
        s_qout = [sem("s_qout0"), sem("s_qout1")]
        s_ld = [[sem(f"s_ld{p}{h}") for h in range(2)] for p in range(2)]
        s_lv = [sem("s_lv0"), sem("s_lv1")]
        s_m = sem("s_m")
        s_s1, s_mx, s_pm, s_mt, s_mts = (sem(n) for n in ("s_s1", "s_mx", "s_pm", "s_mt", "s_mts"))
        s_s2, s_ex2, s_pv = sem("s_s2"), sem("s_ex2"), sem("s_pv")
        s_oc, s_dg, s_rd, s_rg, s_sh, s_am, s_ah, s_al = (sem(n) for n in ("s_oc", "s_dg", "s_rd", "s_rg", "s_sh", "s_am", "s_ah", "s_al"))
        s_pj, s_xa = sem("s_pj"), sem("s_xa")
        s_wr = [sem("s_wr0"), sem("s_wr1")]
        s_wh, s_wl = sem("s_wh"), sem("s_wl")
        s_ws = [sem("s_ws0"), sem("s_ws1")]
        s_we = [sem(f"s_we{e}") for e in range(NE)]
        s_wd = sem("s_wd")
        names = ("up_a", "up_b", "silu", "h", "h_hi", "h_lo", "y", "acc")
        F = {ph: {n: sem(f"s_{n}_{ph}") for n in names} for ph in "CE"}
        s_dp, s_dz, s_dab, s_de, s_du, s_dl, s_dr, s_dx, s_dbc = (
            sem(n) for n in ("s_dp", "s_dz", "s_dab", "s_de", "s_du", "s_dl", "s_dr", "s_dx", "s_dbc"))
        s_out = sem("s_out")

        block = ctx.enter_context(nc.Block())

        x_v = x_in.rearrange("b (k t p) d -> (b k) p t d", t=TPC, p=P)
        o_v = out.rearrange("b (k t p) d -> (b k) p t d", t=TPC, p=P)
        def pairs(eng, count, body, peel_last=False):
            turns = count // 2 - (1 if peel_last else 0)
            with eng.Fori(0, turns) as i:
                body(2 * i, 0, False)
                body(2 * i + 1, 1, False)
            if peel_last:
                body(count - 2, 0, False)
                body(count - 1, 1, True)

        def chunks(eng, body, final):
            body(0, 0, False)
            body(1, 1, False)
            with eng.Fori(1, NCH // 2 - 1) as i:
                body(2 * i, 0, False)
                body(2 * i + 1, 1, False)
            body(NCH - 2, 0, False)
            body(NCH - 1, 1, final)

        def wait_apart(eng, semaphore, value):
            if not isinstance(value, int):
                value = eng.to_reg(value)
            eng.wait_ge(s_const, 1)
            eng.wait_ge(semaphore, value)

        def units(eng, body):
            body(0, 0, True, False)
            with eng.Fori(0, (NU - 2) // 2) as i:
                body(2 * i + 1, 1, False, False)
                body(2 * i + 2, 0, False, False)
            body(NU - 1, 1, False, True)

        @block.sync
        def _(sp):
            sp.dma_start(x[:, 0:TPC, :], x_v[0]).then_inc(s_x0, 16)
            sp.dma_start(wq_raw[:, :, :], wqkv_in.rearrange("(k p) n -> p k n", p=P)).then_inc(s_w, 16)
            sp.dma_start(ub[:, 0:3 * D], uqkv_in[None, :].to_broadcast([P, 3 * D])).then_inc(s_w, 16)
            sp.dma_start(ub[:, 3 * D:4 * D], uproj_in[None, :].to_broadcast([P, D])).then_inc(s_w, 16)
            sp.dma_start(sp_in[:, 0:1], sqkv_in[None, :].to_broadcast([P, 1])).then_inc(s_w, 16)
            sp.dma_start(sp_in[:, 1:2], sproj_in[None, :].to_broadcast([P, 1])).then_inc(s_w, 16)
            wp_v = wproj_in.rearrange("(g h d) n -> h d g n", h=HPG, d=HD)
            sp.wait_ge(s_dconst, 1)
            for h in range(HPG):
                sp.dma_start(wp_raw[32 * h:32 * h + HD, :, :], wp_v[h]).then_inc(s_w, 16)
            for c in range(1, NCH):
                sp.dma_start(x[:, c * TPC:(c + 1) * TPC, :], x_v[c]).then_inc(s_xr, 16)

            def key_ones(p):
                for h in range(HPG):
                    r0 = 64 * (h % 2) + MROW
                    sp.dma_start(kp[p][r0:r0 + 1, h, :].rearrange("o (i q) -> o i q", q=P).bitcast(f32),
                                 ones[0:KT, :]).then_inc(s_lv[p], 16)

            def load(u, p, half):
                b, g = u // NG, u % NG
                t0 = half * (N // 2)
                for r0 in (MROW, 64 + MROW):
                    sp.dma_start(qp[p][r0:r0 + 1, :, t0:t0 + N // 2].bitcast(f32),
                                 kp[p][MROW + 1:MROW + 2, 0:HPG - 1:2, t0:t0 + N // 2].bitcast(f32)).then_inc(s_ld[p][half], 16)
                for base, parts in ((0, (0, 0, 1)), (D, (0, 1, 0))):
                    for s in range(2):
                        for n, hl in enumerate(parts):
                            src = qk_s[hl, bass.ds(g * (HPG * HD) + base, HPG * HD), bass.ds(b * N + t0, N // 2)]
                            src = src.rearrange("(r s f) t -> s f r t", r=2, s=2)[s]
                            r0 = 64 * s + HD * n
                            if base == 0:
                                packed = qp[p][r0:r0 + HD, :, t0:t0 + N // 2]
                            else:
                                packed = kp[p][r0:r0 + HD, s:HPG:2, t0:t0 + N // 2]
                            sp.dma_start(packed.bitcast(f32), src).then_inc(s_ld[p][half], 16)

            def store(c, p, last):
                sp.wait_ge(s_qlo, c * 4 + 4)
                for h in range(2):
                    sp.dma_start(qk_s[h, :, bass.ds(c * CH, CH)].rearrange("(m p) t -> p m t", p=P),
                                 qst[p][h][:, :, :].bitcast(f32)).then_inc(s_qout[p], 16)
                sp.wait_ge(s_ve, c * 2 + 2)
                sp.dma_start(v_s[bass.ds(c * CH, CH), :].rearrange("(t p) n -> p t n", p=P),
                             vst[p][:, :, :, :].rearrange("p t h w -> p t (h w)")).then_inc(s_qout[p], 16)

            with sp.Fori(0, NCH // 4) as i:
                store(2 * i, 0, False)
                store(2 * i + 1, 1, False)
            for p in range(2):
                sp.wait_ge(s_qout[p], NCH // 4 * 48)
            if phases >= 2:
                sp.wait_ge(s_zero[0], 2)
                key_ones(0)
                for half in range(2):
                    load(0, 0, half)
            with sp.Fori(NCH // 4, NCH // 2) as i:
                store(2 * i, 0, False)
                store(2 * i + 1, 1, False)
            for p in range(2):
                sp.wait_ge(s_qout[p], NCH // 2 * 48)

            def load_values(u, p):
                b, g = u // NG, u % NG
                src = v_s[bass.ds(b * N, N), bass.ds(g * (HPG * 32), HPG * 32)]
                sp.dma_start(vt[p][:, :, :], src.rearrange("(j p) n -> p j n", p=P)).then_inc(s_lv[p], 16)

            def max_rows(u, p):
                sp.wait_ge(s_mts, u + 1)
                for h in range(HPG):
                    r0 = 64 * (h % 2) + MROW
                    sp.dma_start(qp[p][r0:r0 + 1, h // 2, :].rearrange("o (i q) -> o i q", q=P).bitcast(f32),
                                 mneg_t[KT * h:KT * (h + 1), :].bitcast(f32)).then_inc(s_m, 16)

            def sums_out(n):
                sp.wait_ge(s_oc, n + 1)
                for h in range(HPG):
                    sp.dma_start(dsum[32 * h:32 * h + 32, :], osb[32 * h + HD:32 * h + HD + 1, :].rearrange(
                        "o (s t) -> o s t", s=32)).then_inc(s_dg, 16)

            def sums_back(n):
                sp.wait_ge(s_rd, n + 1)
                if not isinstance(n, int) or n > 0:
                    sp.wait_ge(s_sh, n)
                for h in range(HPG):
                    sp.dma_start(rden[32 * h:32 * h + 1, :].rearrange("o (s t) -> o s t", s=32),
                                 dsum[32 * h:32 * h + 32, :]).then_inc(s_rg, 16)

            def unit_moves(u, p):
                more = not isinstance(u, int) or u < NU - 2
                for c in range(QCH - 1):
                    sums_out(u * QCH + c)
                    sums_back(u * QCH + c)
                if more:
                    sp.wait_ge(s_s2, u * (2 * NSTEP) + 2 * EARLY)
                    load(u + 2, p, 0)
                if not isinstance(u, int) or u < NU - 1:
                    max_rows(u + 1, 1 - p)
                sums_out(u * QCH + QCH - 1)
                if more:
                    load(u + 2, p, 1)
                sums_back(u * QCH + QCH - 1)
                if more:
                    load_values(u + 2, p)

            if phases >= 2:
                load_values(0, 0)
                sp.wait_ge(s_zero[1], 2)
                key_ones(1)
                for half in range(2):
                    load(1, 1, half)
                load_values(1, 1)
                max_rows(0, 0)
                unit_moves(0, 0)
                with sp.Fori(0, (NU - 4) // 2) as i:
                    unit_moves(2 * i + 1, 1)
                    unit_moves(2 * i + 2, 0)
                unit_moves(NU - 3, 1)
                unit_moves(NU - 2, 0)
                unit_moves(NU - 1, 1)

            if phases >= 3:
                sp.wait_ge(s_pv, NU * NSTEP)
                sp.wait_ge(s_xa, 2 * QCH * NU)
                for i in range(2):
                    sp.wait_ge(s_ws[i], 32 * (NPIECE // 2))
                sp.dma_start(b13[:, :, :], b13_in).then_inc(s_ffnc, 16)
                sp.dma_start(b2[:, :], b2_in).then_inc(s_ffnc, 16)
                sp.dma_start(gb[:, :, :], gb_in[None, None, :].to_broadcast([P, TPC, EXP])).then_inc(s_ffnc, 16)
                sp.dma_start(bd[:, :], bd_in[None, :].to_broadcast([P, DW])).then_inc(s_ffnc, 16)
                for h in range(2):
                    wv = w_s[NPIECE - 2, h].rearrange("p (k n) -> p k n", k=KC)
                    sp.dma_start(wd[h][:, :, 0:D].bitcast(f32), wv).then_inc(s_wd, 16)
                    wv = w_s[NPIECE - 1, h].rearrange("p (k n) -> p k n", k=KC)
                    sp.dma_start(wd[h][:, :, D:GW].bitcast(f32), wv[:, :, 0:GW - D]).then_inc(s_wd, 16)
                for e in range(NE):
                    for h in range(2):
                        for k in range(2):
                            sp.dma_start(w13[e][h][:, k, :, :].bitcast(f32),
                                         w_s[3 * e + k, h].rearrange("p (k n) -> p k n", k=KC)).then_inc(s_we[e], 16)
                        sp.dma_start(w2[e][h][:, :, :].bitcast(f32),
                                     w_s[3 * e + 2, h].rearrange("p (k n) -> p k n", k=KC)).then_inc(s_we[e], 16)

            def emit(c, p, last):
                if phases >= 5:
                    sp.wait_ge(F["E"]["acc"], c * (2 * NE) + 2 * NE + 2)
                sp.dma_start(o_v[bass.ds(c, 1)].rearrange("o p t d -> (o p) t d"), x[:, bass.ds(c * TPC, TPC), :]).then_inc(s_out, 16)

            if phases == 4:
                sp.wait_ge(s_dx, NCH + 1)
            if phases == 3:
                sp.wait_ge(F["C"]["acc"], NCH * 2 * NE + 2)
            if phases == 2:
                sp.wait_ge(s_xa, 2 * QCH * NU)
            pairs(sp, NCH, emit)
            sp.wait_ge(s_out, 16 * NCH)

        @block.gpsimd
        def _(pool):
            pool.memset(mhalf[:, :], -0.5).then_inc(s_const, 1)
            pool.memset(ones[:, :], 1.0).then_inc(s_const, 1)
            pool.memset(ident[:, :], 0.0).then_inc(s_const, 1)
            pool.memset(identb[:, :], 0.0).then_inc(s_const, 1)
            pool.memset(mask_qk[:, :], 0.0).then_inc(s_const, 1)
            pool.memset(mask_kq[:, :], 0.0).then_inc(s_const, 1)
            pool.wait_ge(s_const, 6)
            for m in (ident, identb):
                pool.affine_select(out=m[:, :], in_=m[:, :], compare_op=ALU.not_equal, fill=1.0,
                                   base=0, pattern=[[-1, P]], channel_multiplier=1).then_inc(s_const, 1)
            pool.affine_select(out=mask_qk[:, :], in_=mask_qk[:, :], compare_op=ALU.is_ge, fill=NEG,
                               base=0, pattern=[[-1, P]], channel_multiplier=1).then_inc(s_const, 1)
            pool.affine_select(out=mask_kq[:, :], in_=mask_kq[:, :], compare_op=ALU.is_ge, fill=NEG,
                               base=0, pattern=[[1, P]], channel_multiplier=-1).then_inc(s_const, 1)

            def inverse_std(n):
                pool.wait_ge(s_var, n + 1)
                pool.tensor_tensor(rstd[:, :], vare[:, :], mhalf[:, :], ALU.pow).then_inc(s_rstd, 1)

            inverse_std(0)
            pool.memset(kp[0][:, :, :].bitcast(f32), 0.0).then_inc(s_zero[0], 1)
            pool.wait_ge(s_sig, 4)
            pool.tensor_tensor(rn[:, :], nrm[:, :], mhalf[:, 0:2], ALU.pow).then_inc(s_sig, 1)
            pool.wait_ge(s_sig, 12)
            pool.tensor_tensor(rs[:, :], sg[:, :], mhalf[:, 0:2], ALU.pow).then_inc(s_sig, 1)
            with pool.Fori(1, NCH) as n:
                inverse_std(n)

            def raw(k, i):
                pool.dma_start(wraw[i][:, :].bitcast(f32), wffn_in[bass.ds(k, 1)].rearrange("o p n -> (o p) n")).then_inc(s_wr[i], 16)

            def finish(u, c, begin, end):
                n = u * QCH + c
                pool.wait_ge(s_sh, n + 1)
                pool.tensor_tensor(rdb[:, :], osb[:, :], rdb[:, :], ALU.mult).then_inc(s_am, 1)
                if not (begin and c == 0):
                    wait_apart(pool, s_pj, n * 2)
                wait_apart(pool, s_am, n + 1)
                pool.tensor_copy(ah[:, :], rdb[:, :]).then_inc(s_ah, 1)
                pool.wait_ge(s_ah, n + 1)
                pool.tensor_tensor(al[:, :], rdb[:, :], ah[:, :].bitcast(f32), ALU.subtract).then_inc(s_al, 1)
                i = c % 2
                turn = u * (QCH // 2) + c // 2
                wait_apart(pool, s_wr[i], turn * 16 + 16)
                pool.tensor_copy(whi[i][:, :], wraw[i][:, :].bitcast(f32)).then_inc(s_wh, 1)
                pool.wait_ge(s_wh, n + 1)
                pool.tensor_tensor(wraw[i][:, :], wraw[i][:, :].bitcast(f32), whi[i][:, :].bitcast(f32),
                                   ALU.subtract).then_inc(s_wl, 1)
                pool.wait_ge(s_wl, n + 1)
                pool.dma_start(w_s[bass.ds(n, 1), 0].rearrange("o p n -> (o p) n"), whi[i][:, :].bitcast(f32)).then_inc(s_ws[i], 16)
                pool.dma_start(w_s[bass.ds(n, 1), 1].rearrange("o p n -> (o p) n"), wraw[i][:, :].bitcast(f32)).then_inc(s_ws[i], 16)
                if not (end and c == QCH - 1):
                    if not (begin and c == 0):
                        pool.wait_ge(s_ws[1 - i], turn * 32 + (32 if i == 1 else 0))
                    raw(n + 1, 1 - i)

            def finish_unit(u, begin, end):
                for c in range(QCH):
                    finish(u, c, begin, end)

            if phases >= 2:
                for p in range(2):
                    pool.wait_ge(s_qout[p], NCH // 2 * 48)
                pool.memset(kp[1][:, :, :].bitcast(f32), 0.0).then_inc(s_zero[1], 1)
                raw(0, 0)
                finish_unit(0, True, False)
                with pool.Fori(1, NU - 1) as u:
                    finish_unit(u, False, False)
                finish_unit(NU - 1, False, True)

            if phases >= 3:
                with pool.Fori(NCH, NPREP[phases]) as n:
                    inverse_std(n)

        @block.scalar
        def _(act):
            def split_high(n, p):
                for k in range(KC):
                    act.wait_ge(s_tr, n * KC + k + 1)
                    act.activation(xt[p][0][:, k, :], tr[k][:, :], ACT.Copy).then_inc(s_xhi, 1)

            def evacuate(c, p, last):
                if not last:
                    split_high(c + 1, 1 - p)
                if not isinstance(c, int) or c >= 2:
                    act.wait_ge(s_qout[p], c // 2 * 48)
                for m in range(4):
                    act.wait_ge(s_qk, c * 4 + m + 1)
                    act.activation(qst[p][0][:, m, :], pqk[m][:, :], ACT.Copy).then_inc(s_qhi, 1)
                for k in range(2):
                    act.wait_ge(s_vp, c * 2 + k + 1)
                    act.activation(vst[p][:, 2 * k:2 * k + 2, :, 0:HD], pv_[k][:, :, :, :],
                                   ACT.Copy).then_inc(s_ve, 1)

            split_high(0, 0)
            act.wait_ge(s_dconst, 1)
            evacuate(0, 0, False)
            evacuate(1, 1, False)
            with act.Fori(1, NCH // 2 - 1) as i:
                evacuate(2 * i, 0, False)
                evacuate(2 * i + 1, 1, False)
            evacuate(NCH - 2, 0, False)
            evacuate(NCH - 1, 1, True)

            def transposed_max(u, begin):
                if not begin:
                    act.wait_ge(s_m, u * 64)
                act.wait_ge(s_mt, u + 1)
                act.activation(mneg_t[:, :], pp[0:HPG * KT, 0, 0:P], ACT.Copy).then_inc(s_mts, 1)

            def exps(u, p, begin, end):
                for k, (c, j) in enumerate(STEPS):
                    w0 = max(0, j - TPC * c) * P
                    if not (begin and k < PRING):
                        act.wait_ge(s_pv, u * NSTEP + (k - PRING + 1))
                    for r in range(2):
                        act.wait_ge(s_s2, u * (2 * NSTEP) + (2 * k + r + 1))
                        act.activation(pr[k % PRING][:, 2 * r:2 * r + 2, w0:CH], ps2[r][:, :, w0:CH],
                                       ACT.Exp, scale=HD ** -0.5).then_inc(s_ex2, 1)
                    if k == MAX_BY and not end:
                        transposed_max(u + 1, False)

            if phases >= 2:
                for p in range(2):
                    act.wait_ge(s_qout[p], NCH // 2 * 48)
                transposed_max(0, True)
                units(act, exps)

            def gate_exp(g):
                act.wait_ge(s_lgd, g + 1)
                act.activation(sc[:, :, :], lg[:, :, :], ACT.Exp).then_inc(s_ex, 1)

            def gate_out(g):
                act.wait_ge(s_gt, g + 1)
                act.activation(gate_t[:, :], tr[1][0:EXP + 1, :], ACT.Copy).then_inc(s_gts, 1)

            def experts(S, n0, g0, q0):
                def body(c, p, last):
                    for e in range(NE):
                        for k in range(KC):
                            v = KC * e + k
                            act.wait_ge(S["up_a"], c * (2 * NE) + (v + 1))
                            act.wait_ge(S["h"], c * (2 * NE) + (v + 1))
                            act.activation(sil[k][:, :], pup[k][0][:, :], ACT.Silu,
                                           bias=b13[:, 0, v:v + 1]).then_inc(S["silu"], 1)
                            act.wait_ge(S["h"], c * (2 * NE) + (v + 3))
                            act.wait_ge(S["y"], c * (2 * NE) + (2 * e + 2))
                            act.activation(hh[e % 2][0][:, k, :], hf[k][:, :], ACT.Copy).then_inc(S["h_hi"], 1)
                        if e == 2:
                            gate_out(c + q0)
                        if not last:
                            if e == 4:
                                split_high(c + (n0 + 1), 1 - p)
                            if e == 6:
                                gate_exp(c + (g0 + 1))
                return body

            def softplus(c, p, last):
                act.wait_ge(s_dz, c + 2)
                act.wait_ge(s_dr, c * 4 + 6)
                act.activation(e1[:, :, :], zt[:, :, 0:D], ACT.Abs).then_inc(s_dab, 1)
                act.wait_ge(s_dab, c + 1)
                act.activation(e1[:, :, :], e1[:, :, :], ACT.Exp, scale=-1.0).then_inc(s_de, 1)
                act.wait_ge(s_de, c + 1)
                act.wait_ge(s_dx, c + 1)
                act.activation(l1[:, :, :], e1[:, :, :], ACT.Ln, bias=ones[:, 0:1]).then_inc(s_dl, 1)
                if not last:
                    split_high(c + (2 * NCH + 1), 1 - p)

            if phases >= 3:
                act.wait_ge(s_ffnc, 64)
                split_high(NCH, 0)
                gate_exp(0)
                pairs(act, NCH, experts(F["C"], NCH, 0, 0), peel_last=phases == 3)
            if phases >= 4:
                pairs(act, NCH, softplus, peel_last=phases == 4)
            if phases >= 5:
                gate_exp(NCH + 1)
                pairs(act, NCH, experts(F["E"], 3 * NCH, NCH + 1, NCH), peel_last=True)

        @block.tensor
        def _(pe):
            def three(out_ap, lh, ll, rh, rl, start, stop):
                pe.matmul(out_ap, lh, rh, start=start, stop=False)
                pe.matmul(out_ap, lh, rl, start=False, stop=False)
                return pe.matmul(out_ap, ll, rh, start=False, stop=stop)

            def transposes(n, begin=False, g=None, q=None, src=xn):
                pe.wait_ge(s_xn, n + 1)
                if not begin:
                    pe.wait_ge(s_xlo, n * KC)
                if g is not None:
                    pe.wait_ge(s_lgd, g)
                    pe.wait_ge(s_gts, q)
                for k in range(KC):
                    for t in range(TPC):
                        mm = pe.transpose(tr[k][:, t * P:(t + 1) * P], src[:, t, k * P:(k + 1) * P], ident[:, :])
                    mm.then_inc(s_tr, 1)

            def logits(n, p):
                pe.wait_ge(s_xlo, n * KC + KC)
                for t in range(TPC):
                    ts = slice(t * P, (t + 1) * P)
                    for k in range(KC):
                        mm = three(tr[0][:, t * EXP:(t + 1) * EXP], xt[p][0][:, k, ts], xt[p][1][:, k, ts],
                                   wd[0][:, k, DW:GW], wd[1][:, k, DW:GW], k == 0, k == KC - 1)
                mm.then_inc(s_lg, 1)

            def gates_t(g, n):
                pe.wait_ge(s_gate, g + 1)
                pe.wait_ge(s_xlo, n * KC + KC)
                for t in range(TPC):
                    mm = pe.transpose(tr[1][0:EXP + 1, t * P:(t + 1) * P], gate[:, t, 0:EXP + 1], ident[:, :])
                mm.then_inc(s_gt, 1)

            pe.wait_ge(s_const, 10)
            transposes(0, begin=True)
            pe.wait_ge(s_xlo, KC)
            pe.wait_ge(s_sig, 2)
            for n, (k0, k1) in enumerate(((0, KC), (KC, KC + NG))):
                for k in range(k0, k1):
                    mm = pe.matmul(tr[0][:, n:n + 1], ones[:, :], vsq[:, k:k + 1], start=(k == k0), stop=(k == k1 - 1))
            mm.then_inc(s_sig, 1)
            pe.wait_ge(s_sig, 6)
            for m in range(3 * KC):
                for k in range(KC):
                    pe.matmul(tr[1][:, m:m + 1], wq_raw[:, k, m * P:(m + 1) * P], vn[:, k:k + 1],
                              start=(k == 0), stop=(k == KC - 1))
            for m in range(KC):
                for k in range(NG):
                    mm = pe.matmul(tr[1][:, 3 * KC + m:3 * KC + m + 1], wp_raw[:, k, m * P:(m + 1) * P],
                                   vn[:, KC + k:KC + k + 1], start=(k == 0), stop=(k == NG - 1))
            mm.then_inc(s_sig, 1)
            pe.wait_ge(s_sig, 10)
            pe.matmul(tr[0][:, 8:10], ones[:, :], u2s[:, 0:2], start=True, stop=True).then_inc(s_sig, 1)
            pe.wait_ge(s_sig, 20)

            def project(c, p, last):
                if not last:
                    transposes(c + 1)
                pe.wait_ge(s_xlo, c * KC + KC)
                for m in range(4):
                    if not isinstance(c, int) or c > 0:
                        pe.wait_ge(s_qlo, c * 4 + (m - 3))
                    ms = slice(m * P, (m + 1) * P)
                    for k in range(KC):
                        mm = three(pqk[m][:, :], wq_hl[0][:, k, ms], wq_hl[1][:, k, ms],
                                   xt[p][0][:, k, :], xt[p][1][:, k, :], k == 0, k == KC - 1)
                    mm.then_inc(s_qk, 1)
                for t in range(TPC):
                    if t % 2 == 0 and (not isinstance(c, int) or c > 0):
                        pe.wait_ge(s_ve, c * 2 + (t // 2 - 1))
                    ts = slice(t * P, (t + 1) * P)
                    for k in range(KC):
                        mm = three(pv_[t // 2][:, t % 2, :, :].rearrange("p h w -> p (h w)"),
                                   xt[p][0][:, k, ts], xt[p][1][:, k, ts],
                                   wq_hl[0][:, k, 2 * D:3 * D], wq_hl[1][:, k, 2 * D:3 * D],
                                   k == 0, k == KC - 1)
                    if t % 2 == 1:
                        mm.then_inc(s_vp, 1)

            project(0, 0, False)
            project(1, 1, False)
            with pe.Fori(1, NCH // 2 - 1) as i:
                project(2 * i, 0, False)
                project(2 * i + 1, 1, False)
            project(NCH - 2, 0, False)
            project(NCH - 1, 1, True)

            def max_scores(u, p, bank, begin, banks):
                i, cc, w, hb, n = BANKS[bank]
                if not (begin and bank < len(banks)):
                    pe.wait_ge(s_mx, u * NBANK + (bank - len(banks) + 1))
                diag = cc == i // TPC
                for q in range(hb):
                    h = n * hb + q
                    o = banks[bank % len(banks)][:, q * w:(q + 1) * w]
                    mm = pe.matmul(o, qp[p][0:ROWS, h // 2, i * P:(i + 1) * P], kp[p][0:ROWS, h, cc * CH:cc * CH + w],
                                   start=True, stop=not diag)
                    if diag:
                        mm = pe.matmul(o[:, w - P:w], identb[:, :], mask_qk[:, :], start=False, stop=True)
                mm.then_inc(s_s1, 1)

            def transpose_max(u, wait_free):
                if wait_free is not None:
                    wait_apart(pe, s_xa, wait_free)
                wait_apart(pe, s_pm, u + 1)
                pe.transpose(pp[0:HPG * KT, 0, 0:P], mneg[:, :], ident[:, :]).then_inc(s_mt, 1)

            def scores(u, p, k, r, begin):
                c, j = STEPS[k]
                w0 = max(0, j - TPC * c) * P
                if not (begin and k == 0):
                    pe.wait_ge(s_ex2, u * (2 * NSTEP) + (2 * k + r - 1))
                for s in range(2):
                    h = 2 * r + s
                    mm = pe.matmul(ps2[r][:, s, w0:CH], kp[p][0:ROWS, h, j * P:(j + 1) * P],
                                   qp[p][0:ROWS, h // 2, c * CH + w0:(c + 1) * CH], start=True, stop=j < TPC * c)
                if j >= TPC * c:
                    for s in range(2):
                        mm = pe.matmul(ps2[r][:, s, w0:w0 + P], identb[:, :], mask_kq[:, :], start=False, stop=True)
                mm.then_inc(s_s2, 1)

            def values(u, p, k, begin):
                c, j = STEPS[k]
                w0 = max(0, j - TPC * c) * P
                pe.wait_ge(s_ex2, u * (2 * NSTEP) + (2 * k + 2))
                if j == 0 and not (begin and c == 0):
                    pe.wait_ge(s_oc, u * QCH + c)
                for h in range(HPG):
                    mm = pe.matmul(po[32 * h:32 * h + 32, w0:CH], vt[p][:, j, 32 * h:32 * h + 32],
                                   pr[k % PRING][:, h, w0:CH], start=(j == 0), stop=(j == TPC * c + TPC - 1))
                mm.then_inc(s_pv, 1)

            def project_out(n, g, half, begin, after_max):
                if half == 0:
                    pe.wait_ge(s_al, n + 1)
                if not (begin and half == 0):
                    pe.wait_ge(s_xa, n * 2 + half)
                if after_max is not None:
                    pe.wait_ge(s_mts, after_max)
                for t in range(2):
                    ts = slice((2 * half + t) * P, (2 * half + t + 1) * P)
                    mm = three(pp[:, t, :], ah[:, ts], al[:, ts],
                               wph[:, bass.ds(g, 1), :].rearrange("p g n -> p (g n)"),
                               wpl[:, bass.ds(g, 1), :].rearrange("p g n -> p (g n)"), True, True)
                mm.then_inc(s_pj, 1)

            def unit(u, p, begin, end):
                turn = u // 2
                pe.wait_ge(s_lv[p], turn * 16 + (HPG + 1) * 16)
                pe.wait_ge(s_m, u * 64 + 64)
                def next_max(banks):
                    for bank in banks:
                        if bank == 0:
                            pe.wait_ge(s_ld[1 - p][0], (u + 1) // 2 * HALF_LD + HALF_LD)
                        if BANKS[bank][0] == KT // 2 and BANKS[bank][1] == 0 and BANKS[bank][4] == 0:
                            pe.wait_ge(s_ld[1 - p][1], (u + 1) // 2 * HALF_LD + HALF_LD)
                        max_scores(u + 1, 1 - p, bank, False, ps1)

                for k in range(NSTEP + LAG):
                    banks = max_slot(k) if not end and k < NSTEP else []
                    if k < NSTEP:
                        scores(u, p, k, 0, begin)
                        next_max(banks[0:1])
                        scores(u, p, k, 1, begin)
                        next_max(banks[1:3])
                    if k >= LAG:
                        values(u, p, k - LAG, begin)
                    next_max(banks[3:])
                    if k in (PROJ[3][0], PROJ[3][1]) and not begin:
                        n = u * QCH - 1
                        project_out(n, (u - 1) % NG, PROJ[3].index(k), False, u + 1 if k == PROJ[3][0] else None)
                    for c in range(QCH - 1):
                        if k in PROJ[c]:
                            project_out(u * QCH + c, u % NG, PROJ[c].index(k), begin and c == 0,
                                        u + 1 if begin and c == 0 else None)
                    if k == MAX_BY and not end:
                        transpose_max(u + 1, (u * QCH + QCH - 1) * 2)

            if phases >= 2:
                pe.wait_ge(s_ld[0][0], HALF_LD)
                pe.wait_ge(s_ld[0][1], HALF_LD)
                pe.wait_ge(s_qlo, NCH * 4)
                pe.wait_ge(s_ve, NCH * 2)
                for bank in range(NBANK):
                    max_scores(0, 0, bank, True, every)
                transpose_max(0, None)
                units(pe, unit)
                for half in range(2):
                    project_out(NU * QCH - 1, NG - 1, half, False, None)

            def experts(S, n0, g0, q0, weights):
                def up(c, p, e, k):
                    v = KC * e + k
                    if weights and k == 0:
                        pe.wait_ge(s_we[e], 96)
                    pe.wait_ge(S["h"], c * (2 * NE) + (v + 1))
                    ks = slice(k * P, (k + 1) * P)
                    for q, done in enumerate(("up_a", "up_b")):
                        for kk in range(KC):
                            mm = three(pup[k][q][:, :], w13[e][0][:, q, kk, ks], w13[e][1][:, q, kk, ks],
                                       xt[p][0][:, kk, :], xt[p][1][:, kk, :], kk == 0, kk == KC - 1)
                        mm.then_inc(S[done], 1)

                def down(c, e):
                    pe.wait_ge(S["h_lo"], c * (2 * NE) + (2 * e + 2))
                    for half in range(2):
                        pe.wait_ge(S["acc"], c * (2 * NE) + (2 * e + half + 1))
                        for t in range(2):
                            ts = slice((2 * half + t) * P, (2 * half + t + 1) * P)
                            if e == EXP:
                                if t == 0 and half == 0:
                                    pe.wait_ge(s_gts, c + (q0 + 1))
                                pe.matmul(py[half][:, t, :], gate_t[:, ts], b2[:, :], start=True, stop=False)
                            for kk in range(KC):
                                mm = three(py[half][:, t, :], hh[e % 2][0][:, kk, ts], hh[e % 2][1][:, kk, ts],
                                           w2[e][0][:, kk, :], w2[e][1][:, kk, :],
                                           kk == 0 and e != EXP, kk == KC - 1)
                        mm.then_inc(S["y"], 1)

                def body(c, p, last):
                    for e in range(NE):
                        up(c, p, e, 0)
                        up(c, p, e, 1)
                        if e > 0:
                            down(c, e - 1)
                        elif not isinstance(c, int) or c > 0:
                            down(c - 1, NE - 1)
                        if e == 2:
                            gates_t(c + g0, c + n0)
                        if not last:
                            if e == 3:
                                transposes(c + (n0 + 1), g=c + (g0 + 1), q=c + (q0 + 1))
                            if e == 5:
                                logits(c + (n0 + 1), 1 - p)
                    if isinstance(c, int) and c == NCH - 1:
                        down(c, NE - 1)
                return body

            def gate_stage(c, p, last):
                pe.wait_ge(s_xlo, (c + 2 * NCH) * KC + KC)
                pe.wait_ge(s_dz, c + 1)
                for t in range(TPC):
                    ts = slice(t * P, (t + 1) * P)
                    for k in range(KC):
                        mm = three(pd[t][:, 0:DW], xt[p][0][:, k, ts], xt[p][1][:, k, ts],
                                   wd[0][:, k, 0:DW], wd[1][:, k, 0:DW], k == 0, k == KC - 1)
                    mm.then_inc(s_dp, 1)
                if not last:
                    transposes(c + (2 * NCH + 1), g=NCH + 1, q=NCH, src=(xn, xn_b)[1 - p])

            if phases >= 3:
                pe.wait_ge(s_wd, 64)
                pe.wait_ge(s_xa, 2 * QCH * NU)
                transposes(NCH)
                logits(NCH, 0)
                chunks(pe, experts(F["C"], NCH, 0, 0, True), phases == 3)
            if phases >= 4:
                pe.wait_ge(F["C"]["acc"], NCH * 2 * NE + 2)
                pairs(pe, NCH, gate_stage, peel_last=phases == 4)
            if phases >= 5:
                pe.wait_ge(s_dx, NCH + 1)
                logits(3 * NCH, 0)
                chunks(pe, experts(F["E"], 3 * NCH, NCH + 1, NCH, False), True)

        @block.vector
        def _(dve):
            def statistics(n, t0):
                for t in range(TPC):
                    i = dve.bn_stats(stats[:, t, :], x[:, bass.ds(t0 + t, 1), :].rearrange("p o d -> p (o d)"))
                i.then_inc(s_stats, 1)
                wait_apart(dve, s_stats, n + 1)
                for t in range(TPC):
                    i = dve.bn_aggr(mv[:, t, :], stats[:, t, :])
                i.then_inc(s_aggr, 1)
                dve.wait_ge(s_aggr, n + 1)
                dve.tensor_scalar(vare[:, :], mv[:, :, 1], EPS, None, ALU.add).then_inc(s_var, 1)

            def normalise(n, t0, dst=xn):
                dve.wait_ge(s_rstd, n + 1)
                if not isinstance(n, int) or n > 0:
                    dve.wait_ge(s_tr, n * KC)
                for t in range(TPC):
                    i = dve.tensor_scalar(dst[:, t, :], x[:, bass.ds(t0 + t, 1), :].rearrange("p o d -> p (o d)"),
                                          mv[:, t, 0:1], rstd[:, t:t + 1], ALU.subtract, ALU.mult)
                i.then_inc(s_xn, 1)

            def split_low(n, p):
                for k in range(KC):
                    dve.wait_ge(s_xhi, n * KC + k + 1)
                    dve.tensor_tensor(xt[p][1][:, k, :], tr[k][:, :], xt[p][0][:, k, :].bitcast(f32),
                                      ALU.subtract).then_inc(s_xlo, 1)

            ROUTE = 17

            def over(col):
                return col[:, :].unsqueeze(2).to_broadcast([P, TPC, EXP])

            def route_logits(g):
                dve.wait_ge(s_lg, g + 1)
                dve.tensor_tensor(lg[:, :, :], tr[0][:, 0:TPC * EXP].rearrange("p (t e) -> p t e", e=EXP),
                                  gb[:, :, :], ALU.add).then_inc(s_rt, 1)
                dve.wait_ge(s_rt, g * ROUTE + 1)
                dve.tensor_reduce(mx[:, :], lg[:, :, :], AX.X, ALU.max).then_inc(s_rt, 1)
                dve.wait_ge(s_rt, g * ROUTE + 2)
                dve.tensor_tensor(lg[:, :, :], lg[:, :, :], over(mx), ALU.subtract).then_inc(s_lgd, 1)

            def route(g):
                at = [2]

                def step(ins):
                    at[0] += 1
                    ins.then_inc(s_rt, 1)
                    dve.wait_ge(s_rt, g * ROUTE + at[0])

                dve.wait_ge(s_ex, g + 1)
                step(dve.tensor_reduce(mx[:, :], sc[:, :, :], AX.X, ALU.add))
                step(dve.reciprocal(mx[:, :], mx[:, :]))
                step(dve.tensor_tensor(sc[:, :, :], sc[:, :, :], over(mx), ALU.mult))
                for src, hot in ((sc, oh), (lg, eq)):
                    step(dve.tensor_reduce(mx[:, :], src[:, :, :], AX.X, ALU.max))
                    step(dve.tensor_tensor(eq[:, :, :], src[:, :, :], over(mx), ALU.is_equal))
                    step(dve.tensor_tensor(eq[:, :, :], eq[:, :, :], rev[:, :, :], ALU.mult))
                    step(dve.tensor_reduce(mx[:, :], eq[:, :, :], AX.X, ALU.max))
                    step(dve.tensor_tensor(hot[:, :, :], eq[:, :, :], over(mx), ALU.is_equal))
                    if hot is oh:
                        step(dve.scalar_tensor_tensor(lg[:, :, :], oh[:, :, :], -2.0, sc[:, :, :], ALU.mult, ALU.add))
                step(dve.tensor_tensor(eq[:, :, :], eq[:, :, :], oh[:, :, :], ALU.add))
                assert at[0] == ROUTE, at[0]
                dve.tensor_tensor(gate[:, :, 0:EXP], sc[:, :, :], eq[:, :, :], ALU.mult).then_inc(s_gate, 1)

            for ph in "CE":
                dve.sem_inc(F[ph]["h"], 2)
                dve.sem_inc(F[ph]["acc"], 2)
                dve.sem_inc(F[ph]["y"], 4)
            dve.sem_inc(s_dr, 8)
            dve.sem_inc(s_dx, 1)
            dve.sem_inc(s_dz, 1)
            dve.memset(wp_raw[:, :, :], 0.0)
            for p in range(2):
                i = dve.memset(vst[p][:, :, :, :], 1.0)
            i.then_inc(s_dconst, 1)
            dve.memset(qp[0][:, :, :].bitcast(f32), 0.0).then_inc(s_zero[0], 1)
            for p in range(2):
                i = dve.memset(part[p][:, :, :, :], 3e38)
            i.then_inc(s_dconst, 1)

            dve.wait_ge(s_x0, 16)
            statistics(0, 0)
            normalise(0, 0)
            split_low(0, 0)
            dve.wait_ge(s_w, 9 * 16)
            for k in range(KC):
                dve.tensor_tensor_reduce(out=prod[:, k * 3 * D:(k + 1) * 3 * D], in0=wq_raw[:, k, :], in1=ub[:, 0:3 * D], scale=1.0, scalar=0.0,
                                         op0=ALU.mult, op1=ALU.add, accum_out=vr[:, k:k + 1])
            for k in range(NG):
                i = dve.tensor_tensor_reduce(out=prod[:, KC * 3 * D + k * D:KC * 3 * D + (k + 1) * D], in0=wp_raw[:, k, :], in1=ub[:, 3 * D:4 * D], scale=1.0,
                                             scalar=0.0, op0=ALU.mult, op1=ALU.add, accum_out=vr[:, KC + k:KC + k + 1])
            i.then_inc(s_sig, 1)
            dve.wait_ge(s_sig, 1)
            dve.tensor_tensor(vsq[:, :], vr[:, :], vr[:, :], ALU.mult).then_inc(s_sig, 1)
            dve.wait_ge(s_sig, 3)
            dve.tensor_copy(nrm[:, :], tr[0][:, 0:2]).then_inc(s_sig, 1)
            dve.wait_ge(s_sig, 5)
            dve.tensor_scalar(vn[:, 0:KC], vr[:, 0:KC], rn[:, 0:1], None, ALU.mult)
            dve.tensor_scalar(vn[:, KC:KC + NG], vr[:, KC:KC + NG], rn[:, 1:2], None, ALU.mult).then_inc(s_sig, 1)
            dve.wait_ge(s_sig, 7)
            dve.tensor_copy(u2[:, :], tr[1][:, 0:8]).then_inc(s_sig, 1)
            dve.wait_ge(s_sig, 8)
            dve.tensor_tensor(u2q[:, :], u2[:, :], u2[:, :], ALU.mult).then_inc(s_sig, 1)
            dve.wait_ge(s_sig, 9)
            dve.tensor_reduce(u2s[:, 0:1], u2q[:, 0:3 * KC], AX.X, ALU.add)
            dve.tensor_reduce(u2s[:, 1:2], u2q[:, 3 * KC:4 * KC], AX.X, ALU.add).then_inc(s_sig, 1)
            dve.wait_ge(s_sig, 11)
            dve.tensor_copy(sg[:, :], tr[0][:, 8:10]).then_inc(s_sig, 1)
            dve.wait_ge(s_sig, 13)
            dve.tensor_tensor(scl[:, :], rs[:, :], sp_in[:, :], ALU.mult).then_inc(s_sig, 1)
            dve.wait_ge(s_sig, 14)
            dve.tensor_scalar(wq_raw[:, :, :], wq_raw[:, :, :], scl[:, 0:1], None, ALU.mult).then_inc(s_sig, 1)
            dve.tensor_scalar(wp_raw[:, :, :], wp_raw[:, :, :], scl[:, 1:2], None, ALU.mult).then_inc(s_sig, 1)
            dve.wait_ge(s_sig, 16)
            dve.tensor_copy(wq_hl[0][:, :, :], wq_raw[:, :, :]).then_inc(s_sig, 1)
            dve.tensor_copy(wph[:, :, :], wp_raw[:, :, :]).then_inc(s_sig, 1)
            dve.wait_ge(s_sig, 18)
            dve.tensor_tensor(wq_hl[1][:, :, :], wq_raw[:, :, :], wq_hl[0][:, :, :].bitcast(f32),
                              ALU.subtract).then_inc(s_sig, 1)
            dve.tensor_tensor(wpl[:, :, :], wp_raw[:, :, :], wph[:, :, :].bitcast(f32), ALU.subtract).then_inc(s_sig, 1)

            dve.wait_ge(s_xr, (NCH - 1) * 16)

            def low_parts(c, p, last):
                if not last:
                    statistics(c + 1, (c + 1) * TPC)
                    normalise(c + 1, (c + 1) * TPC)
                    split_low(c + 1, 1 - p)
                for m in range(4):
                    dve.wait_ge(s_qhi, c * 4 + m + 1)
                    dve.tensor_tensor(qst[p][1][:, m, :], pqk[m][:, :], qst[p][0][:, m, :].bitcast(f32),
                                      ALU.subtract).then_inc(s_qlo, 1)

            pairs(dve, NCH, low_parts, peel_last=True)

            def take_max(u, p, bank, banks):
                i, cc, w, hb, n = BANKS[bank]
                dve.wait_ge(s_s1, u * NBANK + (bank + 1))
                dve.tensor_reduce(part[p][:, n * hb:(n + 1) * hb, i, cc], banks[bank % len(banks)][:, 0:hb * w].rearrange("p (h w) -> p h w", w=w),
                                  AX.X, ALU.max, negate=True).then_inc(s_mx, 1)

            def join_max(u, p, begin):
                if not begin:
                    dve.wait_ge(s_mt, u)
                dve.wait_ge(s_mx, u * NBANK + NBANK)
                dve.tensor_reduce(mneg[:, :], part[p][:, :, :, :].rearrange("p h i c -> p (h i) c"),
                                  AX.X, ALU.min).then_inc(s_pm, 1)

            def take_outputs(n, done, begin):
                dve.wait_ge(s_pv, done)
                if not begin:
                    dve.wait_ge(s_am, n)
                dve.tensor_copy(osb[:, :], po[:, :]).then_inc(s_oc, 1)

            def reciprocals(n):
                dve.wait_ge(s_dg, n * (HPG * 16) + HPG * 16)
                dve.reciprocal(dsum[:, :], dsum[:, :]).then_inc(s_rd, 1)

            def spread(n, begin):
                if not begin:
                    wait_apart(dve, s_al, n)
                wait_apart(dve, s_rg, n * (HPG * 16) + HPG * 16)
                dve.stream_shuffle(rdb[:, :], rden[:, :], [0] * 32).then_inc(s_sh, 1)

            def add_out(n, t0, half):
                dve.wait_ge(s_pj, n * 2 + (half + 1))
                xs = x[:, bass.ds(t0 + 2 * half, 2), :]
                dve.tensor_tensor(xs, xs, pp[:, :, :], ALU.add).then_inc(s_xa, 1)

            def unit(u, p, begin, end):
                for k in range(NSTEP + LAG):
                    if not end and k < NSTEP:
                        for bank in max_slot(k):
                            take_max(u + 1, 1 - p, bank, ps1)
                    if k == MAX_BY - 1 and not end:
                        join_max(u + 1, 1 - p, False)
                    if k in PROJ[3] and not begin:
                        n, v = u * QCH - 1, u - 1
                        add_out(n, v // NG * KT + (QCH - 1) * TPC, PROJ[3].index(k))
                    for c in range(QCH - 1):
                        if k in PROJ[c]:
                            add_out(u * QCH + c, u // NG * KT + c * TPC, PROJ[c].index(k))
                    for c in range(QCH):
                        at = TPC * (c + 1) * (c + 2) // 2 - 1 + LAG
                        n = u * QCH + c
                        if k == at:
                            take_outputs(n, u * NSTEP + (at - LAG + 1), begin and c == 0)
                        if k == at + RECIP:
                            reciprocals(n)
                        if k == at + SPREAD:
                            spread(n, begin and c == 0)
                    if k == RECIP - 1 and not begin:
                        reciprocals(u * QCH - 1)
                    if k == SPREAD - 1 and not begin:
                        spread(u * QCH - 1, False)

            if phases >= 2:
                dve.wait_ge(s_dconst, 2)
                for bank in range(NBANK):
                    if bank == NBANK // 4:
                        for p in range(2):
                            dve.wait_ge(s_qout[p], NCH // 2 * 48)
                        dve.memset(qp[1][:, :, :].bitcast(f32), 0.0).then_inc(s_zero[1], 1)
                        dve.memset(rden[:, :], 1.0).then_inc(s_dconst, 1)
                    take_max(0, 0, bank, every)
                join_max(0, 0, True)
                dve.wait_ge(s_dconst, 3)
                units(dve, unit)
                reciprocals(NU * QCH - 1)
                spread(NU * QCH - 1, False)
                for half in range(2):
                    add_out(NU * QCH - 1, (NU - 1) // NG * KT + (QCH - 1) * TPC, half)

            def experts(S, n0, g0):
                def body(c, p, last):
                    nt = (c + 1) % NCH * TPC
                    n, g = c + (n0 + 1), c + (g0 + 1)

                    def add_expert(c, e):
                        for half in range(2):
                            dve.wait_ge(S["y"], c * (2 * NE) + (2 * e + half + 5))
                            for t in range(2):
                                tile = 2 * half + t
                                xs = x[:, bass.ds(c * TPC + tile, 1), :].rearrange("p o d -> p (o d)")
                                i = dve.scalar_tensor_tensor(xs, py[half][:, t, :], gate[:, tile, e:e + 1], xs,
                                                             ALU.mult, ALU.add)
                            i.then_inc(S["acc"], 1)

                    for e in range(NE):
                        for k in range(KC):
                            v = KC * e + k
                            dve.wait_ge(S["silu"], c * (2 * NE) + (v + 1))
                            dve.wait_ge(S["up_b"], c * (2 * NE) + (v + 1))
                            dve.scalar_tensor_tensor(hf[k][:, :], pup[k][1][:, :], b13[:, 1, v:v + 1], sil[k][:, :],
                                                     ALU.add, ALU.mult).then_inc(S["h"], 1)
                            dve.wait_ge(S["h_hi"], c * (2 * NE) + (v + 1))
                            dve.tensor_tensor(hh[e % 2][1][:, k, :], hf[k][:, :], hh[e % 2][0][:, k, :].bitcast(f32),
                                              ALU.subtract).then_inc(S["h_lo"], 1)
                        if e > 0:
                            add_expert(c, e - 1)
                        elif not isinstance(c, int) or c > 0:
                            add_expert(c - 1, NE - 1)
                        if not last:
                            if e == 1:
                                statistics(n, nt)
                            if e == 2:
                                normalise(n, nt)
                            if e == 4:
                                split_low(n, 1 - p)
                            if e == 6:
                                route_logits(g)
                    if isinstance(c, int) and c == NCH - 1:
                        add_expert(c, NE - 1)
                    if not last:
                        route(g)
                return body

            def gate_stage(c, p, last):
                nt, n = (c + 1) % NCH * TPC, c + (2 * NCH + 1)
                if not last:
                    statistics(n, nt)
                for t in range(TPC):
                    dve.wait_ge(s_dp, c * TPC + (t + 1))
                    i = dve.tensor_tensor(zt[:, t, :], pd[t][:, 0:DW], bd[:, :], ALU.add)
                i.then_inc(s_dz, 1)
                dve.wait_ge(s_dz, c + 2)
                dve.tensor_tensor(bcp[:, :, :], zt[:, :, D:D + NST], zt[:, :, D + NST:DW], ALU.mult).then_inc(s_dbc, 1)
                dve.wait_ge(s_dbc, c * 2 + 1)
                dve.tensor_reduce(bcs[:, :], bcp[:, :, :], AX.X, ALU.add).then_inc(s_dbc, 1)
                if not last:
                    normalise(n, nt, (xn, xn_b)[1 - p])
                dve.wait_ge(s_de, c + 1)
                dve.tensor_scalar(u1[:, :, :], e1[:, :, :], 1.0, 1.0, ALU.add, ALU.subtract).then_inc(s_du, 1)
                dve.wait_ge(s_du, c + 1)
                dve.wait_ge(s_dl, c + 1)
                dve.tensor_tensor(e1[:, :, :], u1[:, :, :], e1[:, :, :], ALU.subtract).then_inc(s_dr, 1)
                dve.wait_ge(s_dr, c * 4 + 9)
                dve.tensor_tensor(l1[:, :, :], l1[:, :, :], e1[:, :, :], ALU.subtract).then_inc(s_dr, 1)
                dve.wait_ge(s_dr, c * 4 + 10)
                dve.scalar_tensor_tensor(l1[:, :, :], zt[:, :, 0:D], 0.0, l1[:, :, :], ALU.max, ALU.add).then_inc(s_dr, 1)
                if not last:
                    split_low(n, 1 - p)
                dve.wait_ge(s_dr, c * 4 + 11)
                dve.tensor_tensor(l1[:, :, :], l1[:, :, :], (xn, xn_b)[p][:, :, :], ALU.mult).then_inc(s_dr, 1)
                dve.wait_ge(s_dr, c * 4 + 12)
                dve.wait_ge(s_dbc, c * 2 + 2)
                for t in range(TPC):
                    xs = x[:, bass.ds(c * TPC + t, 1), :].rearrange("p o d -> p (o d)")
                    i = dve.scalar_tensor_tensor(xs, l1[:, t, :], bcs[:, t:t + 1], xs, ALU.mult, ALU.add)
                i.then_inc(s_dx, 1)

            if phases >= 3:
                dve.wait_ge(s_wd, 64)
                dve.wait_ge(s_ffnc, 64)
                for e in range(EXP):
                    dve.memset(rev[:, :, e], float(EXP - e))
                dve.memset(gate[:, :, EXP:NE], 1.0).then_inc(s_dconst, 1)
                dve.wait_ge(s_dconst, 4)
                statistics(NCH, 0)
                normalise(NCH, 0)
                split_low(NCH, 0)
                route_logits(0)
                route(0)
                chunks(dve, experts(F["C"], NCH, 0), phases == 3)
            if phases >= 4:
                pairs(dve, NCH, gate_stage, peel_last=phases == 4)
            if phases >= 5:
                route_logits(NCH + 1)
                route(NCH + 1)
                chunks(dve, experts(F["E"], 3 * NCH, NCH + 1), True)


_KINDS = ["x_in", "wqkv_in", "uqkv_in", "sqkv_in", "wproj_in", "uproj_in", "sproj_in",
          "wffn_in", "b13_in", "b2_in", "gb_in", "bd_in"]


def kernel(**inputs):
    import numpy as np
    import concourse.bacc as bacc
    from concourse.bass_utils import run_bass_kernel_spmd

    a = {k.removeprefix("L0_"): np.asarray(v) for k, v in inputs.items()}

    def rows(m):
        return m.reshape(KC, P, -1).transpose(1, 0, 2).reshape(P, -1)

    pieces = []
    for e in range(NE):
        if e < EXP:
            up, gated, down = a["ffn_w1"][e].T, a["ffn_w3"][e].T, a["ffn_w2"][e].T
        else:
            s = slice((e - EXP) * D, (e - EXP + 1) * D)
            up, gated, down = a["ffn_ws1"][s].T, a["ffn_ws3"][s].T, a["ffn_ws2"][:, s].T
        pieces += [rows(up), rows(gated), rows(down)]
    pieces.append(rows(a["attn_b_W1"].T))
    rest = [a["attn_b_W2"].T, a["attn_b_W3"].T, a["ffn_gate_w"].T]
    rest.append(np.zeros((D, D - 2 * NST - EXP), rest[0].dtype))
    pieces.append(rows(np.concatenate(rest, axis=1)))

    def hidden(m, s):
        return np.concatenate([m.reshape(-1), s]).reshape(NE * KC, P).T

    b13 = np.stack([hidden(a["ffn_b1"], a["ffn_bs1"]), hidden(a["ffn_b3"], a["ffn_bs3"])], axis=1)
    arrays = [a["attn_a_batch"], a["attn_a_W_qkv"], a["attn_a_u_qkv"], a["attn_a_sigma_qkv"], a["attn_a_W_proj"],
              a["attn_a_u_proj"], a["attn_a_sigma_proj"], np.stack(pieces), b13,
              np.concatenate([a["ffn_b2"], a["ffn_bs2"][None]]), a["ffn_gate_b"],
              np.concatenate([a["attn_b_b1"], a["attn_b_b2"], a["attn_b_b3"]])]
    nc = bacc.Bacc("TRN2", target_bir_lowering=False, num_devices=1)
    feeds, args = {}, []
    for name, v in zip(_KINDS, arrays):
        feeds[name] = np.ascontiguousarray(v)
        args.append(nc.dram_tensor(name, v.shape, mybir.dt.from_np(v.dtype), kind="ExternalInput").ap())
    args.append(nc.dram_tensor("x_out", (B, N, D), mybir.dt.float32, kind="ExternalOutput").ap())
    build(nc, *args)
    return run_bass_kernel_spmd(nc, [feeds], core_ids=[0]).results[0]["x_out"]
```

```python
import concourse.bass as bass
from concourse import mybir
from contextlib import ExitStack

P = 128
B, N, D = 2, 2048, 256
H, HD = 16, 16
KC = D // P
TOK = B * N
CH = 512
TPC = CH // P
NCH = TOK // CH
EXP = 8
NE = 10
NST = 16
DW = D + 2 * NST
GW = DW + EXP
EPS = 1e-5
NEG = -1e30

HPG = 4
NG = H // HPG
NU = B * NG
QCH = N // CH
KT = N // P
PACK = 3 * HD
MROW = PACK

NPIECE = 3 * NE + 2
ROWS = 64 + MROW + 1
HALF_LD = 14 * 16
NEXT_AT = 3
STEPS = [(c, j) for c in range(QCH) for j in range(TPC * (c + 1))]
NSTEP = len(STEPS)
LAG = 2
PRING = 4
RECIP, SPREAD = 2, 4
PROJ = ((12, 13), (20, 21), (32, 33), (7, 8))
MAXES = []
for _i in range(KT):
    for _c in range(_i // TPC + 1):
        _w = min(CH, (_i + 1) * P - _c * CH)
        MAXES.append((_i, _c, _w, CH // _w))
NBANK = sum(HPG // hb for _, _, _, hb in MAXES)
EARLY = NSTEP - TPC * (QCH // 2)
MAX_FROM, MAX_BY = 0, NSTEP - 2


BANKS = [(i, c, w, hb, n) for i, c, w, hb in MAXES for n in range(HPG // hb)]


def max_slot(k):
    total = sum(w * hb for _, _, w, hb, _ in BANKS)
    lo = total * (k - MAX_FROM) / (MAX_BY - MAX_FROM)
    hi = total * (k + 1 - MAX_FROM) / (MAX_BY - MAX_FROM)
    at, n = 0, []
    for bank, (_, _, w, hb, _) in enumerate(BANKS):
        if lo <= at < hi:
            n.append(bank)
        at += w * hb
    return n


RING = 3
ITEMS = []
for _k in range(NSTEP + LAG):
    ITEMS += [("max", _b) for _b in (max_slot(_k) if _k < NSTEP else [])]
    ITEMS += [("out", _c, PROJ[_c].index(_k)) for _c in range(QCH) if _k in PROJ[_c]]
    ITEMS += [("turn",)] if _k == MAX_BY else []
ITEMS += [None] * (-len(ITEMS) % RING)
PLACE = {item: at % RING for at, item in enumerate(ITEMS)}


def bank_user(item, begin, end):
    at, back = ITEMS.index(item) - RING, 0
    while True:
        if at < 0:
            if begin or back:
                return None
            at, back = at + len(ITEMS), 1
        it = ITEMS[at]
        absent = it is None or (back == 0 and (begin and it[:2] == ("out", QCH - 1) or end and it[0] != "out"))
        if not absent:
            return it, back
        at -= RING


def build(nc, x_in, wqkv_in, uqkv_in, sqkv_in, wproj_in, uproj_in, sproj_in,
          wffn_in, b13_in, b2_in, gb_in, bd_in, out):
    f32, f32r, bf16 = mybir.dt.float32, mybir.dt.float32r, mybir.dt.bfloat16
    ALU = mybir.AluOpType
    ACT = mybir.ActivationFunctionType
    AX = mybir.AxisListType

    qk_s = nc.dram_tensor("qk_split", [2, 2 * D, TOK], f32, kind="Internal").ap()
    v_s = nc.dram_tensor("v_ones", [TOK, H * 32], f32, kind="Internal").ap()
    w_s = nc.dram_tensor("w_split", [NPIECE, 2, P, KC * D], f32, kind="Internal").ap()

    ctx = ExitStack()
    with ctx:
        def sb(name, shape, dt=f32, stack=ctx):
            return stack.enter_context(nc.sbuf_tensor(name, shape, dt))

        def sem(name):
            return ctx.enter_context(nc.semaphore(name))

        x = sb("x", [P, TOK // P, D])
        tok = ExitStack()
        xn = sb("xn", [P, TPC, D], f32, tok)
        xt = [[sb(f"xt{p}{h}", [P, KC, CH], f32r, tok) for h in range(2)] for p in range(2)]
        tok.close()
        pr = [sb(f"pr{i}", [P, HPG, CH]) for i in range(2)]
        osb = sb("osb", [P, CH])
        rdb = sb("rdb", [P, CH])
        stats = sb("stats", [P, TPC, 6])
        mv = sb("mv", [P, TPC, 2])
        vare = sb("vare", [P, TPC])
        rstd = sb("rstd", [P, TPC])
        mhalf = sb("mhalf", [P, TPC])
        ones = sb("ones", [P, P])
        ident = sb("ident", [P, P])
        att = ExitStack()
        identb = sb("identb", [P, P], bf16, att)
        mask_qk = sb("mask_qk", [P, P], bf16, att)
        mask_kq = sb("mask_kq", [P, P], bf16, att)
        wph = sb("wph", [P, NG, D], f32r, att)
        wpl = sb("wpl", [P, NG, D], f32r, att)
        wraw = [sb(f"wraw{i}", [P, KC * D], f32r, att) for i in range(2)]
        whi = [sb(f"whi{i}", [P, KC * D], f32r, att) for i in range(2)]
        prj = ExitStack()
        wq_raw = sb("wq_raw", [P, KC, 3 * D], f32, prj)
        wq_hl = [sb(f"wq_{h}", [P, KC, 3 * D], f32r, prj) for h in range(2)]
        wp_raw = sb("wp_raw", [P, NG, D], f32, prj)
        ub = sb("ub", [P, 3 * D + D], f32, prj)
        prod = sb("prod", [P, KC * 3 * D + NG * D], f32, prj)
        vr = sb("vr", [P, KC + NG], f32, prj)
        vsq = sb("vsq", [P, KC + NG], f32, prj)
        vn = sb("vn", [P, KC + NG], f32, prj)
        nrm = sb("nrm", [P, 2], f32, prj)
        rn = sb("rn", [P, 2], f32, prj)
        u2 = sb("u2", [P, 8], f32, prj)
        u2q = sb("u2q", [P, 8], f32, prj)
        u2s = sb("u2s", [P, 2], f32, prj)
        sg = sb("sg", [P, 2], f32, prj)
        rs = sb("rs", [P, 2], f32, prj)
        sp_in = sb("sp_in", [P, 2], f32, prj)
        scl = sb("scl", [P, 2], f32, prj)
        qst = [[sb(f"qst{p}{h}", [P, 4, CH], f32r, prj) for h in range(2)] for p in range(2)]
        vst = [sb(f"vst{p}", [P, TPC, H, 32], f32, prj) for p in range(2)]
        prj.close()
        dsum = sb("dsum", [P, HPG * CH // P], f32, att)
        rden = sb("rden", [P, CH], f32, att)
        ah = sb("ah", [P, CH], f32r, att)
        al = sb("al", [P, CH], f32r, att)
        qp1 = sb("qp1", [P, 2, N], f32r, att)
        kp1 = sb("kp1", [P, HPG, N], f32r, att)
        vt = [sb(f"vt{p}", [P, KT, HPG * 32], f32, att) for p in range(2)]
        pr += [sb(f"pr{i}", [P, HPG, CH], f32, att) for i in range(2, PRING)]
        qp = [sb("qp0", [P, 2, N], f32r, att), qp1]
        kp = [sb("kp0", [P, HPG, N], f32r, att), kp1]
        part = [sb(f"part{p}", [P, HPG, KT, QCH], f32, att) for p in range(2)]
        mneg = sb("mneg", [P, HPG * KT], f32, att)
        mneg_t = sb("mneg_t", [HPG * KT, P], f32r, att)
        att.close()
        ffn = ExitStack()
        w13, w2 = [None] * NE, [None] * NE
        for e in reversed(range(NE)):
            w13[e] = [sb(f"w13_{e}_{h}", [P, 2, KC, D], f32r, ffn) for h in range(2)]
            w2[e] = [sb(f"w2_{e}_{h}", [P, KC, D], f32r, ffn) for h in range(2)]
        wd = [sb(f"wd_{h}", [P, KC, GW], f32r, ffn) for h in range(2)]
        b13 = sb("b13", [P, 2, NE * KC], f32, ffn)
        b2 = sb("b2", [EXP + 1, D], f32, ffn)
        gb = sb("gb", [P, TPC, EXP], f32, ffn)
        bd = sb("bd", [P, DW], f32, ffn)
        rev = sb("rev", [P, TPC, EXP], f32, ffn)
        gate = sb("gate", [P, TPC, NE], f32, ffn)
        gate_t = sb("gate_t", [EXP + 1, CH], f32, ffn)
        lg = sb("lg", [P, TPC, EXP], f32, ffn)
        sc = sb("sc", [P, TPC, EXP], f32, ffn)
        eq = sb("eq", [P, TPC, EXP], f32, ffn)
        oh = sb("oh", [P, TPC, EXP], f32, ffn)
        mx = sb("mx", [P, TPC], f32, ffn)
        hst = ExitStack()
        hh = [[sb(f"hh{p}{h}", [P, KC, CH], f32r, hst) for h in range(2)] for p in range(2)]
        sil = [sb(f"sil{p}", [P, CH], f32, hst) for p in range(2)]
        hf = [sb(f"hf{p}", [P, CH], f32, hst) for p in range(2)]
        hst.close()
        xn_b = sb("xn_b", [P, TPC, D], f32, hst)
        zt = sb("zt", [P, TPC, DW], f32, hst)
        e1 = sb("e1", [P, TPC, D], f32, hst)
        l1 = sb("l1", [P, TPC, D], f32, hst)
        u1 = sb("u1", [P, TPC, D], f32, hst)
        bcp = sb("bcp", [P, TPC, NST], f32, hst)
        bcs = sb("bcs", [P, TPC], f32, hst)
        hst.close()
        ffn.close()

        def ps(name, shape, stack):
            return stack.enter_context(nc.psum_tensor(name, shape, f32))

        pa = ExitStack()
        tr = [ps(f"tr{k}", [P, CH], pa) for k in range(2)]
        pa2 = ExitStack()
        pqk = [ps(f"pqk{m}", [P, CH], pa2) for m in range(4)]
        pv_ = [ps(f"pv{k}", [P, 2, H, HD], pa2) for k in range(2)]
        pa2.close()
        pup = [[ps(f"pup{p}{k}", [P, CH], pa2) for k in range(2)] for p in range(2)]
        py = [ps(f"py{k}", [P, 2, D], pa2) for k in range(2)]
        pa2.close()
        pd = [ps(f"pd{t}", [P, CH], pa2) for t in range(TPC)]
        pa2.close()
        pa.close()
        ps2 = [ps(f"ps2_{k}", [P, 2, CH], pa) for k in range(2)]
        ring = [ps(f"ring{k}", [P, CH], pa) for k in range(RING)]
        po = ps("po", [P, CH], pa)
        pa.close()

        every = [ring[0], ring[1]] + [ps2[k][:, i, :] for k in range(2) for i in range(2)]

        s_x0, s_xr, s_w, s_ffnc = sem("s_x0"), sem("s_xr"), sem("s_w"), sem("s_ffnc")
        s_zero = [sem("s_zero0"), sem("s_zero1")]
        s_vones = sem("s_vones")
        s_const, s_dconst = sem("s_const"), sem("s_dconst")
        s_sig = sem("s_sig")
        s_stats, s_aggr, s_var, s_rstd, s_xn = (sem(n) for n in ("s_stats", "s_aggr", "s_var", "s_rstd", "s_xn"))
        s_tr, s_xhi, s_xlo = sem("s_tr"), sem("s_xhi"), sem("s_xlo")
        s_lg, s_lgd, s_ex, s_gate, s_gt, s_gts = (sem(n) for n in ("s_lg", "s_lgd", "s_ex", "s_gate", "s_gt", "s_gts"))
        s_rt = sem("s_rt")
        s_qk, s_qhi, s_qlo, s_vp, s_ve = (sem(n) for n in ("s_qk", "s_qhi", "s_qlo", "s_vp", "s_ve"))
        s_qout = [sem("s_qout0"), sem("s_qout1")]
        s_ld = [[sem(f"s_ld{p}{h}") for h in range(2)] for p in range(2)]
        s_lv = [sem("s_lv0"), sem("s_lv1")]
        s_m = sem("s_m")
        s_s1, s_mx, s_pm, s_mt, s_mts = (sem(n) for n in ("s_s1", "s_mx", "s_pm", "s_mt", "s_mts"))
        s_s2, s_ex2, s_pv = sem("s_s2"), sem("s_ex2"), sem("s_pv")
        s_oc, s_dg, s_rd, s_rg, s_sh, s_am, s_ah, s_al = (sem(n) for n in ("s_oc", "s_dg", "s_rd", "s_rg", "s_sh", "s_am", "s_ah", "s_al"))
        s_pj, s_xa = sem("s_pj"), sem("s_xa")
        s_wr = [sem("s_wr0"), sem("s_wr1")]
        s_wh, s_wl = sem("s_wh"), sem("s_wl")
        s_ws = [sem("s_ws0"), sem("s_ws1")]
        s_we = [sem(f"s_we{e}") for e in range(NE)]
        s_wd = sem("s_wd")
        names = ("up_a", "up_b", "silu", "h", "h_hi", "h_lo", "y", "acc")
        F = {ph: {n: sem(f"s_{n}_{ph}") for n in names} for ph in "CE"}
        s_dp, s_dz, s_dab, s_de, s_du, s_dl, s_dr, s_dx, s_dbc = (
            sem(n) for n in ("s_dp", "s_dz", "s_dab", "s_de", "s_du", "s_dl", "s_dr", "s_dx", "s_dbc"))
        s_out = sem("s_out")

        block = ctx.enter_context(nc.Block())

        x_v = x_in.rearrange("b (k t p) d -> (b k) p t d", t=TPC, p=P)
        o_v = out.rearrange("b (k t p) d -> (b k) p t d", t=TPC, p=P)
        def pairs(eng, count, body, peel_last=False):
            turns = count // 2 - (1 if peel_last else 0)
            with eng.Fori(0, turns) as i:
                body(2 * i, 0, False)
                body(2 * i + 1, 1, False)
            if peel_last:
                body(count - 2, 0, False)
                body(count - 1, 1, True)

        def chunks(eng, body, final):
            body(0, 0, False)
            body(1, 1, False)
            with eng.Fori(1, NCH // 2 - 1) as i:
                body(2 * i, 0, False)
                body(2 * i + 1, 1, False)
            body(NCH - 2, 0, False)
            body(NCH - 1, 1, final)

        def routed(S, c):
            return not (S is F["C"] and isinstance(c, int) and c == NCH - 1)

        def wait_apart(eng, semaphore, value):
            if not isinstance(value, int):
                value = eng.to_reg(value)
            eng.wait_ge(s_const, 1)
            eng.wait_ge(semaphore, value)

        def units(eng, body):
            body(0, 0, True, False)
            with eng.Fori(0, (NU - 2) // 2) as i:
                body(2 * i + 1, 1, False, False)
                body(2 * i + 2, 0, False, False)
            body(NU - 1, 1, False, True)

        @block.sync
        def _(sp):
            sp.dma_start(x[:, 0:TPC, :], x_v[0]).then_inc(s_x0, 16)
            sp.dma_start(wq_raw[:, :, :], wqkv_in.rearrange("(k p) n -> p k n", p=P)).then_inc(s_w, 16)
            sp.dma_start(ub[:, 0:3 * D], uqkv_in[None, :].to_broadcast([P, 3 * D])).then_inc(s_w, 16)
            sp.dma_start(ub[:, 3 * D:4 * D], uproj_in[None, :].to_broadcast([P, D])).then_inc(s_w, 16)
            sp.dma_start(sp_in[:, 0:1], sqkv_in[None, :].to_broadcast([P, 1])).then_inc(s_w, 16)
            sp.dma_start(sp_in[:, 1:2], sproj_in[None, :].to_broadcast([P, 1])).then_inc(s_w, 16)
            wp_v = wproj_in.rearrange("(g h d) n -> h d g n", h=HPG, d=HD)
            sp.wait_ge(s_dconst, 1)
            for h in range(HPG):
                sp.dma_start(wp_raw[32 * h:32 * h + HD, :, :], wp_v[h]).then_inc(s_w, 16)
            for c in range(1, NCH):
                sp.dma_start(x[:, c * TPC:(c + 1) * TPC, :], x_v[c]).then_inc(s_xr, 16)

            def key_ones(p):
                for h in range(HPG):
                    r0 = 64 * (h % 2) + MROW
                    sp.dma_start(kp[p][r0:r0 + 1, h, :].rearrange("o (i q) -> o i q", q=P).bitcast(f32),
                                 ones[0:KT, :]).then_inc(s_lv[p], 16)

            def load(u, p, half, operands="qk"):
                b, g = u // NG, u % NG
                t0 = half * (N // 2)
                for r0 in (MROW, 64 + MROW) if "q" in operands else ():
                    sp.dma_start(qp[p][r0:r0 + 1, :, t0:t0 + N // 2].bitcast(f32),
                                 kp[p][MROW + 1:MROW + 2, 0:HPG - 1:2, t0:t0 + N // 2].bitcast(f32)).then_inc(s_ld[p][half], 16)
                for base, parts in ((0, (0, 0, 1)), (D, (0, 1, 0))):
                    if "qk"[base // D] not in operands:
                        continue
                    for s in range(2):
                        for n, hl in enumerate(parts):
                            src = qk_s[hl, bass.ds(g * (HPG * HD) + base, HPG * HD), bass.ds(b * N + t0, N // 2)]
                            src = src.rearrange("(r s f) t -> s f r t", r=2, s=2)[s]
                            r0 = 64 * s + HD * n
                            if base == 0:
                                packed = qp[p][r0:r0 + HD, :, t0:t0 + N // 2]
                            else:
                                packed = kp[p][r0:r0 + HD, s:HPG:2, t0:t0 + N // 2]
                            sp.dma_start(packed.bitcast(f32), src).then_inc(s_ld[p][half], 16)

            def store(c, p, last):
                sp.wait_ge(s_qlo, c * 4 + 4)
                for h in range(2):
                    sp.dma_start(qk_s[h, :, bass.ds(c * CH, CH)].rearrange("(m p) t -> p m t", p=P),
                                 qst[p][h][:, :, :].bitcast(f32)).then_inc(s_qout[p], 16)
                sp.wait_ge(s_ve, c * 2 + 2)
                sp.dma_start(v_s[bass.ds(c * CH, CH), :].rearrange("(t p) n -> p t n", p=P),
                             vst[p][:, :, :, :].rearrange("p t h w -> p t (h w)")).then_inc(s_qout[p], 16)

            with sp.Fori(0, NCH // 4) as i:
                store(2 * i, 0, False)
                store(2 * i + 1, 1, False)
            for c in range(NCH // 2, NCH):
                store(c, c % 2, False)
                if c == NCH // 2:
                    for p in range(2):
                        sp.wait_ge(s_qout[p], NCH // 4 * 48)
                    sp.wait_ge(s_zero[0], 2)
                    key_ones(0)
                    load(0, 0, 0)
                elif c < NCH - 1:
                    load(0, 0, 1, "qk"[c - NCH // 2 - 1])
            for p in range(2):
                sp.wait_ge(s_qout[p], NCH // 2 * 48)

            def load_values(u, p):
                b, g = u // NG, u % NG
                src = v_s[bass.ds(b * N, N), bass.ds(g * (HPG * 32), HPG * 32)]
                sp.dma_start(vt[p][:, :, :], src.rearrange("(j p) n -> p j n", p=P)).then_inc(s_lv[p], 16)

            def max_rows(u, p):
                sp.wait_ge(s_mts, u + 1)
                for s in range(2):
                    r0 = 64 * s + MROW
                    sp.dma_start(qp[p][r0:r0 + 1, :, :].rearrange("o r (i q) -> o (r i) q", q=P).bitcast(f32),
                                 mneg_t[2 * KT * s:2 * KT * (s + 1), :].bitcast(f32)).then_inc(s_m, 16)

            def sums_out(n):
                sp.wait_ge(s_oc, n + 1)
                for h in range(HPG):
                    sp.dma_start(dsum[32 * h:32 * h + 32, :], osb[32 * h + HD:32 * h + HD + 1, :].rearrange(
                        "o (s t) -> o s t", s=32)).then_inc(s_dg, 16)

            def sums_back(n):
                sp.wait_ge(s_rd, n + 1)
                if not isinstance(n, int) or n > 0:
                    sp.wait_ge(s_sh, n)
                for h in range(HPG):
                    sp.dma_start(rden[32 * h:32 * h + 1, :].rearrange("o (s t) -> o s t", s=32),
                                 dsum[32 * h:32 * h + 32, :]).then_inc(s_rg, 16)

            def unit_moves(u, p):
                more = not isinstance(u, int) or u < NU - 2
                for c in range(QCH - 1):
                    sums_out(u * QCH + c)
                    sums_back(u * QCH + c)
                if more:
                    sp.wait_ge(s_s2, u * (2 * NSTEP) + 2 * EARLY)
                    load(u + 2, p, 0)
                if not isinstance(u, int) or u < NU - 1:
                    max_rows(u + 1, 1 - p)
                if not isinstance(u, int) or u < NU - 1:
                    sums_out(u * QCH + QCH - 1)
                if more:
                    load(u + 2, p, 1)
                if not isinstance(u, int) or u < NU - 1:
                    sums_back(u * QCH + QCH - 1)
                if more:
                    load_values(u + 2, p)

            load_values(0, 0)
            sp.wait_ge(s_zero[1], 2)
            key_ones(1)
            for half in range(2):
                load(1, 1, half)
            load_values(1, 1)
            max_rows(0, 0)
            unit_moves(0, 0)
            with sp.Fori(0, (NU - 4) // 2) as i:
                unit_moves(2 * i + 1, 1)
                unit_moves(2 * i + 2, 0)
            unit_moves(NU - 3, 1)
            unit_moves(NU - 2, 0)
            unit_moves(NU - 1, 1)

            sp.wait_ge(s_pv, NU * NSTEP)
            for i in range(2):
                sp.wait_ge(s_ws[i], 32 * (NPIECE // 2))
            sp.dma_start(b13[:, :, :], b13_in).then_inc(s_ffnc, 16)
            sp.dma_start(b2[:, :], b2_in).then_inc(s_ffnc, 16)
            sp.dma_start(gb[:, :, :], gb_in[None, None, :].to_broadcast([P, TPC, EXP])).then_inc(s_ffnc, 16)
            sp.dma_start(bd[:, :], bd_in[None, :].to_broadcast([P, DW])).then_inc(s_ffnc, 16)
            for h in range(2):
                wv = w_s[NPIECE - 2, h].rearrange("p (k n) -> p k n", k=KC)
                sp.dma_start(wd[h][:, :, 0:D].bitcast(f32), wv).then_inc(s_wd, 16)
                wv = w_s[NPIECE - 1, h].rearrange("p (k n) -> p k n", k=KC)
                sp.dma_start(wd[h][:, :, D:GW].bitcast(f32), wv[:, :, 0:GW - D]).then_inc(s_wd, 16)
            for e in range(NE):
                if e == NE - 2:
                    sp.wait_ge(s_xa, 2 * QCH * NU)
                for h in range(2):
                    for k in range(2):
                        sp.dma_start(w13[e][h][:, k, :, :].bitcast(f32),
                                     w_s[3 * e + k, h].rearrange("p (k n) -> p k n", k=KC)).then_inc(s_we[e], 16)
                    sp.dma_start(w2[e][h][:, :, :].bitcast(f32),
                                 w_s[3 * e + 2, h].rearrange("p (k n) -> p k n", k=KC)).then_inc(s_we[e], 16)

            def emit(c, p, last):
                sp.wait_ge(F["E"]["acc"], c * (2 * NE) + 2 * NE + 2)
                sp.dma_start(o_v[bass.ds(c, 1)].rearrange("o p t d -> (o p) t d"), x[:, bass.ds(c * TPC, TPC), :]).then_inc(s_out, 16)

            pairs(sp, NCH, emit)
            sp.wait_ge(s_out, 16 * NCH)

        @block.gpsimd
        def _(pool):
            pool.memset(mhalf[:, :], -0.5).then_inc(s_const, 1)
            pool.memset(ones[:, :], 1.0).then_inc(s_const, 1)
            pool.memset(ident[:, :], 0.0).then_inc(s_const, 1)
            pool.memset(identb[:, :], 0.0).then_inc(s_const, 1)
            pool.memset(mask_qk[:, :], 0.0).then_inc(s_const, 1)
            pool.memset(mask_kq[:, :], 0.0).then_inc(s_const, 1)
            pool.wait_ge(s_const, 6)
            for m in (ident, identb):
                pool.affine_select(out=m[:, :], in_=m[:, :], compare_op=ALU.not_equal, fill=1.0,
                                   base=0, pattern=[[-1, P]], channel_multiplier=1).then_inc(s_const, 1)
            pool.affine_select(out=mask_qk[:, :], in_=mask_qk[:, :], compare_op=ALU.is_ge, fill=NEG,
                               base=0, pattern=[[-1, P]], channel_multiplier=1).then_inc(s_const, 1)
            pool.affine_select(out=mask_kq[:, :], in_=mask_kq[:, :], compare_op=ALU.is_ge, fill=NEG,
                               base=0, pattern=[[1, P]], channel_multiplier=-1).then_inc(s_const, 1)

            def inverse_std(n):
                pool.wait_ge(s_var, n + 1)
                pool.tensor_tensor(rstd[:, :], vare[:, :], mhalf[:, :], ALU.pow).then_inc(s_rstd, 1)

            for p in range(2):
                pool.memset(vst[p][:, :, :, :], 1.0).then_inc(s_vones, 1)
            inverse_std(0)
            pool.memset(kp[0][:, :, :].bitcast(f32), 0.0).then_inc(s_zero[0], 1)
            pool.wait_ge(s_sig, 4)
            pool.tensor_tensor(rn[:, :], nrm[:, :], mhalf[:, 0:2], ALU.pow).then_inc(s_sig, 1)
            pool.wait_ge(s_sig, 12)
            pool.tensor_tensor(rs[:, :], sg[:, :], mhalf[:, 0:2], ALU.pow).then_inc(s_sig, 1)
            with pool.Fori(1, NCH) as n:
                inverse_std(n)

            def raw(k, i):
                pool.dma_start(wraw[i][:, :].bitcast(f32), wffn_in[bass.ds(k, 1)].rearrange("o p n -> (o p) n")).then_inc(s_wr[i], 16)

            def finish(u, c, begin, end):
                n = u * QCH + c
                i = c % 2
                turn = u * (QCH // 2) + c // 2
                wait_apart(pool, s_wr[i], turn * 16 + 16)
                pool.tensor_copy(whi[i][:, :], wraw[i][:, :].bitcast(f32)).then_inc(s_wh, 1)
                pool.wait_ge(s_wh, n + 1)
                pool.tensor_tensor(wraw[i][:, :], wraw[i][:, :].bitcast(f32), whi[i][:, :].bitcast(f32),
                                   ALU.subtract).then_inc(s_wl, 1)
                pool.wait_ge(s_wl, n + 1)
                pool.dma_start(w_s[bass.ds(n, 1), 0].rearrange("o p n -> (o p) n"), whi[i][:, :].bitcast(f32)).then_inc(s_ws[i], 16)
                pool.dma_start(w_s[bass.ds(n, 1), 1].rearrange("o p n -> (o p) n"), wraw[i][:, :].bitcast(f32)).then_inc(s_ws[i], 16)
                if not (end and c == QCH - 1):
                    if not (begin and c == 0):
                        pool.wait_ge(s_ws[1 - i], turn * 32 + (32 if i == 1 else 0))
                    raw(n + 1, 1 - i)
                pool.wait_ge(s_sh, n + 1)
                pool.tensor_tensor(rdb[:, :], osb[:, :], rdb[:, :], ALU.mult).then_inc(s_am, 1)
                if not (begin and c == 0):
                    wait_apart(pool, s_pj, n * 2)
                wait_apart(pool, s_am, n + 1)
                pool.tensor_copy(ah[:, :], rdb[:, :]).then_inc(s_ah, 1)
                pool.wait_ge(s_ah, n + 1)
                pool.tensor_tensor(al[:, :], rdb[:, :], ah[:, :].bitcast(f32), ALU.subtract).then_inc(s_al, 1)

            def finish_unit(u, begin, end):
                for c in range(QCH):
                    finish(u, c, begin, end)

            for p in range(2):
                pool.wait_ge(s_qout[p], NCH // 2 * 48)
            pool.memset(kp[1][:, :, :].bitcast(f32), 0.0).then_inc(s_zero[1], 1)
            raw(0, 0)
            finish_unit(0, True, False)
            with pool.Fori(1, NU - 1) as u:
                finish_unit(u, False, False)
            finish_unit(NU - 1, False, True)

            with pool.Fori(NCH, 4 * NCH) as n:
                inverse_std(n)

        @block.scalar
        def _(act):
            def split_high(n, p):
                for k in range(KC):
                    act.wait_ge(s_tr, n * KC + k + 1)
                    act.activation(xt[p][0][:, k, :], tr[k][:, :], ACT.Copy).then_inc(s_xhi, 1)

            def evacuate(c, p, last):
                if not isinstance(c, int) or c >= 2:
                    act.wait_ge(s_qout[p], c // 2 * 48)
                for m in range(4):
                    if m == NEXT_AT and not last:
                        split_high(c + 1, 1 - p)
                    act.wait_ge(s_qk, c * 4 + m + 1)
                    act.activation(qst[p][0][:, m, :], pqk[m][:, :], ACT.Copy).then_inc(s_qhi, 1)
                for k in range(2):
                    act.wait_ge(s_vp, c * 2 + k + 1)
                    act.activation(vst[p][:, 2 * k:2 * k + 2, :, 0:HD], pv_[k][:, :, :, :],
                                   ACT.Copy).then_inc(s_ve, 1)

            split_high(0, 0)
            act.wait_ge(s_vones, 2)
            evacuate(0, 0, False)
            evacuate(1, 1, False)
            with act.Fori(1, NCH // 2 - 1) as i:
                evacuate(2 * i, 0, False)
                evacuate(2 * i + 1, 1, False)
            evacuate(NCH - 2, 0, False)
            evacuate(NCH - 1, 1, True)

            def transposed_max(u, begin):
                turned = ring[RING - 1 if begin else PLACE[("turn",)]]
                if not begin:
                    act.wait_ge(s_m, u * 32)
                act.wait_ge(s_mt, u + 1)
                act.activation(mneg_t[:, :], turned[0:HPG * KT, 0:P], ACT.Copy).then_inc(s_mts, 1)

            def exps(u, p, begin, end):
                for k, (c, j) in enumerate(STEPS):
                    w0 = max(0, j - TPC * c) * P
                    if not (begin and k < PRING):
                        act.wait_ge(s_pv, u * NSTEP + (k - PRING + 1))
                    for r in range(2):
                        act.wait_ge(s_s2, u * (2 * NSTEP) + (2 * k + r + 1))
                        act.activation(pr[k % PRING][:, 2 * r:2 * r + 2, w0:CH], ps2[r][:, :, w0:CH],
                                       ACT.Exp, scale=HD ** -0.5).then_inc(s_ex2, 1)
                    if k == MAX_BY and not end:
                        transposed_max(u + 1, False)

            for p in range(2):
                act.wait_ge(s_qout[p], NCH // 2 * 48)
            transposed_max(0, True)
            units(act, exps)

            def gate_exp(g):
                act.wait_ge(s_lgd, g + 1)
                act.activation(sc[:, :, :], lg[:, :, :], ACT.Exp).then_inc(s_ex, 1)

            def gate_out(g):
                act.wait_ge(s_gt, g + 1)
                act.activation(gate_t[:, :], tr[1][0:EXP + 1, :], ACT.Copy).then_inc(s_gts, 1)

            def experts(S, n0, g0, q0):
                def body(c, p, last):
                    for e in range(NE):
                        for k in range(KC):
                            v = KC * e + k
                            act.wait_ge(S["up_a"], c * (2 * NE) + (v + 1))
                            act.wait_ge(S["h"], c * (2 * NE) + (v + 1))
                            act.activation(sil[k][:, :], pup[k][0][:, :], ACT.Silu,
                                           bias=b13[:, 0, v:v + 1]).then_inc(S["silu"], 1)
                            act.wait_ge(S["h"], c * (2 * NE) + (v + 3))
                            act.wait_ge(S["y"], c * (2 * NE) + (2 * e + 2))
                            act.activation(hh[e % 2][0][:, k, :], hf[k][:, :], ACT.Copy).then_inc(S["h_hi"], 1)
                        if e == 2:
                            gate_out(c + q0)
                        if not last:
                            if e == 4:
                                split_high(c + (n0 + 1), 1 - p)
                            if e == 6 and routed(S, c):
                                gate_exp(c + (g0 + 1))
                return body

            def softplus(c, p, last):
                act.wait_ge(s_dz, c + 2)
                act.wait_ge(s_dr, c * 4 + 6)
                act.activation(e1[:, :, :], zt[:, :, 0:D], ACT.Abs).then_inc(s_dab, 1)
                act.wait_ge(s_dab, c + 1)
                act.activation(e1[:, :, :], e1[:, :, :], ACT.Exp, scale=-1.0).then_inc(s_de, 1)
                split_high(c + (2 * NCH + 1), 1 - p)
                act.wait_ge(s_de, c + 1)
                act.wait_ge(s_dx, c + 1)
                act.activation(l1[:, :, :], e1[:, :, :], ACT.Ln, bias=ones[:, 0:1]).then_inc(s_dl, 1)

            act.wait_ge(s_ffnc, 64)
            split_high(NCH, 0)
            gate_exp(0)
            chunks(act, experts(F["C"], NCH, 0, 0), False)
            pairs(act, NCH, softplus)
            gate_exp(NCH)
            act.wait_ge(s_dx, NCH + 1)
            chunks(act, experts(F["E"], 3 * NCH, NCH, NCH), True)

        @block.tensor
        def _(pe):
            def three(out_ap, lh, ll, rh, rl, start, stop):
                pe.matmul(out_ap, lh, rh, start=start, stop=False)
                pe.matmul(out_ap, lh, rl, start=False, stop=False)
                return pe.matmul(out_ap, ll, rh, start=False, stop=stop)

            def transposes(n, begin=False, g=None, q=None, src=xn):
                pe.wait_ge(s_xn, n + 1)
                if not begin:
                    pe.wait_ge(s_xlo, n * KC)
                if g is not None:
                    pe.wait_ge(s_lgd, g)
                    pe.wait_ge(s_gts, q)
                for k in range(KC):
                    for t in range(TPC):
                        mm = pe.transpose(tr[k][:, t * P:(t + 1) * P], src[:, t, k * P:(k + 1) * P], ident[:, :])
                    mm.then_inc(s_tr, 1)

            def logits(n, p):
                pe.wait_ge(s_xlo, n * KC + KC)
                for t in range(TPC):
                    ts = slice(t * P, (t + 1) * P)
                    for k in range(KC):
                        mm = three(tr[0][:, t * EXP:(t + 1) * EXP], xt[p][0][:, k, ts], xt[p][1][:, k, ts],
                                   wd[0][:, k, DW:GW], wd[1][:, k, DW:GW], k == 0, k == KC - 1)
                mm.then_inc(s_lg, 1)

            def gates_t(g, n):
                pe.wait_ge(s_gate, g + 1)
                pe.wait_ge(s_xlo, n * KC + KC)
                for t in range(TPC):
                    mm = pe.transpose(tr[1][0:EXP + 1, t * P:(t + 1) * P], gate[:, t, 0:EXP + 1], ident[:, :])
                mm.then_inc(s_gt, 1)

            pe.wait_ge(s_const, 10)
            transposes(0, begin=True)
            pe.wait_ge(s_xlo, KC)
            pe.wait_ge(s_sig, 2)
            for n, (k0, k1) in enumerate(((0, KC), (KC, KC + NG))):
                for k in range(k0, k1):
                    mm = pe.matmul(tr[0][:, n:n + 1], ones[:, :], vsq[:, k:k + 1], start=(k == k0), stop=(k == k1 - 1))
            mm.then_inc(s_sig, 1)
            pe.wait_ge(s_sig, 6)
            for m in range(3 * KC):
                for k in range(KC):
                    pe.matmul(tr[1][:, m:m + 1], wq_raw[:, k, m * P:(m + 1) * P], vn[:, k:k + 1],
                              start=(k == 0), stop=(k == KC - 1))
            for m in range(KC):
                for k in range(NG):
                    mm = pe.matmul(tr[1][:, 3 * KC + m:3 * KC + m + 1], wp_raw[:, k, m * P:(m + 1) * P],
                                   vn[:, KC + k:KC + k + 1], start=(k == 0), stop=(k == NG - 1))
            mm.then_inc(s_sig, 1)
            pe.wait_ge(s_sig, 10)
            pe.matmul(tr[0][:, 8:10], ones[:, :], u2s[:, 0:2], start=True, stop=True).then_inc(s_sig, 1)
            pe.wait_ge(s_sig, 20)

            def project(c, p, last):
                pe.wait_ge(s_xlo, c * KC + KC)
                for m in range(4):
                    if m == NEXT_AT and not last:
                        transposes(c + 1)
                    if not isinstance(c, int) or c > 0:
                        pe.wait_ge(s_qlo, c * 4 + (m - 3))
                    ms = slice(m * P, (m + 1) * P)
                    for k in range(KC):
                        mm = three(pqk[m][:, :], wq_hl[0][:, k, ms], wq_hl[1][:, k, ms],
                                   xt[p][0][:, k, :], xt[p][1][:, k, :], k == 0, k == KC - 1)
                    mm.then_inc(s_qk, 1)
                for t in range(TPC):
                    if t % 2 == 0 and (not isinstance(c, int) or c > 0):
                        pe.wait_ge(s_ve, c * 2 + (t // 2 - 1))
                    ts = slice(t * P, (t + 1) * P)
                    for k in range(KC):
                        mm = three(pv_[t // 2][:, t % 2, :, :].rearrange("p h w -> p (h w)"),
                                   xt[p][0][:, k, ts], xt[p][1][:, k, ts],
                                   wq_hl[0][:, k, 2 * D:3 * D], wq_hl[1][:, k, 2 * D:3 * D],
                                   k == 0, k == KC - 1)
                    if t % 2 == 1:
                        mm.then_inc(s_vp, 1)

            project(0, 0, False)
            project(1, 1, False)
            with pe.Fori(1, NCH // 2 - 1) as i:
                project(2 * i, 0, False)
                project(2 * i + 1, 1, False)
            project(NCH - 2, 0, False)
            project(NCH - 1, 1, True)

            def max_scores(p, bank, psum):
                i, cc, w, hb, n = BANKS[bank]
                diag = cc == i // TPC
                for q in range(hb):
                    h = n * hb + q
                    o = psum[:, q * w:(q + 1) * w]
                    mm = pe.matmul(o, qp[p][0:ROWS, h // 2, i * P:(i + 1) * P], kp[p][0:ROWS, h, cc * CH:cc * CH + w],
                                   start=True, stop=not diag)
                    if diag:
                        mm = pe.matmul(o[:, w - P:w], identb[:, :], mask_qk[:, :], start=False, stop=True)
                mm.then_inc(s_s1, 1)

            def bank_free(u, item, begin, end):
                before = bank_user(item, begin, end)
                if before is None:
                    return
                it, back = before
                v = u - back
                if it[0] == "max":
                    wait_apart(pe, s_mx, (v + 1) * NBANK + (it[1] + 1))
                elif it[0] == "turn":
                    wait_apart(pe, s_mts, v + 2)
                else:
                    n = v * QCH + (it[1] - QCH if it[1] == QCH - 1 else it[1])
                    wait_apart(pe, s_xa, n * 2 + (it[2] + 1))

            def transpose_max(u, turned):
                wait_apart(pe, s_pm, u + 1)
                pe.transpose(turned[0:HPG * KT, 0:P], mneg[:, :], ident[:, :]).then_inc(s_mt, 1)

            def scores(u, p, k, r, begin):
                c, j = STEPS[k]
                w0 = max(0, j - TPC * c) * P
                if not (begin and k == 0):
                    pe.wait_ge(s_ex2, u * (2 * NSTEP) + (2 * k + r - 1))
                for s in range(2):
                    h = 2 * r + s
                    mm = pe.matmul(ps2[r][:, s, w0:CH], kp[p][0:ROWS, h, j * P:(j + 1) * P],
                                   qp[p][0:ROWS, h // 2, c * CH + w0:(c + 1) * CH], start=True, stop=j < TPC * c)
                if j >= TPC * c:
                    for s in range(2):
                        mm = pe.matmul(ps2[r][:, s, w0:w0 + P], identb[:, :], mask_kq[:, :], start=False, stop=True)
                mm.then_inc(s_s2, 1)

            def values(u, p, k, begin):
                c, j = STEPS[k]
                w0 = max(0, j - TPC * c) * P
                pe.wait_ge(s_ex2, u * (2 * NSTEP) + (2 * k + 2))
                if j == 0 and not (begin and c == 0):
                    pe.wait_ge(s_oc, u * QCH + c)
                for h in range(HPG):
                    mm = pe.matmul(po[32 * h:32 * h + 32, w0:CH], vt[p][:, j, 32 * h:32 * h + 32],
                                   pr[k % PRING][:, h, w0:CH], start=(j == 0), stop=(j == TPC * c + TPC - 1))
                mm.then_inc(s_pv, 1)

            def project_out(n, g, half, psum):
                if half == 0:
                    pe.wait_ge(s_al, n + 1)
                for t in range(2):
                    ts = slice((2 * half + t) * P, (2 * half + t + 1) * P)
                    mm = three(psum[:, t * D:(t + 1) * D], ah[:, ts], al[:, ts],
                               wph[:, bass.ds(g, 1), :].rearrange("p g n -> p (g n)"),
                               wpl[:, bass.ds(g, 1), :].rearrange("p g n -> p (g n)"), True, True)
                mm.then_inc(s_pj, 1)

            def unit(u, p, begin, end):
                turn = u // 2
                pe.wait_ge(s_lv[p], turn * 16 + (HPG + 1) * 16)
                pe.wait_ge(s_m, u * 32 + 32)
                def next_max(banks):
                    for bank in banks:
                        if bank == 0:
                            pe.wait_ge(s_ld[1 - p][0], (u + 1) // 2 * HALF_LD + HALF_LD)
                        if BANKS[bank][0] == KT // 2 and BANKS[bank][1] == 0 and BANKS[bank][4] == 0:
                            pe.wait_ge(s_ld[1 - p][1], (u + 1) // 2 * HALF_LD + HALF_LD)
                        bank_free(u, ("max", bank), begin, end)
                        max_scores(1 - p, bank, ring[PLACE[("max", bank)]])

                for k in range(NSTEP + LAG):
                    banks = max_slot(k) if not end and k < NSTEP else []
                    if k < NSTEP:
                        scores(u, p, k, 0, begin)
                        next_max(banks[0:1])
                        scores(u, p, k, 1, begin)
                        next_max(banks[1:3])
                    if k >= LAG:
                        values(u, p, k - LAG, begin)
                    next_max(banks[3:])
                    for c in range(QCH):
                        if k in PROJ[c] and not (begin and c == QCH - 1):
                            v = u - 1 if c == QCH - 1 else u
                            item = ("out", c, PROJ[c].index(k))
                            bank_free(u, item, begin, end)
                            project_out(v * QCH + c, v % NG, item[2], ring[PLACE[item]])
                    if k == MAX_BY and not end:
                        bank_free(u, ("turn",), begin, end)
                        transpose_max(u + 1, ring[PLACE[("turn",)]])

            pe.wait_ge(s_qlo, NCH * 4)
            pe.wait_ge(s_ve, NCH * 2)
            for bank in range(NBANK):
                if bank == 0:
                    pe.wait_ge(s_ld[0][0], HALF_LD)
                if BANKS[bank][0] == KT // 2 and BANKS[bank][1] == 0 and BANKS[bank][4] == 0:
                    pe.wait_ge(s_ld[0][1], HALF_LD)
                if bank >= len(every):
                    pe.wait_ge(s_mx, bank - len(every) + 1)
                max_scores(0, bank, every[bank % len(every)])
            transpose_max(0, ring[RING - 1])
            units(pe, unit)
            for half in range(2):
                pe.wait_ge(s_xa, (NU * QCH - 1) * 2 + half)
                project_out(NU * QCH - 1, NG - 1, half, ring[half])

            def experts(S, n0, g0, q0, weights):
                def up(c, p, e, k):
                    v = KC * e + k
                    if weights and k == 0:
                        pe.wait_ge(s_we[e], 96)
                    pe.wait_ge(S["h"], c * (2 * NE) + (v + 1))
                    ks = slice(k * P, (k + 1) * P)
                    for q, done in enumerate(("up_a", "up_b")):
                        for kk in range(KC):
                            mm = three(pup[k][q][:, :], w13[e][0][:, q, kk, ks], w13[e][1][:, q, kk, ks],
                                       xt[p][0][:, kk, :], xt[p][1][:, kk, :], kk == 0, kk == KC - 1)
                        mm.then_inc(S[done], 1)

                def down(c, e):
                    pe.wait_ge(S["h_lo"], c * (2 * NE) + (2 * e + 2))
                    for half in range(2):
                        pe.wait_ge(S["acc"], c * (2 * NE) + (2 * e + half + 1))
                        for t in range(2):
                            ts = slice((2 * half + t) * P, (2 * half + t + 1) * P)
                            if e == EXP:
                                if t == 0 and half == 0:
                                    pe.wait_ge(s_gts, c + (q0 + 1))
                                pe.matmul(py[half][:, t, :], gate_t[:, ts], b2[:, :], start=True, stop=False)
                            for kk in range(KC):
                                mm = three(py[half][:, t, :], hh[e % 2][0][:, kk, ts], hh[e % 2][1][:, kk, ts],
                                           w2[e][0][:, kk, :], w2[e][1][:, kk, :],
                                           kk == 0 and e != EXP, kk == KC - 1)
                        mm.then_inc(S["y"], 1)

                def body(c, p, last):
                    for e in range(NE):
                        up(c, p, e, 0)
                        up(c, p, e, 1)
                        if e > 0:
                            down(c, e - 1)
                        elif not isinstance(c, int) or c > 0:
                            down(c - 1, NE - 1)
                        if e == 2:
                            gates_t(c + g0, c + n0)
                        if not last:
                            if e == 3:
                                transposes(c + (n0 + 1), g=c + (g0 + 1), q=c + (q0 + 1))
                            if e == 5 and routed(S, c):
                                logits(c + (n0 + 1), 1 - p)
                    if isinstance(c, int) and c == NCH - 1:
                        down(c, NE - 1)
                return body

            def gate_stage(c, p, last):
                pe.wait_ge(s_xlo, (c + 2 * NCH) * KC + KC)
                pe.wait_ge(s_dz, c + 1)
                for t in range(TPC):
                    ts = slice(t * P, (t + 1) * P)
                    for k in range(KC):
                        mm = three(pd[t][:, 0:DW], xt[p][0][:, k, ts], xt[p][1][:, k, ts],
                                   wd[0][:, k, 0:DW], wd[1][:, k, 0:DW], k == 0, k == KC - 1)
                    mm.then_inc(s_dp, 1)
                transposes(c + (2 * NCH + 1), g=NCH, q=NCH, src=(xn, xn_b)[1 - p])

            pe.wait_ge(s_wd, 64)
            pe.wait_ge(s_xa, 2 * QCH * NU)
            transposes(NCH)
            logits(NCH, 0)
            chunks(pe, experts(F["C"], NCH, 0, 0, True), False)
            pairs(pe, NCH, gate_stage)
            pe.wait_ge(s_dz, NCH + 1)
            logits(3 * NCH, 0)
            chunks(pe, experts(F["E"], 3 * NCH, NCH, NCH, False), True)

        @block.vector
        def _(dve):
            def statistics(n, t0):
                for t in range(TPC):
                    i = dve.bn_stats(stats[:, t, :], x[:, bass.ds(t0 + t, 1), :].rearrange("p o d -> p (o d)"))
                i.then_inc(s_stats, 1)
                wait_apart(dve, s_stats, n + 1)
                for t in range(TPC):
                    i = dve.bn_aggr(mv[:, t, :], stats[:, t, :])
                i.then_inc(s_aggr, 1)
                dve.wait_ge(s_aggr, n + 1)
                dve.tensor_scalar(vare[:, :], mv[:, :, 1], EPS, None, ALU.add).then_inc(s_var, 1)

            def normalise(n, t0, dst=xn):
                dve.wait_ge(s_rstd, n + 1)
                if not isinstance(n, int) or n > 0:
                    dve.wait_ge(s_tr, n * KC)
                for t in range(TPC):
                    i = dve.tensor_scalar(dst[:, t, :], x[:, bass.ds(t0 + t, 1), :].rearrange("p o d -> p (o d)"),
                                          mv[:, t, 0:1], rstd[:, t:t + 1], ALU.subtract, ALU.mult)
                i.then_inc(s_xn, 1)

            def split_low(n, p):
                for k in range(KC):
                    dve.wait_ge(s_xhi, n * KC + k + 1)
                    dve.tensor_tensor(xt[p][1][:, k, :], tr[k][:, :], xt[p][0][:, k, :].bitcast(f32),
                                      ALU.subtract).then_inc(s_xlo, 1)

            ROUTE = 17

            def over(col):
                return col[:, :].unsqueeze(2).to_broadcast([P, TPC, EXP])

            def route_logits(g):
                dve.wait_ge(s_lg, g + 1)
                dve.tensor_tensor(lg[:, :, :], tr[0][:, 0:TPC * EXP].rearrange("p (t e) -> p t e", e=EXP),
                                  gb[:, :, :], ALU.add).then_inc(s_rt, 1)
                dve.wait_ge(s_rt, g * ROUTE + 1)
                dve.tensor_reduce(mx[:, :], lg[:, :, :], AX.X, ALU.max).then_inc(s_rt, 1)
                dve.wait_ge(s_rt, g * ROUTE + 2)
                dve.tensor_tensor(lg[:, :, :], lg[:, :, :], over(mx), ALU.subtract).then_inc(s_lgd, 1)

            def route(g):
                at = [2]

                def step(ins):
                    at[0] += 1
                    ins.then_inc(s_rt, 1)
                    dve.wait_ge(s_rt, g * ROUTE + at[0])

                dve.wait_ge(s_ex, g + 1)
                step(dve.tensor_reduce(mx[:, :], sc[:, :, :], AX.X, ALU.add))
                step(dve.reciprocal(mx[:, :], mx[:, :]))
                step(dve.tensor_tensor(sc[:, :, :], sc[:, :, :], over(mx), ALU.mult))
                for src, hot in ((sc, oh), (lg, eq)):
                    step(dve.tensor_reduce(mx[:, :], src[:, :, :], AX.X, ALU.max))
                    step(dve.tensor_tensor(eq[:, :, :], src[:, :, :], over(mx), ALU.is_equal))
                    step(dve.tensor_tensor(eq[:, :, :], eq[:, :, :], rev[:, :, :], ALU.mult))
                    step(dve.tensor_reduce(mx[:, :], eq[:, :, :], AX.X, ALU.max))
                    step(dve.tensor_tensor(hot[:, :, :], eq[:, :, :], over(mx), ALU.is_equal))
                    if hot is oh:
                        step(dve.scalar_tensor_tensor(lg[:, :, :], oh[:, :, :], -2.0, sc[:, :, :], ALU.mult, ALU.add))
                step(dve.tensor_tensor(eq[:, :, :], eq[:, :, :], oh[:, :, :], ALU.add))
                assert at[0] == ROUTE, at[0]
                dve.tensor_tensor(gate[:, :, 0:EXP], sc[:, :, :], eq[:, :, :], ALU.mult).then_inc(s_gate, 1)

            for ph in "CE":
                dve.sem_inc(F[ph]["h"], 2)
                dve.sem_inc(F[ph]["acc"], 2)
                dve.sem_inc(F[ph]["y"], 4)
            dve.sem_inc(s_dr, 8)
            dve.sem_inc(s_dx, 1)
            dve.sem_inc(s_dz, 1)
            dve.memset(wp_raw[:, :, :], 0.0).then_inc(s_dconst, 1)

            dve.wait_ge(s_x0, 16)
            statistics(0, 0)
            normalise(0, 0)
            split_low(0, 0)
            dve.wait_ge(s_w, 9 * 16)
            for k in range(KC):
                dve.tensor_tensor_reduce(out=prod[:, k * 3 * D:(k + 1) * 3 * D], in0=wq_raw[:, k, :], in1=ub[:, 0:3 * D], scale=1.0, scalar=0.0,
                                         op0=ALU.mult, op1=ALU.add, accum_out=vr[:, k:k + 1])
            for k in range(NG):
                i = dve.tensor_tensor_reduce(out=prod[:, KC * 3 * D + k * D:KC * 3 * D + (k + 1) * D], in0=wp_raw[:, k, :], in1=ub[:, 3 * D:4 * D], scale=1.0,
                                             scalar=0.0, op0=ALU.mult, op1=ALU.add, accum_out=vr[:, KC + k:KC + k + 1])
            i.then_inc(s_sig, 1)
            dve.wait_ge(s_sig, 1)
            dve.tensor_tensor(vsq[:, :], vr[:, :], vr[:, :], ALU.mult).then_inc(s_sig, 1)
            dve.wait_ge(s_sig, 3)
            dve.tensor_copy(nrm[:, :], tr[0][:, 0:2]).then_inc(s_sig, 1)
            dve.wait_ge(s_sig, 5)
            dve.tensor_scalar(vn[:, 0:KC], vr[:, 0:KC], rn[:, 0:1], None, ALU.mult)
            dve.tensor_scalar(vn[:, KC:KC + NG], vr[:, KC:KC + NG], rn[:, 1:2], None, ALU.mult).then_inc(s_sig, 1)
            dve.memset(qp[0][:, :, :].bitcast(f32), 0.0).then_inc(s_zero[0], 1)
            for p in range(2):
                i = dve.memset(part[p][:, :, :, :], 3e38)
            i.then_inc(s_dconst, 1)
            dve.wait_ge(s_sig, 7)
            dve.tensor_copy(u2[:, :], tr[1][:, 0:8]).then_inc(s_sig, 1)
            dve.wait_ge(s_sig, 8)
            dve.tensor_tensor(u2q[:, :], u2[:, :], u2[:, :], ALU.mult).then_inc(s_sig, 1)
            dve.wait_ge(s_sig, 9)
            dve.tensor_reduce(u2s[:, 0:1], u2q[:, 0:3 * KC], AX.X, ALU.add)
            dve.tensor_reduce(u2s[:, 1:2], u2q[:, 3 * KC:4 * KC], AX.X, ALU.add).then_inc(s_sig, 1)
            dve.wait_ge(s_sig, 11)
            dve.tensor_copy(sg[:, :], tr[0][:, 8:10]).then_inc(s_sig, 1)
            dve.wait_ge(s_sig, 13)
            dve.tensor_tensor(scl[:, :], rs[:, :], sp_in[:, :], ALU.mult).then_inc(s_sig, 1)
            dve.wait_ge(s_sig, 14)
            dve.tensor_scalar(wq_raw[:, :, :], wq_raw[:, :, :], scl[:, 0:1], None, ALU.mult).then_inc(s_sig, 1)
            dve.tensor_scalar(wp_raw[:, :, :], wp_raw[:, :, :], scl[:, 1:2], None, ALU.mult).then_inc(s_sig, 1)
            dve.wait_ge(s_sig, 16)
            dve.tensor_copy(wq_hl[0][:, :, :], wq_raw[:, :, :]).then_inc(s_sig, 1)
            dve.tensor_copy(wph[:, :, :], wp_raw[:, :, :]).then_inc(s_sig, 1)
            dve.wait_ge(s_sig, 18)
            dve.tensor_tensor(wq_hl[1][:, :, :], wq_raw[:, :, :], wq_hl[0][:, :, :].bitcast(f32),
                              ALU.subtract).then_inc(s_sig, 1)
            dve.tensor_tensor(wpl[:, :, :], wp_raw[:, :, :], wph[:, :, :].bitcast(f32), ALU.subtract).then_inc(s_sig, 1)

            dve.wait_ge(s_xr, (NCH - 1) * 16)

            def low_parts(c, p, last):
                if not last:
                    statistics(c + 1, (c + 1) * TPC)
                for m in range(4):
                    if m == 1 and not last:
                        normalise(c + 1, (c + 1) * TPC)
                    dve.wait_ge(s_qhi, c * 4 + m + 1)
                    dve.tensor_tensor(qst[p][1][:, m, :], pqk[m][:, :], qst[p][0][:, m, :].bitcast(f32),
                                      ALU.subtract).then_inc(s_qlo, 1)
                if not last:
                    split_low(c + 1, 1 - p)

            pairs(dve, NCH, low_parts, peel_last=True)

            def take_max(u, p, bank, psum):
                i, cc, w, hb, n = BANKS[bank]
                dve.wait_ge(s_s1, u * NBANK + (bank + 1))
                dve.tensor_reduce(part[p][:, n * hb:(n + 1) * hb, i, cc], psum[:, 0:hb * w].rearrange("p (h w) -> p h w", w=w),
                                  AX.X, ALU.max, negate=True).then_inc(s_mx, 1)

            def join_max(u, p, begin):
                if not begin:
                    dve.wait_ge(s_mt, u)
                dve.wait_ge(s_mx, u * NBANK + NBANK)
                for s in range(2):
                    i = dve.tensor_reduce(mneg[:, 2 * KT * s:2 * KT * (s + 1)].rearrange("p (r i) -> p r i", r=2),
                                          part[p][:, s:HPG:2, :, :], AX.X, ALU.min)
                i.then_inc(s_pm, 1)

            def take_outputs(n, done, begin):
                dve.wait_ge(s_pv, done)
                if not begin:
                    dve.wait_ge(s_am, n)
                dve.tensor_copy(osb[:, :], po[:, :]).then_inc(s_oc, 1)

            def reciprocals(n):
                dve.wait_ge(s_dg, n * (HPG * 16) + HPG * 16)
                dve.reciprocal(dsum[:, :], dsum[:, :]).then_inc(s_rd, 1)

            def spread(n, begin):
                if not begin:
                    wait_apart(dve, s_al, n)
                wait_apart(dve, s_rg, n * (HPG * 16) + HPG * 16)
                dve.stream_shuffle(rdb[:, :], rden[:, :], [0] * 32).then_inc(s_sh, 1)

            def add_out(n, t0, half, psum):
                dve.wait_ge(s_pj, n * 2 + (half + 1))
                xs = x[:, bass.ds(t0 + 2 * half, 2), :]
                dve.tensor_tensor(xs, xs, psum[:, :].rearrange("p (t d) -> p t d", d=D), ALU.add).then_inc(s_xa, 1)

            def unit(u, p, begin, end):
                for k in range(NSTEP + LAG):
                    if not end and k < NSTEP:
                        for bank in max_slot(k):
                            take_max(u + 1, 1 - p, bank, ring[PLACE[("max", bank)]])
                    if k == MAX_BY - 1 and not end:
                        join_max(u + 1, 1 - p, False)
                    for c in range(QCH):
                        if k in PROJ[c] and not (begin and c == QCH - 1):
                            v = u - 1 if c == QCH - 1 else u
                            half = PROJ[c].index(k)
                            add_out(v * QCH + c, v // NG * KT + c * TPC, half, ring[PLACE[("out", c, half)]])
                    for c in range(QCH):
                        at = TPC * (c + 1) * (c + 2) // 2 - 1 + LAG
                        n = u * QCH + c
                        if k == at:
                            take_outputs(n, u * NSTEP + (at - LAG + 1), begin and c == 0)
                        if k == at + RECIP:
                            reciprocals(n)
                        if k == at + SPREAD:
                            spread(n, begin and c == 0)
                    if k == RECIP - 1 and not begin:
                        reciprocals(u * QCH - 1)
                    if k == SPREAD - 1 and not begin:
                        spread(u * QCH - 1, False)

            dve.wait_ge(s_dconst, 2)
            for bank in range(NBANK):
                if bank == NBANK // 4:
                    for p in range(2):
                        dve.wait_ge(s_qout[p], NCH // 2 * 48)
                    dve.memset(qp[1][:, :, :].bitcast(f32), 0.0).then_inc(s_zero[1], 1)
                    dve.memset(rden[:, :], 1.0).then_inc(s_dconst, 1)
                take_max(0, 0, bank, every[bank % len(every)])
            join_max(0, 0, True)
            dve.wait_ge(s_dconst, 3)
            units(dve, unit)
            dve.wait_ge(s_oc, NU * QCH)
            dve.reciprocal(rden[:, :], osb[:, :]).then_inc(s_rd, 1)
            wait_apart(dve, s_rd, NU * QCH)
            wait_apart(dve, s_al, NU * QCH - 1)
            dve.stream_shuffle(rdb[:, :], rden[:, :], [HD + i % HD for i in range(32)]).then_inc(s_sh, 1)
            statistics(NCH, 0)
            for half in range(2):
                add_out(NU * QCH - 1, (NU - 1) // NG * KT + (QCH - 1) * TPC, half, ring[half])

            def experts(S, n0, g0):
                def body(c, p, last):
                    nt = (c + 1) % NCH * TPC
                    n, g = c + (n0 + 1), c + (g0 + 1)

                    def add_expert(c, e):
                        for half in range(2):
                            dve.wait_ge(S["y"], c * (2 * NE) + (2 * e + half + 5))
                            for t in range(2):
                                tile = 2 * half + t
                                xs = x[:, bass.ds(c * TPC + tile, 1), :].rearrange("p o d -> p (o d)")
                                i = dve.scalar_tensor_tensor(xs, py[half][:, t, :], gate[:, tile, e:e + 1], xs,
                                                             ALU.mult, ALU.add)
                            i.then_inc(S["acc"], 1)

                    for e in range(NE):
                        for k in range(KC):
                            v = KC * e + k
                            dve.wait_ge(S["silu"], c * (2 * NE) + (v + 1))
                            dve.wait_ge(S["up_b"], c * (2 * NE) + (v + 1))
                            dve.scalar_tensor_tensor(hf[k][:, :], pup[k][1][:, :], b13[:, 1, v:v + 1], sil[k][:, :],
                                                     ALU.add, ALU.mult).then_inc(S["h"], 1)
                            dve.wait_ge(S["h_hi"], c * (2 * NE) + (v + 1))
                            dve.tensor_tensor(hh[e % 2][1][:, k, :], hf[k][:, :], hh[e % 2][0][:, k, :].bitcast(f32),
                                              ALU.subtract).then_inc(S["h_lo"], 1)
                        if e > 0:
                            add_expert(c, e - 1)
                        elif not isinstance(c, int) or c > 0:
                            add_expert(c - 1, NE - 1)
                        if not last:
                            if e == 1:
                                statistics(n, nt)
                            if e == 2:
                                normalise(n, nt)
                            if e == 4:
                                split_low(n, 1 - p)
                            if e == 6 and routed(S, c):
                                route_logits(g)
                    if isinstance(c, int) and c == NCH - 1:
                        add_expert(c, NE - 1)
                    if not last and routed(S, c):
                        route(g)
                return body

            def gate_stage(c, p, last):
                n = c + (2 * NCH + 1)
                for t in range(TPC):
                    dve.wait_ge(s_dp, c * TPC + (t + 1))
                    i = dve.tensor_tensor(zt[:, t, :], pd[t][:, 0:DW], bd[:, :], ALU.add)
                i.then_inc(s_dz, 1)
                dve.wait_ge(s_dz, c + 2)
                dve.tensor_tensor(bcp[:, :, :], zt[:, :, D:D + NST], zt[:, :, D + NST:DW], ALU.mult).then_inc(s_dbc, 1)
                dve.wait_ge(s_dbc, c * 2 + 1)
                dve.tensor_reduce(bcs[:, :], bcp[:, :, :], AX.X, ALU.add).then_inc(s_dbc, 1)
                normalise(n, (c + 1) % NCH * TPC, (xn, xn_b)[1 - p])
                if not last:
                    statistics(n + 1, (c + 2) % NCH * TPC)
                dve.wait_ge(s_de, c + 1)
                dve.tensor_scalar(u1[:, :, :], e1[:, :, :], 1.0, 1.0, ALU.add, ALU.subtract).then_inc(s_du, 1)
                split_low(n, 1 - p)
                dve.wait_ge(s_du, c + 1)
                dve.tensor_tensor(u1[:, :, :], u1[:, :, :], e1[:, :, :], ALU.subtract).then_inc(s_dr, 1)
                dve.wait_ge(s_dr, c * 4 + 9)
                dve.wait_ge(s_dl, c + 1)
                dve.tensor_tensor(l1[:, :, :], l1[:, :, :], u1[:, :, :], ALU.subtract).then_inc(s_dr, 1)
                dve.wait_ge(s_dr, c * 4 + 10)
                dve.scalar_tensor_tensor(l1[:, :, :], zt[:, :, 0:D], 0.0, l1[:, :, :], ALU.max, ALU.add).then_inc(s_dr, 1)
                dve.wait_ge(s_dr, c * 4 + 11)
                dve.tensor_tensor(l1[:, :, :], l1[:, :, :], (xn, xn_b)[p][:, :, :], ALU.mult).then_inc(s_dr, 1)
                dve.wait_ge(s_dr, c * 4 + 12)
                dve.wait_ge(s_dbc, c * 2 + 2)
                for t in range(TPC):
                    xs = x[:, bass.ds(c * TPC + t, 1), :].rearrange("p o d -> p (o d)")
                    i = dve.scalar_tensor_tensor(xs, l1[:, t, :], bcs[:, t:t + 1], xs, ALU.mult, ALU.add)
                i.then_inc(s_dx, 1)

            dve.wait_ge(s_wd, 64)
            dve.wait_ge(s_ffnc, 64)
            for e in range(EXP):
                dve.memset(rev[:, :, e], float(EXP - e))
            dve.memset(gate[:, :, EXP:NE], 1.0).then_inc(s_dconst, 1)
            dve.wait_ge(s_dconst, 4)
            normalise(NCH, 0)
            split_low(NCH, 0)
            route_logits(0)
            route(0)
            chunks(dve, experts(F["C"], NCH, 0), False)
            statistics(2 * NCH + 1, TPC)
            pairs(dve, NCH, gate_stage, peel_last=True)
            route_logits(NCH)
            route(NCH)
            chunks(dve, experts(F["E"], 3 * NCH, NCH), True)


_KINDS = ["x_in", "wqkv_in", "uqkv_in", "sqkv_in", "wproj_in", "uproj_in", "sproj_in",
          "wffn_in", "b13_in", "b2_in", "gb_in", "bd_in"]


def kernel(**inputs):
    import numpy as np
    import concourse.bacc as bacc
    from concourse.bass_utils import run_bass_kernel_spmd

    a = {k.removeprefix("L0_"): np.asarray(v) for k, v in inputs.items()}

    def rows(m):
        return m.reshape(KC, P, -1).transpose(1, 0, 2).reshape(P, -1)

    pieces = []
    for e in range(NE):
        if e < EXP:
            up, gated, down = a["ffn_w1"][e].T, a["ffn_w3"][e].T, a["ffn_w2"][e].T
        else:
            s = slice((e - EXP) * D, (e - EXP + 1) * D)
            up, gated, down = a["ffn_ws1"][s].T, a["ffn_ws3"][s].T, a["ffn_ws2"][:, s].T
        pieces += [rows(up), rows(gated), rows(down)]
    pieces.append(rows(a["attn_b_W1"].T))
    rest = [a["attn_b_W2"].T, a["attn_b_W3"].T, a["ffn_gate_w"].T]
    rest.append(np.zeros((D, D - 2 * NST - EXP), rest[0].dtype))
    pieces.append(rows(np.concatenate(rest, axis=1)))

    def hidden(m, s):
        return np.concatenate([m.reshape(-1), s]).reshape(NE * KC, P).T

    b13 = np.stack([hidden(a["ffn_b1"], a["ffn_bs1"]), hidden(a["ffn_b3"], a["ffn_bs3"])], axis=1)
    arrays = [a["attn_a_batch"], a["attn_a_W_qkv"], a["attn_a_u_qkv"], a["attn_a_sigma_qkv"], a["attn_a_W_proj"],
              a["attn_a_u_proj"], a["attn_a_sigma_proj"], np.stack(pieces), b13,
              np.concatenate([a["ffn_b2"], a["ffn_bs2"][None]]), a["ffn_gate_b"],
              np.concatenate([a["attn_b_b1"], a["attn_b_b2"], a["attn_b_b3"]])]
    nc = bacc.Bacc("TRN2", target_bir_lowering=False, num_devices=1)
    feeds, args = {}, []
    for name, v in zip(_KINDS, arrays):
        feeds[name] = np.ascontiguousarray(v)
        args.append(nc.dram_tensor(name, v.shape, mybir.dt.from_np(v.dtype), kind="ExternalInput").ap())
    args.append(nc.dram_tensor("x_out", (B, N, D), mybir.dt.float32, kind="ExternalOutput").ap())
    build(nc, *args)
    return run_bass_kernel_spmd(nc, [feeds], core_ids=[0]).results[0]["x_out"]
```
